# Optimizing a Trainium2 kernel written in Bass

```python
import numpy as np
import jax
import jax.numpy as jnp

def _softmax(x, axis=-1):
    return jax.nn.softmax(x, axis=axis)

def _gelu(x):
    return jax.nn.gelu(x, approximate=True)

def _silu(x):
    return jax.nn.silu(x)

def _sigmoid(x):
    return jax.nn.sigmoid(x)

def _layernorm(x, axis=-1, eps=1e-05):
    m = jnp.mean(x, axis=axis, keepdims=True)
    v = jnp.var(x, axis=axis, keepdims=True)
    return (x - m) / jnp.sqrt(v + eps)

def _scatter_add(tgt, idx, src, axis=0):
    return tgt.at[idx].add(src)

def _segment_sum(src, seg, n):
    return jax.ops.segment_sum(src, seg, n)
kernel_name = 'mk_hybrid_d1_jaxref_r8_d144c7'

def setup_inputs(seed: int=0):
    np.random.seed(seed)
    _w = jnp.asarray

    def _L0_attn_a_setup():
        import jax, jax.numpy as jnp
        import numpy as np
        B, T, C, FFN, N_LAYER, LAYER_ID = (4, 256, 128, 512, 24, 1)
        EPS = 1e-05

        def _ln(z, g, b):
            m = jnp.mean(z, axis=-1, keepdims=True)
            v = jnp.mean(jnp.square(z - m), axis=-1, keepdims=True)
            return (z - m) * jax.lax.rsqrt(v + EPS) * g + b

        def _shift(z):
            return jnp.pad(z, ((0, 0), (1, 0), (0, 0)))[:, :-1]

        def _wkv(time_decay, u, k, v):
            w = -jnp.exp(time_decay)
            kt = jnp.moveaxis(k, 1, 0)
            vt = jnp.moveaxis(v, 1, 0)
            aa = jnp.zeros_like(kt[0])
            bb = jnp.zeros_like(kt[0])
            pp = jnp.full_like(kt[0], -1e+38)

            def step(carry, kv):
                aa, bb, pp = carry
                kk, vv = kv
                ww = u + kk
                p = jnp.maximum(pp, ww)
                e1 = jnp.exp(pp - p)
                e2 = jnp.exp(ww - p)
                out = (e1 * aa + e2 * vv) / (e1 * bb + e2)
                ww2 = pp + w
                p2 = jnp.maximum(ww2, kk)
                e1b = jnp.exp(ww2 - p2)
                e2b = jnp.exp(kk - p2)
                return ((e1b * aa + e2b * vv, e1b * bb + e2b, p2), out)
            _, out = jax.lax.scan(step, (aa, bb, pp), (kt, vt))
            return jnp.moveaxis(out, 0, 1)
        key = jax.random.key(seed)
        ks = jax.random.split(key, 10)
        scale = 0.02

        def w(k, shape):
            return jax.random.normal(k, shape, jnp.float32) * scale
        r01 = LAYER_ID / (N_LAYER - 1)
        r10 = 1.0 - LAYER_ID / N_LAYER
        ddd = np.arange(C, dtype=np.float64) / C
        h = np.arange(C, dtype=np.float64)
        decay = -5.0 + 8.0 * (h / (C - 1)) ** (0.7 + 1.3 * r01)
        zigzag = np.array([(i + 1) % 3 - 1 for i in range(C)], dtype=np.float64) * 0.5
        tfirst = np.log(0.3) + zigzag
        return {'x': jax.random.normal(ks[0], (B, T, C), jnp.float32), 'ln1_w': jnp.ones((C,), jnp.float32), 'ln1_b': jnp.zeros((C,), jnp.float32), 'ln2_w': jnp.ones((C,), jnp.float32), 'ln2_b': jnp.zeros((C,), jnp.float32), 'time_decay': jnp.asarray(decay, jnp.float32), 'time_first': jnp.asarray(tfirst, jnp.float32), 'tmk': jnp.asarray(ddd ** r10, jnp.float32), 'tmv': jnp.asarray(ddd ** r10 + 0.3 * r01, jnp.float32), 'tmr': jnp.asarray(ddd ** (0.5 * r10), jnp.float32), 'att_kw': w(ks[1], (C, C)), 'att_vw': w(ks[2], (C, C)), 'att_rw': w(ks[3], (C, C)), 'att_ow': w(ks[4], (C, C)), 'f_tmk': jnp.asarray(ddd ** r10, jnp.float32), 'f_tmr': jnp.asarray(ddd ** r10, jnp.float32), 'f_kw': w(ks[5], (FFN, C)), 'f_rw': w(ks[6], (C, C)), 'f_vw': w(ks[7], (C, FFN))}
    _L0_attn_a_in = _L0_attn_a_setup()

    def _L0_attn_b_setup():
        import jax, jax.numpy as jnp
        import numpy as np
        EMBED_DIM = 128
        NUM_HEADS = 16
        HEAD_DIM = EMBED_DIM // NUM_HEADS
        B, N = (2, 256)
        BIAS_S = 32

        def _interp_matrix(n, s):
            pos = jnp.arange(n, dtype=jnp.float32) * ((s - 1) / (n - 1))
            i0 = jnp.floor(pos).astype(jnp.int32)
            i1 = jnp.minimum(i0 + 1, s - 1)
            frac = pos - i0.astype(jnp.float32)
            rows = jnp.arange(n)
            M = jnp.zeros((n, s), dtype=jnp.float32)
            M = M.at[rows, i0].add(1.0 - frac).at[rows, i1].add(frac)
            return M
        key = jax.random.key(seed)
        ks = jax.random.split(key, 12)
        std = 0.02
        d = {'x': jax.random.normal(ks[0], (B, N, EMBED_DIM), dtype=jnp.float32), 'Wq': jax.random.normal(ks[1], (EMBED_DIM, EMBED_DIM), dtype=jnp.float32) * std, 'bq': jnp.zeros((EMBED_DIM,), dtype=jnp.float32), 'Wk': jax.random.normal(ks[2], (EMBED_DIM, EMBED_DIM), dtype=jnp.float32) * std, 'bk': jnp.zeros((EMBED_DIM,), dtype=jnp.float32), 'Wv': jax.random.normal(ks[3], (EMBED_DIM, EMBED_DIM), dtype=jnp.float32) * std, 'bv': jnp.zeros((EMBED_DIM,), dtype=jnp.float32), 'Wo': jax.random.normal(ks[4], (EMBED_DIM, EMBED_DIM), dtype=jnp.float32) * std, 'bo': jnp.zeros((EMBED_DIM,), dtype=jnp.float32), 'gamma': jnp.ones((EMBED_DIM,), dtype=jnp.float32), 'beta': jnp.zeros((EMBED_DIM,), dtype=jnp.float32), 'rel_bias': jax.random.normal(ks[5], (NUM_HEADS, BIAS_S, BIAS_S), dtype=jnp.float32) * std}
        return d
    _L0_attn_b_in = _L0_attn_b_setup()

    def _L0_ffn_setup():
        import jax, jax.numpy as jnp
        import numpy as np
        B, T, D, H, E = (4, 256, 128, 256, 8)
        TOP_K = int(E * 0.25)
        key = jax.random.key(seed)
        ks = jax.random.split(key, 6)
        x = jax.random.normal(ks[0], (B, T, D), dtype=jnp.float32)
        gate = jax.random.normal(ks[1], (D, E), dtype=jnp.float32)
        W1 = jax.random.normal(ks[2], (E, D, H), dtype=jnp.float32) * D ** (-0.5)
        b1 = jnp.zeros((E, H), dtype=jnp.float32)
        W2 = jax.random.normal(ks[3], (E, H, D), dtype=jnp.float32) * H ** (-0.5)
        b2 = jnp.zeros((E, D), dtype=jnp.float32)
        return {'x': x, 'gate': gate, 'W1': W1, 'b1': b1, 'W2': W2, 'b2': b2}
    _L0_ffn_in = _L0_ffn_setup()
    _d = {'L0_attn_a_x': _L0_attn_a_in['x'], 'L0_attn_a_ln1_w': _L0_attn_a_in['ln1_w'], 'L0_attn_a_ln1_b': _L0_attn_a_in['ln1_b'], 'L0_attn_a_ln2_w': _L0_attn_a_in['ln2_w'], 'L0_attn_a_ln2_b': _L0_attn_a_in['ln2_b'], 'L0_attn_a_time_decay': _L0_attn_a_in['time_decay'], 'L0_attn_a_time_first': _L0_attn_a_in['time_first'], 'L0_attn_a_tmk': _L0_attn_a_in['tmk'], 'L0_attn_a_tmv': _L0_attn_a_in['tmv'], 'L0_attn_a_tmr': _L0_attn_a_in['tmr'], 'L0_attn_a_att_kw': _L0_attn_a_in['att_kw'], 'L0_attn_a_att_vw': _L0_attn_a_in['att_vw'], 'L0_attn_a_att_rw': _L0_attn_a_in['att_rw'], 'L0_attn_a_att_ow': _L0_attn_a_in['att_ow'], 'L0_attn_a_f_tmk': _L0_attn_a_in['f_tmk'], 'L0_attn_a_f_tmr': _L0_attn_a_in['f_tmr'], 'L0_attn_a_f_kw': _L0_attn_a_in['f_kw'], 'L0_attn_a_f_rw': _L0_attn_a_in['f_rw'], 'L0_attn_a_f_vw': _L0_attn_a_in['f_vw'], 'L0_attn_b_Wq': _L0_attn_b_in['Wq'], 'L0_attn_b_bq': _L0_attn_b_in['bq'], 'L0_attn_b_Wk': _L0_attn_b_in['Wk'], 'L0_attn_b_bk': _L0_attn_b_in['bk'], 'L0_attn_b_Wv': _L0_attn_b_in['Wv'], 'L0_attn_b_bv': _L0_attn_b_in['bv'], 'L0_attn_b_Wo': _L0_attn_b_in['Wo'], 'L0_attn_b_bo': _L0_attn_b_in['bo'], 'L0_attn_b_gamma': _L0_attn_b_in['gamma'], 'L0_attn_b_beta': _L0_attn_b_in['beta'], 'L0_attn_b_rel_bias': _L0_attn_b_in['rel_bias'], 'L0_ffn_gate': _L0_ffn_in['gate'], 'L0_ffn_W1': _L0_ffn_in['W1'], 'L0_ffn_b1': _L0_ffn_in['b1'], 'L0_ffn_W2': _L0_ffn_in['W2'], 'L0_ffn_b2': _L0_ffn_in['b2']}
    _x0 = _d['L0_attn_a_x']
    _d['L0_attn_a_x'] = jax.random.normal(jax.random.fold_in(jax.random.key(seed), 1), (4, 1024, 128), dtype=_x0.dtype)
    del _x0
    return _d

def reference(L0_attn_a_x, L0_attn_a_ln1_w, L0_attn_a_ln1_b, L0_attn_a_ln2_w, L0_attn_a_ln2_b, L0_attn_a_time_decay, L0_attn_a_time_first, L0_attn_a_tmk, L0_attn_a_tmv, L0_attn_a_tmr, L0_attn_a_att_kw, L0_attn_a_att_vw, L0_attn_a_att_rw, L0_attn_a_att_ow, L0_attn_a_f_tmk, L0_attn_a_f_tmr, L0_attn_a_f_kw, L0_attn_a_f_rw, L0_attn_a_f_vw, L0_attn_b_Wq, L0_attn_b_bq, L0_attn_b_Wk, L0_attn_b_bk, L0_attn_b_Wv, L0_attn_b_bv, L0_attn_b_Wo, L0_attn_b_bo, L0_attn_b_gamma, L0_attn_b_beta, L0_attn_b_rel_bias, L0_ffn_gate, L0_ffn_W1, L0_ffn_b1, L0_ffn_W2, L0_ffn_b2):

    def _L0_attn_a_ref(x, ln1_w, ln1_b, ln2_w, ln2_b, time_decay, time_first, tmk, tmv, tmr, att_kw, att_vw, att_rw, att_ow, f_tmk, f_tmr, f_kw, f_rw, f_vw):
        import jax, jax.numpy as jnp
        import numpy as np
        B, T, C, FFN, N_LAYER, LAYER_ID = (4, 256, 128, 512, 24, 1)
        EPS = 1e-05

        def _ln(z, g, b):
            m = jnp.mean(z, axis=-1, keepdims=True)
            v = jnp.mean(jnp.square(z - m), axis=-1, keepdims=True)
            return (z - m) * jax.lax.rsqrt(v + EPS) * g + b

        def _shift(z):
            return jnp.pad(z, ((0, 0), (1, 0), (0, 0)))[:, :-1]

        def _wkv(time_decay, u, k, v):
            w = -jnp.exp(time_decay)
            kt = jnp.moveaxis(k, 1, 0)
            vt = jnp.moveaxis(v, 1, 0)
            aa = jnp.zeros_like(kt[0])
            bb = jnp.zeros_like(kt[0])
            pp = jnp.full_like(kt[0], -1e+38)

            def step(carry, kv):
                aa, bb, pp = carry
                kk, vv = kv
                ww = u + kk
                p = jnp.maximum(pp, ww)
                e1 = jnp.exp(pp - p)
                e2 = jnp.exp(ww - p)
                out = (e1 * aa + e2 * vv) / (e1 * bb + e2)
                ww2 = pp + w
                p2 = jnp.maximum(ww2, kk)
                e1b = jnp.exp(ww2 - p2)
                e2b = jnp.exp(kk - p2)
                return ((e1b * aa + e2b * vv, e1b * bb + e2b, p2), out)
            _, out = jax.lax.scan(step, (aa, bb, pp), (kt, vt))
            return jnp.moveaxis(out, 0, 1)
        h = _ln(x, ln1_w, ln1_b)
        hx = _shift(h)
        xk = h * tmk + hx * (1.0 - tmk)
        xv = h * tmv + hx * (1.0 - tmv)
        xr = h * tmr + hx * (1.0 - tmr)
        k = jnp.einsum('btc,dc->btd', xk, att_kw)
        v = jnp.einsum('btc,dc->btd', xv, att_vw)
        sr = jax.nn.sigmoid(jnp.einsum('btc,dc->btd', xr, att_rw))
        rwkv = sr * _wkv(time_decay, time_first, k, v)
        x = x + jnp.einsum('btd,cd->btc', rwkv, att_ow)
        h = _ln(x, ln2_w, ln2_b)
        hx = _shift(h)
        xk = h * f_tmk + hx * (1.0 - f_tmk)
        xr = h * f_tmr + hx * (1.0 - f_tmr)
        kk = jnp.square(jax.nn.relu(jnp.einsum('btc,fc->btf', xk, f_kw)))
        kv = jnp.einsum('btf,cf->btc', kk, f_vw)
        x = x + jax.nn.sigmoid(jnp.einsum('btc,dc->btd', xr, f_rw)) * kv
        return x

    def _L0_attn_b_ref(x, Wq, bq, Wk, bk, Wv, bv, Wo, bo, gamma, beta, rel_bias):
        import jax, jax.numpy as jnp
        import numpy as np
        EMBED_DIM = 128
        NUM_HEADS = 16
        HEAD_DIM = EMBED_DIM // NUM_HEADS
        B, N = (2, 256)
        BIAS_S = 32

        def _interp_matrix(n, s):
            pos = jnp.arange(n, dtype=jnp.float32) * ((s - 1) / (n - 1))
            i0 = jnp.floor(pos).astype(jnp.int32)
            i1 = jnp.minimum(i0 + 1, s - 1)
            frac = pos - i0.astype(jnp.float32)
            rows = jnp.arange(n)
            M = jnp.zeros((n, s), dtype=jnp.float32)
            M = M.at[rows, i0].add(1.0 - frac).at[rows, i1].add(frac)
            return M
        Bx, Nx, C = x.shape
        H, D = (NUM_HEADS, HEAD_DIM)
        scale = 1.0 / jnp.sqrt(jnp.float32(D))
        mu = jnp.mean(x, axis=-1, keepdims=True)
        var = jnp.mean(jnp.square(x - mu), axis=-1, keepdims=True)
        xn = (x - mu) * jax.lax.rsqrt(var + 1e-05) * gamma + beta
        q = (xn @ Wq.T + bq).reshape(Bx, Nx, H, D).transpose(0, 2, 1, 3)
        k = (xn @ Wk.T + bk).reshape(Bx, Nx, H, D).transpose(0, 2, 1, 3)
        v = (xn @ Wv.T + bv).reshape(Bx, Nx, H, D).transpose(0, 2, 1, 3)
        attn = jnp.einsum('bhnd,bhmd->bhnm', q, k) * scale
        M = _interp_matrix(Nx, BIAS_S)
        rel = jnp.einsum('ni,hij,mj->hnm', M, rel_bias, M)
        rel = rel.at[:, -1, :].set(0.0).at[:, :, -1].set(0.0)
        attn = attn + rel[None]
        mask = jnp.triu(jnp.ones((Nx, Nx), dtype=bool), k=1)
        attn = jnp.where(mask, -jnp.inf, attn)
        attn = jax.nn.softmax(attn, axis=-1)
        out = jnp.einsum('bhnm,bhmd->bhnd', attn, v)
        out = out.transpose(0, 2, 1, 3).reshape(Bx, Nx, C)
        out = out @ Wo.T + bo
        return out

    def _L0_ffn_ref(x, gate, W1, b1, W2, b2):
        import jax, jax.numpy as jnp
        import numpy as np
        B, T, D, H, E = (4, 256, 128, 256, 8)
        TOP_K = int(E * 0.25)
        raw_gate = jax.nn.softmax(jnp.einsum('btd,de->bte', x, gate), axis=-1)
        topk_scores, topk_idx = jax.lax.top_k(raw_gate, TOP_K)
        mask = jax.nn.one_hot(topk_idx, E, dtype=raw_gate.dtype).sum(axis=-2)
        gate_topk = mask * raw_gate
        gate_topk = gate_topk / jnp.maximum(gate_topk.sum(axis=-1, keepdims=True), 1e-12)
        h = jax.nn.relu(jnp.einsum('btd,edh->beth', x, W1) + b1[None, :, None, :])
        expert_out = jnp.einsum('beth,ehd->betd', h, W2) + b2[None, :, None, :]
        out = jnp.einsum('bte,betd->btd', gate_topk, expert_out)
        return out
    x = L0_attn_a_x
    x = x + _L0_attn_a_ref(_layernorm(x, axis=-1), L0_attn_a_ln1_w, L0_attn_a_ln1_b, L0_attn_a_ln2_w, L0_attn_a_ln2_b, L0_attn_a_time_decay, L0_attn_a_time_first, L0_attn_a_tmk, L0_attn_a_tmv, L0_attn_a_tmr, L0_attn_a_att_kw, L0_attn_a_att_vw, L0_attn_a_att_rw, L0_attn_a_att_ow, L0_attn_a_f_tmk, L0_attn_a_f_tmr, L0_attn_a_f_kw, L0_attn_a_f_rw, L0_attn_a_f_vw)
    x = x + _L0_ffn_ref(_layernorm(x, axis=-1), L0_ffn_gate, L0_ffn_W1, L0_ffn_b1, L0_ffn_W2, L0_ffn_b2)
    x = x + _L0_attn_b_ref(_layernorm(x, axis=-1), L0_attn_b_Wq, L0_attn_b_bq, L0_attn_b_Wk, L0_attn_b_bk, L0_attn_b_Wv, L0_attn_b_bv, L0_attn_b_Wo, L0_attn_b_bo, L0_attn_b_gamma, L0_attn_b_beta, L0_attn_b_rel_bias)
    x = x + _L0_ffn_ref(_layernorm(x, axis=-1), L0_ffn_gate, L0_ffn_W1, L0_ffn_b1, L0_ffn_W2, L0_ffn_b2)
    return x

_drawn_inputs = setup_inputs


def setup_inputs(seed=0):
    import zlib

    import numpy as np

    out = dict(_drawn_inputs(seed))
    spreads = {'L0_attn_a_ln1_w': (1.0, 0.6),
     'L0_attn_a_ln1_b': (0.0, 0.8),
     'L0_attn_a_ln2_w': (1.0, 0.6),
     'L0_attn_a_ln2_b': (0.0, 0.8),
     'L0_attn_b_bq': (0.0, 2.0),
     'L0_attn_b_bk': (0.0, 2.0),
     'L0_attn_b_bv': (0.0, 2.0),
     'L0_attn_b_bo': (0.0, 2.0),
     'L0_attn_b_gamma': (1.0, 0.6),
     'L0_attn_b_beta': (0.0, 2.0),
     'L0_ffn_b1': (0.0, 0.8),
     'L0_ffn_b2': (0.0, 2.0)}
    factors = {'L0_attn_a_time_decay': 5.515,
     'L0_attn_a_time_first': 8.0,
     'L0_attn_a_tmk': 8.0,
     'L0_attn_a_tmv': 6.202,
     'L0_attn_a_tmr': 8.0,
     'L0_attn_a_att_kw': 8.0,
     'L0_attn_a_att_vw': 3.889,
     'L0_attn_a_att_rw': 8.0,
     'L0_attn_a_att_ow': 3.425,
     'L0_attn_a_f_tmk': 7.4,
     'L0_attn_a_f_tmr': 8.0,
     'L0_attn_a_f_kw': 5.029,
     'L0_attn_a_f_rw': 8.0,
     'L0_attn_a_f_vw': 4.25,
     'L0_attn_b_Wq': 31.063,
     'L0_attn_b_Wk': 30.705,
     'L0_attn_b_Wv': 22.046,
     'L0_attn_b_Wo': 11.443,
     'L0_attn_b_rel_bias': 200.0,
     'L0_ffn_gate': 4.83,
     'L0_ffn_W1': 5.545,
     'L0_ffn_W2': 4.612}
    for name, (base, spread) in spreads.items():
        noise = np.random.default_rng([zlib.crc32(name.encode()), seed]).standard_normal(out[name].shape)
        drawn = base * np.exp(spread * noise) if base else spread * noise
        out[name] = jnp.asarray(drawn.astype(out[name].dtype))
    for name, factor in factors.items():
        out[name] = (out[name] * factor).astype(out[name].dtype)
    return out
```

```python
from contextlib import ExitStack

import numpy as np
import concourse.bass as bass
from concourse import mybir

F32 = mybir.dt.float32
BF16 = mybir.dt.bfloat16
F32R = mybir.dt.float32r
ALU = mybir.AluOpType
ACT = mybir.ActivationFunctionType
AX = mybir.AxisListType

P = 128
B, T, C = 4, 1024, 128
N = B * T
CH = 512
NCH = N // CH
NBLK = N // P
FB = 4
E, HB = 8, 2
NH, D = 16, 8
HG = 4
S = 32
SW = 17
EPS = 1e-5
NEG = -1.0e30
QK_ROWS = 6 * D
REL0 = QK_ROWS
MAX0 = REL0 + 3 * SW
ROWS = MAX0 + 3
VW = D + 1
VG = 8 * HG * VW
SCALE = D ** -0.5
GRID_SCALE = ((S - 1) / (T - 1)) ** 2

PACKS = [
    [(0, 0, 512, 0)], [(1, 128, 384, 0), (3, 384, 128, 384)], [(2, 256, 256, 0)],
    [(0, 512, 512, 0)], [(1, 512, 512, 0)], [(2, 512, 512, 0)], [(3, 512, 512, 0)],
    [(4, 512, 512, 0)], [(5, 640, 384, 0), (7, 896, 128, 384)], [(6, 768, 256, 0)],
]
HALF_END = (2, 9)
NP_ = len(PACKS)
NPB = 4

PIECES = []
for _j in range(HG):
    for _q in range(8):
        if _q >= 4:
            PIECES.append((_j, _q, 0, 512, False))
        _k0 = 512 * (_q // 4)
        PIECES.append((_j, _q, _k0, (_q + 1) * P - _k0, True))


class Steps:

    def __init__(self, sem, names):
        self.sem, self.names = sem, names

    def start(self, eng):
        eng.sem_inc(self.sem, len(self.names))

    def at(self, name, it):
        return it * len(self.names) + (self.names.index(name) + 1)

    def wait(self, eng, name, it):
        eng.wait_ge(self.sem, self.at(name, it))


def build(nc, x, w, out):
    with ExitStack() as ctx:
        def sb(name, shape, dt=F32):
            return ctx.enter_context(nc.sbuf_tensor(name, shape, dt))

        def sem(name):
            return ctx.enter_context(nc.semaphore(name))

        bank = [ctx.enter_context(nc.psum_tensor(f"bank{i}", [P, CH], F32)) for i in range(3)]
        psum_pair = [ctx.enter_context(nc.psum_tensor(f"pair{i}", [P, 2, CH], F32)) for i in range(2)]
        bank += [psum_pair[0][:, 0, :], psum_pair[0][:, 1, :], psum_pair[1][:, 0, :], psum_pair[1][:, 1, :]]
        bank.append(ctx.enter_context(nc.psum_tensor("bank7", [P, CH], F32)))
        bank = [b if i in (3, 4, 5, 6) else b[:, :] for i, b in enumerate(bank)]

        X = sb("X", [P, N])
        H = sb("H", [P, B * (T + 1) + CH + 1])
        centre = sb("centre", [P, P])
        mean_at = sb("mean_at", [P, 127])
        ident = sb("ident", [P, P])
        ident16 = sb("ident16", [P, P], BF16)
        pick = sb("pick", [P, S], BF16)
        pick_e = sb("pick_e", [P, E], BF16)
        tie = sb("tie", [P, E])
        mask = sb("mask", [P, CH])
        mask_t = sb("mask_t", [P, P], BF16)
        vecs = sb("vecs", [P, 15])
        (LN1W, LN1B, LN2W, LN2B, DECAY, FIRST, TMK, TMV, TMR, FTMK, FTMR, GAM, BET, BO, BV) = range(15)
        bqk = sb("bqk", [P, 2])
        b1 = sb("b1", [P, E * HB])
        b2rep = sb("b2rep", [P, 3, P])
        b2p = sb("b2p", [P, 3, P], BF16)
        b2t = sb("b2t", [P, 2, P])
        var = [sb(f"lnv{i}", [96, P]) for i in range(6)]
        rp = sb("rp", [96, 2, P], BF16)
        lr = sb("lr", [96, 2, P])
        ln_scratch = sb("ln_scratch", [P, 4, CH])
        with ExitStack() as room:
            HG_HI, HG_LO = (room.enter_context(nc.sbuf_tensor(name, [P, 4, HB, CH], F32R))
                            for name in ("gated_hi", "gated_lo"))
        XC = sb("XC", [P, N])
        XP = sb("XP", [P, N])
        with ExitStack() as room:
            w1_hi, w1_lo = (room.enter_context(nc.sbuf_tensor(name, [P, E, HB * P], F32R))
                            for name in ("w1_hi", "w1_lo"))
            w2_hi, w2_lo = (room.enter_context(nc.sbuf_tensor(name, [P, E, HB, P], F32R))
                            for name in ("w2_hi", "w2_lo"))
            h_hi, h_lo = (room.enter_context(nc.sbuf_tensor(name, [P, N + CH], F32R))
                          for name in ("h_hi", "h_lo"))
        OPERANDS = 4 * E * HB * P + 2 * (N + CH)
        ARENA = 30 * 1024
        arena = sb("arena", [P, ARENA])
        used = [0]

        def cut(*dims, dt=F32):
            n = int(np.prod(dims))
            words = n if dt == F32 else (n + 1) // 2
            a = arena[:, used[0]:used[0] + words]
            used[0] += words
            assert used[0] <= ARENA, used
            if dt != F32:
                a = a.bitcast(dt)
            if len(dims) == 1:
                return a
            names = "abcd"[:len(dims)]
            return a.rearrange(f"p ({' '.join(names)}) -> p {' '.join(names)}",
                               **{k: v for k, v in zip(names[1:], dims[1:])})

        block = ctx.enter_context(nc.Block())
        progs = {k: [] for k in ("pe", "dve", "act", "pool", "sp")}

        def vec(i):
            return vecs[:, i:i + 1]

        def col(t, a, n=CH):
            return t[:, bass.ds(a, n)]

        s_x = sem("x_loaded")
        s_const = sem("constants_loaded")
        consts = [(centre[:, :], w["centre"]), (mean_at[:, :], w["mean_at"]), (ident[:, :], w["ident"]),
                  (ident16[:, :], w["ident16"]), (pick[:, :], w["pick"]), (pick_e[:, :], w["pick_e"]),
                  (tie[:, :], w["tie"]), (mask[:, :], w["mask"]), (mask_t[:, :], w["mask_t"]), (vecs[:, :], w["vecs"]),
                  (bqk[:, :], w["bqk"]), (b1[:, :], w["b1"])]
        n_const = 16 * len(consts)

        waits_met = {e.engine: sem(f"waits_met_{n}") for n, e in (("dve", nc.vector), ("pool", nc.gpsimd))}

        def apart(e):
            e.sem_inc(waits_met[e.engine], 1)

        def load_sp(sp):
            for c in range(4):
                sp.dma_start(X[:, c * T:(c + 1) * T], x[:, c * T:(c + 1) * T]).then_inc(s_x, 16)

        def load_act(act):
            for dst, src in consts:
                act.dma_start(dst, src).then_inc(s_const, 16)
        s_b2 = sem("b2_loaded")
        s_b2z = sem("b2_zeroed")

        def zero_b2(pool):
            pool.memset(b2rep[:, :, :], 0.0).then_inc(s_b2z, 1)

        def load_b2(sp):
            sp.wait_ge(s_b2z, 1)
            for k in range(3):
                for part in range(3 - k):
                    sp.dma_start(b2rep[part * E:(part + 1) * E, k, :], w["b2"]).then_inc(s_b2, 16)
        progs["pool"].append(zero_b2)
        progs["sp"] += [load_sp, load_b2]
        progs["act"].append(load_act)

        def layer_norm(tag, src, keep_first, double, affine, shifted, pe_first, dve_first):
            cent = sem(f"{tag}_centred")
            copied = sem(f"{tag}_copied")
            squared = sem(f"{tag}_squared")
            summed = sem(f"{tag}_summed")
            dchain = sem(f"{tag}_dve_chain")
            rooted = sem(f"{tag}_rooted")
            scaled = sem(f"{tag}_scale_parts")
            spread = sem(f"{tag}_spread")
            normed = sem(f"{tag}_normed")
            done = sem(f"{tag}_done")
            SQ = [ln_scratch[:, i, :] for i in (0, 1)]
            TMP = [ln_scratch[:, i, :] for i in (2, 3)]
            PV = bank[2][0:96, 0:P]
            scales = 2 if keep_first else 1

            def hcol(c):
                return c * CH + (c // 2 + 1 if shifted else 0)

            def pe(e):
                pe_first(e)
                for c in range(NCH + 1):
                    if c < NCH:
                        if c >= 2:
                            e.wait_ge(copied, c - 1)
                        e.matmul(bank[c % 2], centre[:, :], src[:, c * CH:(c + 1) * CH],
                                 start=True, stop=True).then_inc(cent, 1)
                    if c >= 1:
                        e.wait_ge(squared, c)
                        for i in range(4 * (c - 1), 4 * c):
                            m = e.matmul(PV, mean_at[:, 31 - i:127 - i], SQ[(c - 1) % 2][:, (i % 4) * P:(i % 4 + 1) * P],
                                         start=(i == 0), stop=(i == NBLK - 1))
                        m.then_inc(summed, 1)
                for c in range(NCH):
                    if c == 0:
                        e.wait_ge(scaled, 1)
                    if c >= 2:
                        e.wait_ge(normed, scales * (c - 1))
                    for s in range(scales):
                        for i in range(4):
                            m = e.matmul(bank[3 + 2 * (c % 2) + s][:, i * P:(i + 1) * P],
                                         pick[0:96, 4 * c + i:4 * c + i + 1].to_broadcast([96, P]),
                                         rp[:, s, :], start=True, stop=True)
                    m.then_inc(spread, 1)

            def dve(e):
                dve_first(e)
                for c in range(NCH):
                    e.wait_ge(cent, c + 1)
                    e.tensor_copy(XC[:, c * CH:(c + 1) * CH], bank[c % 2]).then_inc(copied, 1)
                n = [0]

                def step(ins):
                    n[0] += 1
                    ins.then_inc(dchain, 1)
                    e.wait_ge(dchain, n[0])
                e.wait_ge(summed, NCH)
                ve, sd, r1, t1, r2, r12 = (v[:, :] for v in var)
                step(e.tensor_scalar(ve, PV, EPS, None, ALU.add))
                e.wait_ge(rooted, 1)
                step(e.reciprocal(r1, sd))
                if double:
                    step(e.tensor_tensor(t1, PV, r1, ALU.mult))
                    step(e.tensor_tensor(t1, t1, r1, ALU.mult))
                    step(e.tensor_scalar(t1, t1, EPS, None, ALU.add))
                    e.wait_ge(rooted, 2)
                    step(e.reciprocal(r2, sd))
                    step(e.tensor_tensor(r12, r1, r2, ALU.mult))
                parts = [r12] if double else [r1]
                if keep_first:
                    parts.append(r1)
                for s, r in enumerate(parts):
                    a, q = rp[:, s, :], lr[:, s, :]
                    step(e.tensor_copy(a, r))
                    step(e.tensor_tensor(q, r, a, ALU.subtract))
                    step(e.tensor_copy(a[32:64], q[32:64]))
                    step(e.tensor_copy(a[64:96], q[64:96]))
                    step(e.tensor_tensor(q[64:96], q[64:96], a[64:96], ALU.subtract))
                    last = e.tensor_copy(a[64:96], q[64:96])
                    if s == len(parts) - 1:
                        last.then_inc(scaled, 1)
                for c in range(NCH):
                    e.wait_ge(spread, c + 1)
                    xc = XC[:, c * CH:(c + 1) * CH]
                    hc = H[:, hcol(c):hcol(c) + CH]
                    if affine:
                        if c >= 2:
                            e.wait_ge(done, c - 1)
                        hc = TMP[c % 2]
                    ins = e.tensor_tensor(hc, xc, bank[3 + 2 * (c % 2)], ALU.mult)
                    ins.then_inc(normed, 1)
                    if keep_first:
                        e.tensor_tensor(XP[:, c * CH:(c + 1) * CH], xc, bank[4 + 2 * (c % 2)],
                                        ALU.mult).then_inc(normed, 1)

            def act(e):
                for c in range(NCH):
                    e.wait_ge(copied, c + 1)
                    if c >= 2:
                        e.wait_ge(summed, c - 1)
                    e.activation(SQ[c % 2], XC[:, c * CH:(c + 1) * CH], ACT.Square).then_inc(squared, 1)
                e.wait_ge(dchain, 1)
                e.activation(var[1][:, :], var[0][:, :], ACT.Sqrt).then_inc(rooted, 1)
                if double:
                    e.wait_ge(dchain, 5)
                    e.activation(var[1][:, :], var[3][:, :], ACT.Sqrt).then_inc(rooted, 1)
                if affine:
                    for c in range(NCH):
                        e.wait_ge(normed, scales * c + 1)
                        e.activation(H[:, hcol(c):hcol(c) + CH], TMP[c % 2], ACT.Identity,
                                     scale=vec(affine[0]), bias=vec(affine[1])).then_inc(done, 1)
            progs["pe"].append(pe)
            progs["dve"].append(dve)
            progs["act"].append(act)
            if affine:
                return lambda e, c: e.wait_ge(done, c)
            return lambda e, c: e.wait_ge(normed, scales * c)

        def time_mix():
            wts = cut(3, P)
            wo = cut(P)
            wm = cut(3, 2, P)
            mix1 = cut(3)
            negw = cut(1)
            PP, AA, BB = cut(T + 1), cut(T + 1), cut(T + 1)
            EA, EX = [cut(4, CH), cut(4, CH)], [cut(4, CH), cut(4, CH)]
            EV, NV, SR = [[cut(CH), cut(CH)] for _ in range(3)]
            G1, G3, PM = [[cut(CH), cut(CH)] for _ in range(3)]
            NUM, DN, RW = G1, G3, PM
            load = sem("tm_weights")
            ready = sem("tm_prepared")
            kvr = sem("tm_kvr_done")
            owd = sem("tm_out_done")
            dve = Steps(sem("tm_dve"), [
                "pp0", "pp1", "a0", "b0", "m0", "a1", "b1", "m1", "d0", "d1",
                "ev0", "ev1", "aa0", "bb0", "nv0", "aa1", "bb1", "nv1",
                "num0", "rec0", "ns0", "num1", "rw0", "rec1", "ns1", "rw1", "x0", "x1"])
            act = Steps(sem("tm_act"), ["sg0", "sg1", "ex0", "ex1"])
            pool = Steps(sem("tm_pool"), ["c0", "c1", "g0", "h0", "den0", "g1", "h1", "den1"])

            def f_sp(e):
                e.dma_start(wts, w["att_kvr"]).then_inc(load, 16)
                e.dma_start(wo, w["att_ow"]).then_inc(load, 16)

            def f_pool(e):
                pool.start(e)
                with e.Fori(1, B + 1) as it:
                    for c in range(2):
                        dve.wait(e, f"m{c}", it)
                        act.wait(e, f"ex{c}", it - 1)
                        e.tensor_tensor(EA[c][:, 2, :], PP[:, c * CH:(c + 1) * CH], PM[c],
                                        ALU.subtract).then_inc(pool.sem, 1)
                    for c in range(2):
                        act.wait(e, f"ex{c}", it)
                        dve.wait(e, f"bb{c}", it)
                        e.tensor_tensor(G1[c], EX[c][:, 2, :], AA[:, c * CH:(c + 1) * CH],
                                        ALU.mult).then_inc(pool.sem, 1)
                        e.tensor_tensor(G3[c], EX[c][:, 2, :], BB[:, c * CH:(c + 1) * CH],
                                        ALU.mult).then_inc(pool.sem, 1)
                        pool.wait(e, f"h{c}", it)
                        e.tensor_tensor(G3[c], G3[c], EX[c][:, 3, :], ALU.add).then_inc(pool.sem, 1)

            def f_act(e):
                e.wait_ge(s_const, n_const)
                e.activation(negw, vec(DECAY), ACT.Exp).then_inc(ready, 1)
                act.start(e)
                with e.Fori(1, B + 1) as it:
                    for c in range(2):
                        e.wait_ge(kvr, it * 2 + (c - 1))
                        dve.wait(e, f"ns{c}", it - 1)
                        e.activation(SR[c], bank[3 * c + 2], ACT.Sigmoid).then_inc(act.sem, 1)
                    for c in range(2):
                        dve.wait(e, f"d{c}", it)
                        pool.wait(e, f"c{c}", it)
                        dve.wait(e, f"num{c}", it - 1)
                        pool.wait(e, f"den{c}", it - 1)
                        e.activation(EX[c], EA[c], ACT.Exp).then_inc(act.sem, 1)

            def f_pe(e):
                e.wait_ge(ready, 3)

                def kvr_of(c, first):
                    for m in range(3):
                        for half in range(2):
                            last = e.matmul(bank[3 * c + m], wm[:, m, half, :], col(H, first - half),
                                            start=(half == 0), stop=(half == 1))
                    last.then_inc(kvr, 1)
                kvr_of(0, 1)
                with e.Fori(1, B + 1) as it:
                    at = it * (T + 1) - (T + 1)
                    dve.wait(e, "nv1", it - 1)
                    act.wait(e, "sg1", it - 1)
                    kvr_of(1, at + 1 + CH)
                    dve.wait(e, "rw0", it)
                    e.matmul(bank[6], wo, PM[0], start=True, stop=True).then_inc(owd, 1)
                    act.wait(e, "sg0", it)
                    kvr_of(0, at + 1 + T + 1)
                    dve.wait(e, "rw1", it)
                    e.matmul(bank[7], wo, PM[1], start=True, stop=True).then_inc(owd, 1)

            def f_dve(e):
                e.wait_ge(load, 32)
                e.wait_ge(s_const, n_const)
                e.memset(PP[:, 0:1], -1e38)
                e.memset(AA[:, 0:1], 0.0)
                e.memset(BB[:, 0:1], 0.0)
                e.tensor_scalar(mix1, vecs[:, TMK:TMR + 1], -1.0, 1.0, ALU.mult, ALU.add).then_inc(ready, 1)
                e.wait_ge(ready, 2)
                for m in range(3):
                    e.tensor_scalar(wm[:, m, 0, :], wts[:, m, :], vecs[:, TMK + m:TMK + m + 1], None, ALU.mult)
                    last = e.tensor_scalar(wm[:, m, 1, :], wts[:, m, :], mix1[:, m:m + 1], None, ALU.mult)
                last.then_inc(ready, 1)
                e.tensor_scalar(negw, negw, -1.0, None, ALU.mult).then_inc(ready, 1)
                e.wait_ge(ready, 4)
                dve.start(e)
                u = vec(FIRST)

                def inc(ins):
                    ins.then_inc(dve.sem, 1)
                with e.Fori(1, B + 1) as it:
                    xcol = it * T - T

                    def w_(name):
                        dve.wait(e, name, it)
                    lo = [slice(c * CH, (c + 1) * CH) for c in range(2)]
                    hi = [slice(c * CH + 1, (c + 1) * CH + 1) for c in range(2)]
                    for c in range(2):
                        e.wait_ge(kvr, it * 2 + (c - 1))
                        if c:
                            w_("pp0")
                        inc(e.tensor_tensor_scan(PP[:, hi[c]], negw.to_broadcast([P, CH]), bank[3 * c],
                                                 PP[:, c * CH:c * CH + 1], ALU.add, ALU.max))
                    for c in range(2):
                        w_(f"pp{c}")
                        inc(e.scalar_tensor_tensor(out=EA[c][:, 0, :], in0=PP[:, lo[c]], scalar=negw,
                                                   in1=PP[:, hi[c]], op0=ALU.add, op1=ALU.subtract))
                        inc(e.tensor_tensor(EA[c][:, 1, :], bank[3 * c], PP[:, hi[c]], ALU.subtract))
                        inc(e.scalar_tensor_tensor(out=PM[c], in0=bank[3 * c], scalar=u, in1=PP[:, lo[c]],
                                                   op0=ALU.add, op1=ALU.max))
                    for c in range(2):
                        w_(f"m{c}")
                        inc(e.scalar_tensor_tensor(out=EA[c][:, 3, :], in0=bank[3 * c], scalar=u, in1=PM[c],
                                                   op0=ALU.add, op1=ALU.subtract))
                    for c in range(2):
                        act.wait(e, f"ex{c}", it)
                        inc(e.tensor_tensor(EV[c], EX[c][:, 1, :], bank[3 * c + 1], ALU.mult))
                    for c in range(2):
                        w_("ev1" if c == 0 else "aa0")
                        inc(e.tensor_tensor_scan(AA[:, hi[c]], EX[c][:, 0, :], EV[c],
                                                 AA[:, c * CH:c * CH + 1], ALU.mult, ALU.add))
                        if c:
                            w_("bb0")
                        inc(e.tensor_tensor_scan(BB[:, hi[c]], EX[c][:, 0, :], EX[c][:, 1, :],
                                                 BB[:, c * CH:c * CH + 1], ALU.mult, ALU.add))
                        inc(e.tensor_tensor(NV[c], EX[c][:, 3, :], bank[3 * c + 1], ALU.mult))

                    def num(c):
                        pool.wait(e, f"den{c}", it)
                        w_(f"nv{c}")
                        inc(e.tensor_tensor(NUM[c], NV[c], G1[c], ALU.add))

                    def rec(c):
                        inc(e.reciprocal(DN[c], DN[c]))

                    def ns(c):
                        w_(f"num{c}")
                        inc(e.tensor_tensor(NUM[c], NUM[c], SR[c], ALU.mult))

                    def rw(c):
                        w_(f"ns{c}")
                        inc(e.tensor_tensor(RW[c], NUM[c], DN[c], ALU.mult))
                    num(0)
                    rec(0)
                    ns(0)
                    num(1)
                    rw(0)
                    rec(1)
                    ns(1)
                    rw(1)
                    for c in range(2):
                        e.wait_ge(owd, it * 2 + (c - 1))
                        xp = col(XP, xcol + c * CH)
                        inc(e.tensor_tensor(xp, bank[6 + c], xp, ALU.add))
            for k, f in (("sp", f_sp), ("pool", f_pool), ("act", f_act), ("pe", f_pe), ("dve", f_dve)):
                progs[k].append(f)
            return dve

        def channel_mix(wait_h):
            wk, wr, wv = cut(FB * P), cut(P), cut(FB, P)
            mix1 = cut(2)
            TK, TR, XK, XR = [[cut(CH), cut(CH)] for _ in range(4)]
            R = [cut(FB, CH), cut(FB, CH)]
            Q = [cut(FB, CH), cut(FB, CH)]
            SR = [cut(CH), cut(CH)]
            KV = [cut(CH), cut(CH)]
            XS = [cut(CH), cut(CH)]
            load = sem("cm_weights")
            ready = sem("cm_prepared")
            hidden = sem("cm_hidden_done")
            out_d = sem("cm_out_done")
            dve = Steps(sem("cm_dve"), ["tk0", "tr0", "xk0", "xr0", "tk1", "tr1", "xk1", "xr1",
                                        "sq0", "sq1", "kv0", "xa0", "kv1", "xa1"])
            act = Steps(sem("cm_act"), ["ra0", "rb0", "sg0", "ra1", "rb1", "sg1"])
            pool = Steps(sem("cm_pool"), ["xs0", "xs1", "sq0", "sq1"])

            def f_sp(e):
                tm_dve.wait(e, "x1", B)
                for dst, src in ((wk, w["f_kw"]), (wr, w["f_rw"]), (wv, w["f_vw"])):
                    e.dma_start(dst, src).then_inc(load, 16)

            def f_pe(e):
                e.wait_ge(load, 48)
                with e.Fori(1, B + 1) as it:
                    for c in range(2):
                        dve.wait(e, f"xr{c}", it)
                        for m in range(FB):
                            if m % 2 == 0:
                                act.wait(e, ("ra", "rb")[m // 2] + str(1 - c), it - 1 if c == 0 else it)
                            last = e.matmul(psum_pair[m // 2][:, m % 2, :], wk[:, m * P:(m + 1) * P], XK[c],
                                            start=True, stop=True)
                            if m % 2:
                                last.then_inc(hidden, 1)
                        act.wait(e, f"sg{c}", it - 1)
                        e.matmul(bank[c], wr, XR[c], start=True, stop=True).then_inc(hidden, 1)
                    for c in range(2):
                        dve.wait(e, f"sq{c}", it)
                        pool.wait(e, f"sq{c}", it)
                        dve.wait(e, f"kv{c}", it - 1)
                        for m in range(FB):
                            last = e.matmul(bank[(2, 7)[c]], wv[:, m, :], Q[c][:, m, :],
                                            start=(m == 0), stop=(m == FB - 1))
                        last.then_inc(out_d, 1)

            def f_act(e):
                act.start(e)
                with e.Fori(1, B + 1) as it:
                    for c in range(2):
                        for k in range(2):
                            e.wait_ge(hidden, it * 6 + (3 * c + k - 5))
                            dve.wait(e, f"sq{c}", it - 1)
                            pool.wait(e, f"sq{c}", it - 1)
                            e.activation(R[c][:, 2 * k:2 * k + 2, :], psum_pair[k][:, :, :],
                                         ACT.Relu).then_inc(act.sem, 1)
                        e.wait_ge(hidden, it * 6 + (3 * c - 3))
                        dve.wait(e, f"kv{c}", it - 1)
                        e.activation(SR[c], bank[c], ACT.Sigmoid).then_inc(act.sem, 1)

            def f_pool(e):
                tm_dve.wait(e, "x1", B)
                pool.start(e)
                with e.Fori(1, B + 1) as it:
                    for c in range(2):
                        at = it * T + (c * CH - T)
                        dve.wait(e, f"xa{c}", it - 1)
                        e.tensor_tensor(XS[c], col(X, at), col(XP, at), ALU.add).then_inc(pool.sem, 1)
                    for c in range(2):
                        act.wait(e, f"rb{c}", it)
                        e.tensor_tensor(Q[c][:, 2:4, :], R[c][:, 2:4, :], R[c][:, 2:4, :],
                                        ALU.mult).then_inc(pool.sem, 1)

            def f_dve(e):
                wait_h(e, NCH)
                e.tensor_scalar(mix1, vecs[:, FTMK:FTMR + 1], -1.0, 1.0, ALU.mult, ALU.add).then_inc(ready, 1)
                e.wait_ge(ready, 1)
                dve.start(e)

                def inc(ins):
                    ins.then_inc(dve.sem, 1)
                with e.Fori(1, B + 1) as it:
                    for c in range(2):
                        at = it * (T + 1) + (c * CH - T)
                        e.wait_ge(hidden, it * 6 + (3 * c - 6))
                        inc(e.tensor_scalar(TK[c], col(H, at - 1), mix1[:, 0:1], None, ALU.mult))
                        inc(e.tensor_scalar(TR[c], col(H, at - 1), mix1[:, 1:2], None, ALU.mult))
                        dve.wait(e, f"tk{c}", it)
                        inc(e.scalar_tensor_tensor(out=XK[c], in0=col(H, at), scalar=vec(FTMK), in1=TK[c],
                                                   op0=ALU.mult, op1=ALU.add))
                        dve.wait(e, f"tr{c}", it)
                        inc(e.scalar_tensor_tensor(out=XR[c], in0=col(H, at), scalar=vec(FTMR), in1=TR[c],
                                                   op0=ALU.mult, op1=ALU.add))
                    for c in range(2):
                        act.wait(e, f"ra{c}", it)
                        inc(e.tensor_tensor(Q[c][:, 0:2, :], R[c][:, 0:2, :], R[c][:, 0:2, :], ALU.mult))
                    for c in range(2):
                        at = it * T + (c * CH - T)
                        e.wait_ge(out_d, it * 2 + (c - 1))
                        act.wait(e, f"sg{c}", it)
                        inc(e.tensor_tensor(KV[c], bank[(2, 7)[c]], SR[c], ALU.mult))
                        dve.wait(e, f"kv{c}", it)
                        pool.wait(e, f"xs{c}", it)
                        inc(e.tensor_tensor(col(X, at), KV[c], XS[c], ALU.add))
            for k, f in (("sp", f_sp), ("pool", f_pool), ("act", f_act), ("pe", f_pe), ("dve", f_dve)):
                progs[k].append(f)
            return dve

        def experts(tag, before, wait_h, last_stage):
            used[0] = OPERANDS
            w1, w2 = cut(E, HB * P), cut(E, HB, P)
            gw = cut(E)
            GT = cut(N + CH, dt=BF16)
            HGT = [cut(HB, CH), cut(HB, CH)]
            r0 = used[0]
            R = [cut(HB, CH), cut(HB, CH)]
            G3 = arena[:, r0:r0 + NBLK * P // 2].bitcast(BF16).rearrange("p (b n) -> p b n", b=NBLK)
            LP, PA, KA, O1, O2 = (cut(NBLK, E) for _ in range(5))
            m1, m2, m3 = cut(NBLK), cut(NBLK), cut(NBLK)
            load = sem(f"{tag}_weights")
            zero = sem(f"{tag}_zeroed")
            logit = sem(f"{tag}_logits")
            chain = sem(f"{tag}_gate_chain")
            expd = sem(f"{tag}_gate_exp")
            turned = sem(f"{tag}_gates_turned")
            turned_s = sem(f"{tag}_gates_in_sbuf")
            z_done = sem(f"{tag}_hidden_done")
            relu_d = sem(f"{tag}_relu_done")
            gated = sem(f"{tag}_gated")
            y_done = sem(f"{tag}_expert_out_done")
            added = sem(f"{tag}_added")
            AHEAD, Y_AHEAD = 2, 4
            LEAD = 3
            hi_done = sem(f"{tag}_hidden_hi")
            lo_done = sem(f"{tag}_hidden_lo")
            w_hi = sem(f"{tag}_weights_hi")
            w_split = sem(f"{tag}_weights_split")
            hi_in = sem(f"{tag}_input_hi")
            in_split = sem(f"{tag}_input_split")

            def f_sp(e):
                before(e)
                for dst, src in ((gw, w["gate"]), (w1, w["W1"]), (w2, w["W2"])):
                    e.dma_start(dst, src).then_inc(load, 16)
                if last_stage:
                    stored = sem("stored")
                    with e.Fori(1, NCH + 1) as it:
                        e.wait_ge(added, it + AHEAD)
                        e.dma_start(out[:, bass.ds(it * CH - CH, CH)], col(X, it * CH - CH)).then_inc(stored, 16)
                    e.wait_ge(stored, 16 * NCH)

            def f_pool(e):
                before(e)
                e.memset(GT[:, N:N + CH], 0.0)
                e.memset(G3, 0.0).then_inc(zero, 1)
                e.memset(h_hi[:, N:N + CH].bitcast(F32), 0.0)
                e.memset(h_lo[:, N:N + CH].bitcast(F32), 0.0).then_inc(zero, 1)
                for k, (x_, hi, lo) in enumerate(((w1, w1_hi, w1_lo), (w2, w2_hi, w2_lo))):
                    e.wait_ge(w_hi, k + 1)
                    e.tensor_tensor(lo[:], x_, hi[:].bitcast(F32), ALU.subtract).then_inc(w_split, 1)
                e.wait_ge(logit, 1)
                for c in range(NCH):
                    r = slice(c * CH, (c + 1) * CH)
                    e.wait_ge(hi_in, c + 1)
                    e.tensor_tensor(h_lo[:, r], H[:, r], h_hi[:, r].bitcast(F32), ALU.subtract).then_inc(in_split, 1)

            n_load = 48
            lg = bank[0][:, 0:NBLK * E].rearrange("p (b e) -> p b e", e=E)
            turn = [bank[1].bitcast(BF16), bank[2].bitcast(BF16)]

            def f_pe(e):
                wait_h(e, NCH)
                e.wait_ge(load, n_load)
                for i in range(NBLK):
                    m = e.matmul(lg[:, i, :], H[:, i * P:(i + 1) * P], gw, start=True, stop=True)
                m.then_inc(logit, 1)
                e.wait_ge(chain, N_GATE)
                for q in range(NCH):
                    if q >= 2:
                        e.wait_ge(turned_s, q - 1)
                    for i in range(4):
                        m = e.transpose(turn[q % 2][:, i * P:(i + 1) * P], G3[:, 4 * q + i, :], ident16[:, :])
                    m.then_inc(turned, 1)

                def z(s, at, ex):
                    e.matmul(bank[1 + s], pick_e[:, ex:ex + 1].to_broadcast([P, P]), col(GT, at),
                             start=True, stop=True)
                    for k in range(HB):
                        ks = slice(k * P, (k + 1) * P)
                        e.matmul(psum_pair[s][:, k, :], w1_hi[:, ex, ks], col(h_hi, at), start=True, stop=False)
                        e.matmul(psum_pair[s][:, k, :], w1_hi[:, ex, ks], col(h_lo, at), start=False, stop=False)
                        m = e.matmul(psum_pair[s][:, k, :], w1_lo[:, ex, ks], col(h_hi, at), start=False, stop=True)
                    m.then_inc(z_done, 1)
                e.wait_ge(turned_s, NCH)
                e.wait_ge(w_split, 2)
                e.wait_ge(in_split, NCH)
                e.wait_ge(zero, 2)
                for ex in range(LEAD):
                    if ex >= 2:
                        e.wait_ge(relu_d, ex - 1 + AHEAD)
                        e.wait_ge(gated, ex - 1 + AHEAD)
                    z(ex % 2, 0, ex)
                with e.Fori(1, NCH // 2 + 1) as it:
                    for cc in range(2):
                        yb = bank[(0, 7)[cc]]
                        at = it * 2 * CH + (cc - 2) * CH
                        for ex in range(E):
                            s = it * 2 * E + ((cc - 2) * E + ex)
                            e.wait_ge(relu_d, s + (LEAD - 1) + AHEAD)
                            e.wait_ge(gated, s + (LEAD - 1) + AHEAD)
                            if ex + LEAD < E:
                                z((ex + LEAD) % 2, at, ex + LEAD)
                            else:
                                z((ex + LEAD) % 2, at + CH, ex + LEAD - E)
                            if ex == 0:
                                e.wait_ge(added, it * 2 + (cc - 2) + AHEAD - 1)
                                for k in range(3):
                                    e.matmul(yb, b2p[:, k, :], col(GT, at), start=(k == 0), stop=False)
                            e.wait_ge(hi_done, s + 1 + AHEAD)
                            e.wait_ge(lo_done, s + 1 + AHEAD)
                            for k in range(HB):
                                hi, lo = HG_HI[:, ex % 4, k, :], HG_LO[:, ex % 4, k, :]
                                e.matmul(yb, w2_hi[:, ex, k, :], hi, start=False, stop=False)
                                e.matmul(yb, w2_hi[:, ex, k, :], lo, start=False, stop=False)
                                m = e.matmul(yb, w2_lo[:, ex, k, :], hi, start=False,
                                             stop=(ex == E - 1 and k == HB - 1))
                            m.then_inc(y_done, 1)

            def f_act(e):
                e.wait_ge(load, n_load)
                e.activation(w1_hi[:], w1, ACT.Copy).then_inc(w_hi, 1)
                e.activation(w2_hi[:], w2, ACT.Copy).then_inc(w_hi, 1)
                for c in range(NCH):
                    wait_h(e, c + 1)
                    r = slice(c * CH, (c + 1) * CH)
                    e.activation(h_hi[:, r], H[:, r], ACT.Copy).then_inc(hi_in, 1)
                e.wait_ge(chain, 2)
                e.activation(PA, LP, ACT.Exp).then_inc(expd, 1)
                e.sem_inc(relu_d, AHEAD)
                e.wait_ge(chain, N_GATE)

                def relu(s, ex):
                    e.wait_ge(z_done, s + 1)
                    e.wait_ge(gated, s - 1 + AHEAD)
                    for k in range(HB):
                        ins = e.activation(R[ex % 2][:, k, :], psum_pair[ex % 2][:, k, :], ACT.Relu,
                                           bias=b1[:, ex * HB + k:ex * HB + k + 1])
                    ins.then_inc(relu_d, 1)
                relu(0, 0)
                with e.Fori(1, NCH // 2 + 1) as it:
                    for cc in range(2):
                        for ex in range(E):
                            s = it * 2 * E + ((cc - 2) * E + ex)
                            relu(s + 1, (ex + 1) % E)
                            e.wait_ge(gated, s + 1 + AHEAD)
                            e.wait_ge(y_done, s - 3 + Y_AHEAD)
                            e.activation(HG_HI[:, ex % 4], HGT[ex % 2], ACT.Copy).then_inc(hi_done, 1)

            N_GATE = 2 + 16 + 5

            def f_dve(e):
                n = [0]

                def step(ins, dep=True):
                    n[0] += 1
                    ins.then_inc(chain, 1)
                    if dep:
                        e.wait_ge(chain, n[0])
                e.wait_ge(load, n_load)
                if tag == "f1":
                    e.wait_ge(s_b2, 96)
                    b2c = sem("b2_chain")
                    cnt = [0]

                    def st(ins):
                        cnt[0] += 1
                        ins.then_inc(b2c, 1)
                        e.wait_ge(b2c, cnt[0])
                    st(e.tensor_copy(b2p[:, :, :], b2rep[:, :, :]))
                    st(e.tensor_tensor(b2t[:, :, :], b2rep[:, 1:3, :], b2p[:, 1:3, :], ALU.subtract))
                    st(e.tensor_copy(b2p[:, 1:3, :], b2t[:, :, :]))
                    st(e.tensor_tensor(b2t[:, 1, :], b2t[:, 1, :], b2p[:, 2, :], ALU.subtract))
                    st(e.tensor_copy(b2p[:, 2, :], b2t[:, 1, :]))

                def over(t):
                    return t.unsqueeze(2).to_broadcast([P, NBLK, E])
                tie_b = tie[:, :].unsqueeze(1).to_broadcast([P, NBLK, E])
                e.wait_ge(logit, 1)
                step(e.tensor_reduce(m1, lg, AX.X, ALU.max))
                step(e.tensor_tensor(LP, lg, over(m1), ALU.subtract))
                e.wait_ge(expd, 1)
                step(e.tensor_reduce(m1, PA, AX.X, ALU.max))
                step(e.tensor_tensor(KA, PA, over(m1), ALU.is_ge))
                step(e.tensor_tensor(KA, KA, tie_b, ALU.mult))
                step(e.tensor_reduce(m2, KA, AX.X, ALU.max))
                step(e.tensor_tensor(O1, KA, over(m2), ALU.is_equal))
                step(e.scalar_tensor_tensor(out=LP, in0=O1, scalar=-2.0, in1=PA, op0=ALU.mult, op1=ALU.add))
                step(e.tensor_reduce(m1, LP, AX.X, ALU.max))
                step(e.tensor_tensor(KA, LP, over(m1), ALU.is_ge))
                step(e.tensor_tensor(KA, KA, tie_b, ALU.mult))
                step(e.tensor_reduce(m2, KA, AX.X, ALU.max))
                step(e.tensor_tensor(O2, KA, over(m2), ALU.is_equal))
                step(e.tensor_tensor(O1, O1, O2, ALU.add))
                step(e.tensor_tensor(PA, PA, O1, ALU.mult))
                step(e.tensor_reduce(m3, PA, AX.X, ALU.add))
                step(e.reciprocal(m1, m3))
                step(e.tensor_tensor(PA, PA, over(m1), ALU.mult))
                e.wait_ge(zero, 1)
                step(e.tensor_copy(G3[:, :, 0:E], PA))
                step(e.tensor_tensor(KA, PA, G3[:, :, 0:E], ALU.subtract))
                step(e.tensor_copy(G3[:, :, E:2 * E], KA))
                step(e.tensor_tensor(LP, KA, G3[:, :, E:2 * E], ALU.subtract))
                step(e.tensor_copy(G3[:, :, 2 * E:3 * E], LP))
                assert n[0] == N_GATE
                for q in range(NCH):
                    e.wait_ge(turned, q + 1)
                    e.tensor_copy(GT[:, q * CH:(q + 1) * CH], turn[q % 2][:, 0:CH]).then_inc(turned_s, 1)
                e.sem_inc(gated, AHEAD)
                e.sem_inc(added, AHEAD)
                e.sem_inc(lo_done, AHEAD)

                def gate(s, ex):
                    e.wait_ge(relu_d, s + 1 + AHEAD)
                    e.wait_ge(hi_done, s - 1 + AHEAD)
                    e.wait_ge(lo_done, s - 1 + AHEAD)
                    e.tensor_tensor(HGT[ex % 2], R[ex % 2],
                                    bank[1 + ex % 2].unsqueeze(1).to_broadcast([P, HB, CH]),
                                    ALU.mult).then_inc(gated, 1)

                def add(chunk, cc):
                    e.wait_ge(y_done, (chunk + 1) * E + Y_AHEAD)
                    xc = col(X, chunk * CH)
                    e.tensor_tensor(xc, bank[(0, 7)[cc]], xc, ALU.add).then_inc(added, 1)

                def body(it, first):
                    for cc in range(2):
                        for ex in range(E):
                            s = it * 2 * E + ((cc - 2) * E + ex)
                            gate(s + 1, (ex + 1) % E)
                            e.wait_ge(gated, s + 1 + AHEAD)
                            e.wait_ge(hi_done, s + 1 + AHEAD)
                            e.tensor_tensor(HG_LO[:, ex % 4], HGT[ex % 2], HG_HI[:, ex % 4].bitcast(F32),
                                            ALU.subtract).then_inc(lo_done, 1)
                            if ex == LEAD and not (first and cc == 0):
                                add(it * 2 + (cc - 3), 1 - cc)
                gate(0, 0)
                body(1, True)
                with e.Fori(2, NCH // 2 + 1) as it:
                    body(it, False)
                add(NCH - 1, 1)

            def f_pool2(e):
                e.sem_inc(y_done, Y_AHEAD)
                e.sem_inc(hi_done, AHEAD)
            for k, f in (("sp", f_sp), ("pool", f_pool), ("pool", f_pool2), ("act", f_act), ("pe", f_pe),
                         ("dve", f_dve)):
                progs[k].append(f)
            return lambda e: e.wait_ge(added, NCH + AHEAD)

        scr_q = nc.dram_tensor("scratch_q_parts", (B, 3, 2, P, CH), BF16, kind="Internal").ap()
        scr_k = nc.dram_tensor("scratch_k_parts", (B, 3, P, T), BF16, kind="Internal").ap()
        scr_v = nc.dram_tensor("scratch_values", (B, HG, P, VG), F32, kind="Internal").ap()
        scr_rel = nc.dram_tensor("scratch_bias_parts", (HG, 3, HG, S, T), BF16, kind="Internal").ap()
        scr_max = nc.dram_tensor("scratch_max_parts", (HG, 3, HG * 8, P), BF16, kind="Internal").ap()

        def attention(before, wait_h):
            QL = cut(HG, 2, HG, CH, dt=BF16)
            QU = cut(HG, HG, CH, dt=BF16)
            KK = cut(HG, HG, T, dt=BF16)
            VS = cut(HG, VG + 32)
            wqkv, wo = cut(3, P), cut(P)
            grid, rel = cut(T), cut(NH * S)
            bqs = cut(1)
            VA = cut(HG, 8, HG * VW)
            dump = [cut(CH, dt=BF16), cut(CH, dt=BF16)]
            NM = [cut(2, HG, 4), cut(2, HG, 4)]
            PF = [cut(HG, 4), cut(HG, 4)]
            NF, NR = cut(P), cut(P)
            N3 = [cut(3, P, dt=BF16), cut(3, P, dt=BF16)]
            RC = [cut(4, HG), cut(4, HG)]
            QF, KF, QR, KR = (XC[:, i * T:(i + 1) * T] for i in range(4))
            half_ = 3 * T // 2
            Q3 = XP[:, 0:half_].bitcast(BF16).rearrange("p (a n) -> p a n", a=3)
            K3 = XP[:, half_:2 * half_].bitcast(BF16).rearrange("p (a n) -> p a n", a=3)
            VT = [XP[:, 2 * half_ + i * CH:2 * half_ + (i + 1) * CH] for i in range(2)]
            PR = [b_[:, i * 4 * CH:(i + 1) * 4 * CH].rearrange("p (j n) -> p j n", j=HG)
                  for b_ in (XC, XP) for i in range(2)]

            ATT = H[:, 0:T].rearrange("p (k c) -> p k c", k=8)
            ATTT = H[:, T:2 * T]
            OS = [H[:, 2 * T + i * CH:2 * T + (i + 1) * CH] for i in range(2)]

            load = sem("at_weights")
            const_rows = sem("at_key_rows")
            prep = sem("at_prepared")
            rel_mm = sem("at_rel_product")
            rel_ch = sem("at_rel_chain")
            rel_st = sem("at_rel_stored")
            rel_ld = sem("at_rel_loaded")
            pe_s = Steps(sem("at_pe"), ["q0", "k0", "v0", "q1", "k1", "v1", "t0", "t1"])
            act_s = Steps(sem("at_act"), ["q0", "k0", "v0", "q1", "k1", "v1", "va0", "va1"])
            dve_s = Steps(sem("at_dve"), ["c1", "r1", "c2", "c3"])
            pool_s = Steps(sem("at_pool"), ["c1", "r1", "c2", "c3"])
            stored = sem("at_parts_stored")
            slot_ld = [sem(f"at_slot{i}_loaded") for i in range(HG)]
            SLOT = 16 * 13
            ring_ready = sem("at_ring_ready")
            ring_free = sem("at_ring_free")
            pm_ready = sem("at_maxima_ready")
            nm_chain = sem("at_max_chain")
            nm_ready = sem("at_max_parts_ready")
            nm_stored = sem("at_max_parts_stored")
            nm_loaded = [sem(f"at_slot{i}_max_rows_loaded") for i in range(HG)]
            sc_ready = sem("at_scores_ready")
            exp_done = sem("at_exp_done")
            pv_done = sem("at_pv_done")
            os_done = sem("at_out_copied")
            rc_done = sem("at_recip_done")
            RING = 3
            PRO = 2 * (len(PIECES) + 1)
            IPB = HG * (len(PIECES) + 3) + 4

            def plan(hg, with_max):
                ev, left = [], list(PIECES) if with_max else []
                for i in range(NP_):
                    for half in range(2):
                        ev.append(("scores", 2 * i + half))
                        for _ in range((3, 2)[half]):
                            if left:
                                ev.append(("piece", left.pop(0)))
                    if i >= 1:
                        ev.append(("pv", i - 1))
                    if i == HALF_END[0] + 2:
                        ev.append(("turn_out", 0))
                while left:
                    ev.append(("piece", left.pop(0)))
                ev += [("pv", NP_ - 1), ("turn_out", 1)]
                if with_max:
                    ev.append(("maxima", None))
                if hg == HG - 1:
                    ev += [("turn_att", 0), ("turn_att", 1), ("out", 0), ("out", 1)]
                return ev

            RINGED = ("piece", "turn_out", "maxima", "turn_att", "out")

            def steps_of(last):
                n, res = 0, []
                for hg in range(HG):
                    ev = []
                    for kind, arg in plan(hg, not last or hg < 2):
                        ev.append((kind, arg, n))
                        n += kind in RINGED
                    res.append((hg, ev))
                return res, n
            assert steps_of(False)[1] == IPB
            TOTAL = PRO + (B - 1) * IPB + steps_of(True)[1]

            def item_no(it, local):
                return it * IPB + (PRO - IPB + local)

            def over_batches(eng, body):
                with eng.Fori(1, B) as it:
                    body(it, False)
                body(B, True)

            def load_slot(e, b, hg):
                bs = bass.ds(b, 1)
                rows = slice(hg * 32, (hg + 1) * 32)

                def move(dst, src):
                    e.dma_start(dst, src).then_inc(slot_ld[hg], 16)
                for part, row, reps in ((0, 0, 3), (1, 3 * D, 2), (2, 5 * D, 1)):
                    dst = slice(row, row + reps * D)
                    for half in range(2):
                        src = scr_q[bs, part, half, rows, :].rearrange("o (d j) n -> o d (j n)", j=HG)
                        if reps > 1:
                            src = src.to_broadcast([reps, D, HG * CH])
                        else:
                            src = src.rearrange("o d n -> (o d) n")
                        move(QL[dst, hg, half, :, :].rearrange("p j n -> p (j n)"), src)
                        if half:
                            move(QU[dst, hg, :, :].rearrange("p j n -> p (j n)"), src)
                    src = scr_k[bs, 0:reps, rows, :].rearrange("o t (d j) n -> (o t) d (j n)", j=HG)
                    move(KK[dst, hg, :, :].rearrange("p j n -> p (j n)"), src)
                e.dma_start(VS[:, hg, 0:VG], scr_v[bs, hg, :, :].rearrange("o p n -> (o p) n"))\
                    .then_inc(slot_ld[hg], 16)

            def send_maxima(e, n, slot, par):
                e.wait_ge(nm_ready, n + 1)
                e.dma_start(scr_max[slot].rearrange("t r i -> r t i"), N3[par][0:32]).then_inc(nm_stored, 16)
                e.wait_ge(nm_stored, n * 16 + 16)
                rows = scr_max[slot].rearrange("t r i -> t (r i)")
                e.dma_start(QL[MAX0:ROWS, slot].rearrange("p a j n -> p (a j n)"), rows).then_inc(nm_loaded[slot], 16)
                e.dma_start(QU[MAX0:ROWS, slot].rearrange("p j n -> p (j n)"), rows[:, HG * CH:])\
                    .then_inc(nm_loaded[slot], 16)

            def f_sp(e):
                before(e)
                for dst, src in ((wqkv, w["wqkv"]), (wo, w["wo"]), (grid[0:S], w["grid_t"]),
                                 (rel[0:S], w["rel"].rearrange("i h j -> i (h j)"))):
                    e.dma_start(dst, src).then_inc(load, 16)
                for s in range(HG):
                    e.dma_start(KK[REL0:ROWS, s, :, :], w["key_rows"].unsqueeze(1).to_broadcast([3 * SW + 3, HG, T]))\
                        .then_inc(const_rows, 16)
                for hg in range(HG):
                    e.wait_ge(rel_ch, 5 * hg + 5)
                    e.dma_start(scr_rel[hg].rearrange("t j s n -> (j s) t n"), Q3).then_inc(rel_st, 16)
                    e.wait_ge(rel_st, 16 * hg + 16)
                    for p in range(3):
                        rows = slice(REL0 + p * SW, REL0 + (p + 1) * SW)
                        for half in range(2):
                            e.dma_start(QL[rows, hg, half, :, :], scr_rel[hg, p, :, 0:SW, half * CH:(half + 1) * CH]
                                        .rearrange("j s n -> s j n")).then_inc(rel_ld, 16)
                        e.dma_start(QU[rows, hg, :, :], scr_rel[hg, p, :, S - SW:S, CH:T]
                                    .rearrange("j s n -> s j n")).then_inc(rel_ld, 16)
                with e.Fori(1, B + 1) as it:
                    bs = bass.ds(it - 1, 1)
                    dve_s.wait(e, "c3", it)
                    e.dma_start(scr_q[bs].rearrange("o t a p n -> (o p) (t a) n"),
                                Q3.rearrange("p t (a n) -> p (t a) n", a=2)).then_inc(stored, 16)
                    pool_s.wait(e, "c3", it)
                    e.dma_start(scr_k[bs].rearrange("o t p n -> (o p) t n"), K3).then_inc(stored, 16)
                    act_s.wait(e, "va1", it)
                    e.dma_start(scr_v[bs].rearrange("o g p n -> (o p) g n"),
                                VA.rearrange("p g k n -> p g (k n)"))\
                        .then_inc(stored, 16)
                e.wait_ge(stored, 48 * B)
                for hg in range(HG):
                    load_slot(e, 0, hg)
                for n in range(2):
                    send_maxima(e, n, n, n % 2)

                def body(it, last):
                    for hg in range(HG):
                        if not last or hg < 2:
                            send_maxima(e, it * HG + (hg - 2), (hg + 2) % HG, hg % 2)
                        if not last:
                            e.wait_ge(pv_done, it * 40 + (10 * hg + 10 + NPB - 40))
                            load_slot(e, it, hg)
                over_batches(e, body)

            def f_pool(e):
                before(e)
                e.memset(VS[:, :, VG:VG + 32], 0.0)
                e.memset(VA.rearrange("p g k n -> p (g k n)")[:, D::VW], 1.0).then_inc(prep, 1)
                pool_s.start(e)
                with e.Fori(1, B + 1) as it:
                    act_s.wait(e, "k1", it)
                    e.wait_ge(stored, it * 48 - 48)
                    apart(e)
                    e.tensor_scalar(K3[:, 0, :], KF, 1.0, None, ALU.mult).then_inc(pool_s.sem, 1)
                    pool_s.wait(e, "c1", it)
                    e.tensor_tensor(KR, KF, K3[:, 0, :], ALU.subtract).then_inc(pool_s.sem, 1)
                    pool_s.wait(e, "r1", it)
                    apart(e)
                    e.tensor_scalar(K3[:, 1, :], KR, 1.0, None, ALU.mult).then_inc(pool_s.sem, 1)
                    pool_s.wait(e, "c2", it)
                    e.tensor_tensor(K3[:, 2, :], KR, K3[:, 1, :], ALU.subtract).then_inc(pool_s.sem, 1)

            def f_act(e):
                before(e)
                e.wait_ge(s_const, n_const)
                e.activation(bqs, bqk[:, 0:1], ACT.Copy, scale=SCALE).then_inc(prep, 1)
                e.wait_ge(prep, 2)
                e.wait_ge(rel_st, 16 * HG)
                act_s.start(e)
                with e.Fori(1, B + 1) as it:
                    for c in range(2):
                        r = slice(c * CH, (c + 1) * CH)
                        pe_s.wait(e, f"q{c}", it)
                        dve_s.wait(e, "r1", it - 1)
                        e.activation(QF[:, r], bank[c], ACT.Identity, bias=bqs, scale=SCALE).then_inc(act_s.sem, 1)
                        pe_s.wait(e, f"k{c}", it)
                        pool_s.wait(e, "r1", it - 1)
                        e.activation(KF[:, r], bank[(2, 7)[c]], ACT.Identity, bias=bqk[:, 1:2])\
                            .then_inc(act_s.sem, 1)
                        pe_s.wait(e, f"v{c}", it)
                        pe_s.wait(e, f"t{c}", it - 1)
                        e.activation(VT[c], bank[3 + c], ACT.Identity, bias=vec(BV)).then_inc(act_s.sem, 1)
                    for c in range(2):
                        pe_s.wait(e, f"t{c}", it)
                        e.wait_ge(stored, it * 48 - 48)
                        for i in range(4):
                            src = bank[5 + c][:, i * P:(i + 1) * P].rearrange("p (g j d) -> p g j d", g=HG, j=HG)
                            dst = VA[:, :, 4 * c + i, :].rearrange("p g (j w) -> p g j w", w=VW)[:, :, :, 0:D]
                            ins = e.activation(dst, src, ACT.Copy)
                        ins.then_inc(act_s.sem, 1)
                e.wait_ge(stored, 48 * B)
                e.sem_inc(exp_done, 2)
                e.sem_inc(os_done, 1)

                def body(it, last):
                    steps, _ = steps_of(last)
                    where = {}
                    for hg, ev in steps:
                        for kind, arg, n in ev:
                            if kind == "turn_out":
                                where[hg, arg] = n
                    before_ = {a: n - IPB for hg, ev in steps_of(False)[0] if hg == HG - 1
                               for kind, a, n in ev if kind == "turn_out"}

                    def copy_out(hg, half):
                        e.wait_ge(pv_done, it * 40 + (10 * hg + HALF_END[half] + 1 + NPB - 40))
                        e.wait_ge(ring_ready, item_no(it, where[hg - 1, half] if hg else before_[half]) + 1)
                        e.activation(OS[half], bank[7], ACT.Copy).then_inc(os_done, 1)
                    for hg in range(HG):
                        for t in range(2 * NP_):
                            i, h = t // 2, t % 2
                            wid = max(p[3] + p[2] for p in PACKS[i])
                            e.wait_ge(sc_ready, it * 80 + (20 * hg + t + 1 - 80))
                            e.wait_ge(pv_done, it * 40 + (10 * hg + i + 1 - 40))
                            e.activation(PR[(10 * hg + i) % NPB][:, 2 * h:2 * h + 2, 0:wid],
                                         psum_pair[t % 2][:, :, 0:wid], ACT.Exp).then_inc(exp_done, 1)
                            if t == 2 * HALF_END[0] + 3:
                                copy_out(hg, 0)
                        copy_out(hg, 1)
                over_batches(e, body)

            def f_pe(e):
                before(e)
                e.wait_ge(load, 64)
                for hg in range(HG):
                    for c in range(2):
                        if hg:
                            e.wait_ge(rel_ch, 5 * hg - 4)
                        m = e.matmul(bank[c], rel[0:S, hg * P:(hg + 1) * P], grid[0:S, c * CH:(c + 1) * CH],
                                     start=True, stop=True)
                    m.then_inc(rel_mm, 1)
                e.wait_ge(rel_ch, 5 * HG - 4)
                wait_h(e, NCH)
                pe_s.start(e)
                with e.Fori(1, B + 1) as it:
                    for c in range(2):
                        for k, bk in enumerate((bank[c], bank[(2, 7)[c]], bank[3 + c])):
                            act_s.wait(e, f"{'qkv'[k]}{c}", it - 1)
                            e.matmul(bk, wqkv[:, k, :], col(H, it * T + (c * CH - T)),
                                     start=True, stop=True).then_inc(pe_s.sem, 1)
                    for c in range(2):
                        act_s.wait(e, f"v{c}", it)
                        act_s.wait(e, f"va{c}", it - 1)
                        for i in range(4):
                            m = e.transpose(bank[5 + c][:, i * P:(i + 1) * P], VT[c][:, i * P:(i + 1) * P],
                                            ident[:, :])
                        m.then_inc(pe_s.sem, 1)
                act_s.wait(e, "va1", B)
                e.wait_ge(const_rows, 16 * HG)
                e.wait_ge(rel_ld, 16 * 9 * HG)

                def piece(slot, p, bk):
                    j, qb, k0, n, _ = p
                    q = slice(qb % 4 * P, qb % 4 * P + P)
                    lhs = QL[0:MAX0, slot, qb // 4, j, q] if k0 == 0 else QU[0:MAX0, slot, j, q]
                    return e.matmul(bk[:, 0:n], lhs, KK[0:MAX0, slot, j, k0:k0 + n], start=True, stop=True)

                def maxima(n, par, bk):
                    e.wait_ge(pm_ready, n + 1)
                    return e.transpose(bk[0:32, 0:P], NM[par].rearrange("p a j q -> p (a j q)"), ident[:, :])
                no = 0
                for g in range(2):
                    e.wait_ge(slot_ld[g], SLOT)
                    for p in PIECES:
                        if no >= RING:
                            e.wait_ge(ring_free, no - RING + 1)
                        piece(g, p, bank[no % RING]).then_inc(ring_ready, 1)
                        no += 1
                    e.wait_ge(ring_free, no - RING + 1)
                    maxima(g, g % 2, bank[no % RING]).then_inc(ring_ready, 1)
                    no += 1
                assert no == PRO
                e.sem_inc(pv_done, NPB)

                def body(it, last):
                    for hg, ev in steps_of(last)[0]:
                        slot2 = (hg + 2) % HG
                        e.wait_ge(nm_loaded[hg], it * 32)
                        e.wait_ge(slot_ld[hg], it * SLOT)
                        if not last or hg < 2:
                            e.wait_ge(slot_ld[slot2], it * SLOT + (SLOT if hg >= 2 else 0))
                        for kind, arg, local in ev:
                            if kind in RINGED:
                                bk = bank[local % RING]
                                e.wait_ge(ring_free, item_no(it, max(local - RING + 1, 0)))
                            if kind == "piece":
                                piece(slot2, arg, bk).then_inc(ring_ready, 1)
                            elif kind == "maxima":
                                maxima(it * HG + (hg - 2), hg % 2, bk).then_inc(ring_ready, 1)
                            elif kind == "scores":
                                e.wait_ge(exp_done, it * 80 + (20 * hg + arg - 1 + 2 - 80))
                                for kb, n0, n, c0 in PACKS[arg // 2]:
                                    diagonal = kb * P == n0
                                    for jj in range(2):
                                        j = 2 * (arg % 2) + jj
                                        q = slice(n0 % CH, n0 % CH + n)
                                        rhs = QL[0:ROWS, hg, n0 // CH, j, q] if kb < 4 else QU[0:ROWS, hg, j, q]
                                        m = e.matmul(psum_pair[arg % 2][:, jj, c0:c0 + n],
                                                     KK[0:ROWS, hg, j, kb * P:(kb + 1) * P], rhs,
                                                     start=True, stop=True)
                                        if diagonal:
                                            m = e.matmul(psum_pair[arg % 2][:, jj, c0:c0 + P], ident16[:, :],
                                                         mask_t[:, :], start=False, stop=True,
                                                         skip_group_check=True)
                                m.then_inc(sc_ready, 1)
                            elif kind == "pv":
                                e.wait_ge(exp_done, it * 80 + (20 * hg + 2 * arg + 2 + 2 - 80))
                                first = arg in (0, HALF_END[0] + 1)
                                if first:
                                    half = int(arg > 0)
                                    e.wait_ge(os_done, it * (2 * HG) + (2 * hg + half + 1 - 2 * HG))
                                for kb, n0, n, c0 in PACKS[arg]:
                                    q0 = n0 % CH
                                    for j in range(HG):
                                        v0 = (kb * HG + j) * VW
                                        m = e.matmul(bank[7][32 * j:32 * j + 32, q0:q0 + n], VS[:, hg, v0:v0 + 32],
                                                     PR[(10 * hg + arg) % NPB][:, j, c0:c0 + n],
                                                     start=first, stop=arg in HALF_END,
                                                     skip_group_check=True)
                                m.then_inc(pv_done, 1)
                            elif kind == "turn_out":
                                e.wait_ge(os_done, it * (2 * HG) + (2 * hg + arg + 2 - 2 * HG))
                                for i in range(4):
                                    m = e.transpose(bk[:, i * P:(i + 1) * P], OS[arg][:, i * P:(i + 1) * P],
                                                    ident[:, :])
                                m.then_inc(ring_ready, 1)
                            elif kind == "turn_att":
                                e.wait_ge(ring_free, item_no(it, local - arg))
                                for i in range(4):
                                    m = e.transpose(bk[:, i * P:(i + 1) * P], ATT[:, 4 * arg + i, :], ident[:, :])
                                m.then_inc(ring_ready, 1)
                            elif kind == "out":
                                e.wait_ge(ring_free, item_no(it, local - 1))
                                e.matmul(bk, wo, ATTT[:, arg * CH:(arg + 1) * CH], start=True, stop=True)\
                                    .then_inc(ring_ready, 1)
                over_batches(e, body)

            def f_dve(e):
                for hg in range(HG):
                    e.wait_ge(rel_mm, hg + 1)
                    if hg:
                        e.wait_ge(rel_st, 16 * hg)
                    for c in range(2):
                        ins = e.tensor_scalar(QF[:, c * CH:(c + 1) * CH], bank[c], GRID_SCALE, None, ALU.mult)
                    ins.then_inc(rel_ch, 1)
                    e.wait_ge(rel_ch, 5 * hg + 1)
                    e.tensor_copy(Q3[:, 0, :], QF).then_inc(rel_ch, 1)
                    e.wait_ge(rel_ch, 5 * hg + 2)
                    e.tensor_tensor(QR, QF, Q3[:, 0, :], ALU.subtract).then_inc(rel_ch, 1)
                    e.wait_ge(rel_ch, 5 * hg + 3)
                    e.tensor_copy(Q3[:, 1, :], QR).then_inc(rel_ch, 1)
                    e.wait_ge(rel_ch, 5 * hg + 4)
                    e.tensor_tensor(Q3[:, 2, :], QR, Q3[:, 1, :], ALU.subtract).then_inc(rel_ch, 1)
                dve_s.start(e)
                with e.Fori(1, B + 1) as it:
                    act_s.wait(e, "q1", it)
                    e.wait_ge(stored, it * 48 - 48)
                    e.tensor_copy(Q3[:, 0, :], QF).then_inc(dve_s.sem, 1)
                    dve_s.wait(e, "c1", it)
                    e.tensor_tensor(QR, QF, Q3[:, 0, :], ALU.subtract).then_inc(dve_s.sem, 1)
                    dve_s.wait(e, "r1", it)
                    e.tensor_copy(Q3[:, 1, :], QR).then_inc(dve_s.sem, 1)
                    dve_s.wait(e, "c2", it)
                    e.tensor_tensor(Q3[:, 2, :], QR, Q3[:, 1, :], ALU.subtract).then_inc(dve_s.sem, 1)

                def piece(p, par, bk, no):
                    j, qb, k0, n, diag = p
                    if not diag:
                        e.tensor_reduce(PF[par][:, j, qb - 4:qb - 3], bk[:, 0:n], AX.X, ALU.max).then_inc(ring_free, 1)
                        return
                    apart(e)
                    e.tensor_tensor_reduce(dump[no % 2][:, 0:n], bk[:, 0:n], mask[:, CH - n:CH], 1.0, 1e8 * NEG,
                                           ALU.add, ALU.max, NM[par][:, qb // 4, j, qb % 4:qb % 4 + 1]).then_inc(ring_free, 1)

                def combine(par, after):
                    e.wait_ge(ring_free, after)
                    e.tensor_tensor(NM[par][:, 1], NM[par][:, 1], PF[par], ALU.max).then_inc(pm_ready, 1)

                def maxima(n, par, bk, after):
                    if not isinstance(n, int) or n >= 2:
                        e.wait_ge(nm_stored, n * 16 - 16)
                    e.tensor_scalar(NF[0:32], bk[0:32, 0:P], -1.0, None, ALU.mult).then_inc(ring_free, 1)
                    e.wait_ge(ring_free, after)
                    e.tensor_copy(N3[par][0:32, 0, :], NF[0:32]).then_inc(nm_chain, 1)
                    e.wait_ge(nm_chain, n * 3 + 1)
                    e.tensor_tensor(NR[0:32], NF[0:32], N3[par][0:32, 0, :], ALU.subtract).then_inc(nm_chain, 1)
                    e.wait_ge(nm_chain, n * 3 + 2)
                    e.tensor_copy(N3[par][0:32, 1, :], NR[0:32]).then_inc(nm_chain, 1)
                    e.wait_ge(nm_chain, n * 3 + 3)
                    e.tensor_tensor(N3[par][0:32, 2, :], NR[0:32], N3[par][0:32, 1, :], ALU.subtract)\
                        .then_inc(nm_ready, 1)
                no = 0
                for g in range(2):
                    for i, p in enumerate(PIECES):
                        e.wait_ge(ring_ready, no + 1)
                        if no >= 2:
                            e.wait_ge(ring_free, no - 1)
                        piece(p, g % 2, bank[no % RING], no)
                        no += 1
                    combine(g % 2, no)
                    e.wait_ge(ring_ready, no + 1)
                    maxima(g, g % 2, bank[no % RING], no + 1)
                    no += 1

                def body(it, last):
                    for hg, ev in steps_of(last)[0]:
                        pieces = 0
                        for kind, arg, local in ev:
                            if kind not in RINGED:
                                continue
                            bk = bank[local % RING]
                            e.wait_ge(ring_ready, item_no(it, local) + 1)
                            e.wait_ge(ring_free, item_no(it, local) - 1)
                            if kind == "piece":
                                piece(arg, hg % 2, bk, local)
                                pieces += 1
                                if pieces == len(PIECES):
                                    combine(hg % 2, item_no(it, local) + 1)
                            elif kind == "maxima":
                                maxima(it * HG + (hg - 2), hg % 2, bk, item_no(it, local) + 1)
                            elif kind == "turn_out":
                                v = bk.rearrange("p (k j w) -> p k j w", k=4, j=HG)
                                e.reciprocal(RC[arg], v[:, :, :, D:VW].rearrange("p k j w -> p k (j w)")).then_inc(rc_done, 1)
                                e.wait_ge(rc_done, it * (2 * HG) + (2 * hg + arg + 1 - 2 * HG))
                                o = ATT[:, 4 * arg:4 * arg + 4, hg * 32:(hg + 1) * 32]
                                e.tensor_tensor(o.rearrange("p k (j d) -> p k j d", j=HG), v[:, :, :, 0:D],
                                                RC[arg].unsqueeze(3).to_broadcast([P, 4, HG, D]), ALU.mult)\
                                    .then_inc(ring_free, 1)
                            elif kind == "turn_att":
                                e.tensor_copy(ATTT[:, arg * CH:(arg + 1) * CH], bk).then_inc(ring_free, 1)
                            elif kind == "out":
                                xc = col(X, it * T + (arg * CH - T))
                                e.scalar_tensor_tensor(out=xc, in0=bk, scalar=vec(BO), in1=xc, op0=ALU.add,
                                                       op1=ALU.add).then_inc(ring_free, 1)
                over_batches(e, body)

            for k, f in (("sp", f_sp), ("pool", f_pool), ("act", f_act), ("pe", f_pe), ("dve", f_dve)):
                progs[k].append(f)
            return lambda e: e.wait_ge(ring_free, TOTAL)

        def zero_first(e):
            for b in range(B):
                e.memset(H[:, b * (T + 1):b * (T + 1) + 1], 0.0)
            e.memset(H[:, B * (T + 1):], 0.0).then_inc(s_hz, 1)
        s_hz = sem("h_padded")

        def pe_first1(e):
            e.wait_ge(s_const, n_const)
            e.wait_ge(s_x, 64)
        h1 = layer_norm("ln1", X, True, True, (LN1W, LN1B), True, pe_first1, zero_first)

        def wait_ln1(e):
            h1(e, NCH)
            e.wait_ge(s_hz, 1)
        progs["pe"].append(wait_ln1)
        progs["dve"].append(wait_ln1)
        used[0] = 0
        tm_dve = time_mix()

        def after_tm(e):
            tm_dve.wait(e, "x1", B)
        used[0] = 0
        h2 = layer_norm("ln2", XP, False, False, (LN2W, LN2B), True, after_tm, lambda e: None)
        cm_dve = channel_mix(h2)

        def after_cm(e):
            cm_dve.wait(e, "xa1", B)
        used[0] = 0
        used[0] = 0
        h3 = layer_norm("ln3", X, False, False, None, False, after_cm, lambda e: None)
        after_f1 = experts("f1", after_cm, h3, False)
        h4 = layer_norm("ln4", X, False, True, (GAM, BET), False, after_f1, lambda e: None)
        used[0] = 0
        after_at = attention(after_f1, h4)
        h5 = layer_norm("ln5", X, False, False, None, False, after_at, lambda e: None)
        used[0] = 0
        experts("f2", after_at, h5, True)

        @block.sync
        def _(e):
            for f in progs["sp"]:
                f(e)

        @block.scalar
        def _(e):
            for f in progs["act"]:
                f(e)

        @block.gpsimd
        def _(e):
            for f in progs["pool"]:
                f(e)

        @block.tensor
        def _(e):
            for f in progs["pe"]:
                f(e)

        @block.vector
        def _(e):
            for f in progs["dve"]:
                f(e)


def bf16_bits(a):
    return (np.ascontiguousarray(a, dtype=np.float32).view(np.uint32) >> 16).astype(np.uint16)


def shape_constants():
    eye = np.eye(P, dtype=np.float32)
    mean_at = np.zeros((P, 127), np.float32)
    mean_at[:, [31, 63, 95]] = 1.0 / C
    pick = np.zeros((P, S), np.float32)
    pick_e = np.zeros((P, E), np.float32)
    for p in range(3):
        pick[p * S:(p + 1) * S] = np.eye(S)
        pick_e[p * E:(p + 1) * E] = np.eye(E)
    mask = np.zeros((P, CH), np.float32)
    mask[:, CH - P:] = np.where(np.arange(P)[None, :] > np.arange(P)[:, None], NEG, 0.0)
    k = (T - 1) // (S - 1)
    m = np.zeros((T, S), np.float32)
    for n in range(T - 1):
        m[n, n // k] += k - n % k
        m[n, min(n // k + 1, S - 1)] += n % k
    keys = np.zeros((3 * SW + 3, T), np.float32)
    for p in range(3):
        keys[p * SW:(p + 1) * SW, :T // 2] = m[:T // 2, :SW].T
        keys[p * SW:(p + 1) * SW, T // 2:] = m[T // 2:, S - SW:].T
    keys[3 * SW:] = 1.0
    return {
        "centre": eye - np.float32(1.0 / C), "mean_at": mean_at, "ident": eye, "ident16": bf16_bits(eye),
        "pick": bf16_bits(pick), "pick_e": bf16_bits(pick_e),
        "tie": np.tile((E - np.arange(E)).astype(np.float32), (P, 1)), "mask": mask,
        "mask_t": bf16_bits(mask[:, CH - P:].T),
        "grid_t": np.ascontiguousarray(m.T), "key_rows": bf16_bits(keys),
    }


def layouts(inp):
    a = {k: np.asarray(v) for k, v in inp.items()}

    def by_width(m):
        return m.reshape(HG, HG, D, -1).transpose(0, 2, 1, 3).reshape(m.shape)
    A, Bt, F = "L0_attn_a_", "L0_attn_b_", "L0_ffn_"
    t = {
        "x": a[A + "x"].reshape(N, C).T,
        "vecs": np.stack([a[A + k] for k in ("ln1_w", "ln1_b", "ln2_w", "ln2_b", "time_decay", "time_first",
                                             "tmk", "tmv", "tmr", "f_tmk", "f_tmr")]
                         + [a[Bt + k] for k in ("gamma", "beta", "bo", "bv")], axis=1),
        "bqk": np.stack([by_width(a[Bt + "bq"]), by_width(a[Bt + "bk"])], axis=1),
        "att_kvr": np.stack([a[A + "att_kw"].T, a[A + "att_vw"].T, a[A + "att_rw"].T], axis=1),
        "att_ow": a[A + "att_ow"].T,
        "f_kw": a[A + "f_kw"].T,
        "f_rw": a[A + "f_rw"].T,
        "f_vw": a[A + "f_vw"].T.reshape(FB, P, C).transpose(1, 0, 2),
        "gate": a[F + "gate"],
        "W1": a[F + "W1"].transpose(1, 0, 2),
        "b1": a[F + "b1"].reshape(E * HB, P).T,
        "W2": a[F + "W2"].reshape(E, HB, P, C).transpose(2, 0, 1, 3),
        "b2": a[F + "b2"],
        "wqkv": np.stack([by_width(a[Bt + "Wq"]).T, by_width(a[Bt + "Wk"]).T, a[Bt + "Wv"].T], axis=1),
        "wo": a[Bt + "Wo"].T,
        "rel": a[Bt + "rel_bias"].transpose(1, 0, 2),
    }
    return {k: np.ascontiguousarray(v) for k, v in t.items()}


def kernel(**inputs):
    import concourse.bacc as _bacc
    from concourse.bass_utils import run_bass_kernel_spmd as _run

    nc = _bacc.Bacc("TRN2", target_bir_lowering=False, num_devices=1)
    arrays, aps = {}, {}
    for name, v in {**layouts(inputs), **shape_constants()}.items():
        arrays[f"in_{name}"] = v
        aps[name] = nc.dram_tensor(f"in_{name}", v.shape, mybir.dt.from_np(v.dtype), kind="ExternalInput").ap()
        if v.dtype == np.uint16:
            aps[name] = aps[name].bitcast(BF16)
    out = nc.dram_tensor("out", (C, N), F32, kind="ExternalOutput").ap()
    x = aps.pop("x")
    build(nc, x, aps, out)
    r = _run(nc, [arrays], core_ids=[0])
    return np.ascontiguousarray(r.results[0]["out"].T).reshape(B, T, C)
```

```python
from contextlib import ExitStack

import numpy as np
import concourse.bass as bass
from concourse import mybir

F32 = mybir.dt.float32
BF16 = mybir.dt.bfloat16
F32R = mybir.dt.float32r
ALU = mybir.AluOpType
ACT = mybir.ActivationFunctionType
AX = mybir.AxisListType

P = 128
B, T, C = 4, 1024, 128
N = B * T
CH = 512
NCH = N // CH
NBLK = N // P
FB = 4
E, HB = 8, 2
NH, D = 16, 8
HG = 4
S = 32
SW = 17
EPS = 1e-5
NEG = -1.0e30
QK_ROWS = 6 * D
REL0 = QK_ROWS
MAX0 = REL0 + 3 * SW
ROWS = MAX0 + 3
VW = D + 1
VG = 8 * HG * VW
SCALE = D ** -0.5
GRID_SCALE = ((S - 1) / (T - 1)) ** 2

PACKS = [
    [(0, 0, 512, 0)], [(1, 128, 384, 0), (3, 384, 128, 384)], [(2, 256, 256, 0)],
    [(0, 512, 512, 0)], [(1, 512, 512, 0)], [(2, 512, 512, 0)], [(3, 512, 512, 0)],
    [(4, 512, 512, 0)], [(5, 640, 384, 0), (7, 896, 128, 384)], [(6, 768, 256, 0)],
]
HALF_END = (2, 9)
NP_ = len(PACKS)
NPB = 4

PIECES = []
for _j in range(HG):
    for _q in range(8):
        if _q >= 4:
            PIECES.append((_j, _q, 0, 512, False))
        _k0 = 512 * (_q // 4)
        PIECES.append((_j, _q, _k0, (_q + 1) * P - _k0, True))


class Steps:

    def __init__(self, sem, names):
        self.sem, self.names = sem, names

    def start(self, eng):
        eng.sem_inc(self.sem, len(self.names))

    def at(self, name, it):
        return it * len(self.names) + (self.names.index(name) + 1)

    def wait(self, eng, name, it):
        eng.wait_ge(self.sem, self.at(name, it))


def build(nc, x, w, out):
    with ExitStack() as ctx:
        def sb(name, shape, dt=F32):
            return ctx.enter_context(nc.sbuf_tensor(name, shape, dt))

        def sem(name):
            return ctx.enter_context(nc.semaphore(name))

        bank = [ctx.enter_context(nc.psum_tensor(f"bank{i}", [P, CH], F32)) for i in range(3)]
        psum_pair = [ctx.enter_context(nc.psum_tensor(f"pair{i}", [P, 2, CH], F32)) for i in range(2)]
        bank += [psum_pair[0][:, 0, :], psum_pair[0][:, 1, :], psum_pair[1][:, 0, :], psum_pair[1][:, 1, :]]
        bank.append(ctx.enter_context(nc.psum_tensor("bank7", [P, CH], F32)))
        bank = [b if i in (3, 4, 5, 6) else b[:, :] for i, b in enumerate(bank)]

        X = sb("X", [P, N])
        H = sb("H", [P, B * (T + 1) + CH + 1])
        centre = sb("centre", [P, P])
        mean_at = sb("mean_at", [P, 127])
        ident = sb("ident", [P, P])
        ident16 = sb("ident16", [P, P], BF16)
        pick = sb("pick", [P, S], BF16)
        pick_e = sb("pick_e", [P, E], BF16)
        tie = sb("tie", [P, E])
        mask = sb("mask", [P, CH])
        mask_t = sb("mask_t", [P, P], BF16)
        vecs = sb("vecs", [P, 15])
        (LN1W, LN1B, LN2W, LN2B, DECAY, FIRST, TMK, TMV, TMR, FTMK, FTMR, GAM, BET, BO, BV) = range(15)
        bqk = sb("bqk", [P, 2])
        b1 = sb("b1", [P, E * HB])
        b2rep = sb("b2rep", [P, 3, P])
        b2p = sb("b2p", [P, 3, P], BF16)
        b2t = sb("b2t", [P, 2, P])
        var = [sb(f"lnv{i}", [96, P]) for i in range(6)]
        rp = sb("rp", [96, 2, P], BF16)
        lr = sb("lr", [96, 2, P])
        ln_scratch = sb("ln_scratch", [P, 4, CH])
        with ExitStack() as room:
            HG_HI, HG_LO = (room.enter_context(nc.sbuf_tensor(name, [P, 4, HB, CH], F32R))
                            for name in ("gated_hi", "gated_lo"))
        XC = sb("XC", [P, N])
        XP = sb("XP", [P, N])
        with ExitStack() as room:
            w1_hi, w1_lo = (room.enter_context(nc.sbuf_tensor(name, [P, E, HB * P], F32R))
                            for name in ("w1_hi", "w1_lo"))
            w2_hi, w2_lo = (room.enter_context(nc.sbuf_tensor(name, [P, E, HB, P], F32R))
                            for name in ("w2_hi", "w2_lo"))
            h_hi, h_lo = (room.enter_context(nc.sbuf_tensor(name, [P, N + CH], F32R))
                          for name in ("h_hi", "h_lo"))
        OPERANDS = 4 * E * HB * P + 2 * (N + CH)
        ARENA = 30 * 1024
        arena = sb("arena", [P, ARENA])
        used = [0]

        def cut(*dims, dt=F32):
            n = int(np.prod(dims))
            words = n if dt == F32 else (n + 1) // 2
            a = arena[:, used[0]:used[0] + words]
            used[0] += words
            assert used[0] <= ARENA, used
            if dt != F32:
                a = a.bitcast(dt)
            if len(dims) == 1:
                return a
            names = "abcd"[:len(dims)]
            return a.rearrange(f"p ({' '.join(names)}) -> p {' '.join(names)}",
                               **{k: v for k, v in zip(names[1:], dims[1:])})

        block = ctx.enter_context(nc.Block())
        progs = {k: [] for k in ("pe", "dve", "act", "pool", "sp")}

        def vec(i):
            return vecs[:, i:i + 1]

        def col(t, a, n=CH):
            return t[:, bass.ds(a, n)]

        s_x = sem("x_loaded")
        s_const = sem("constants_loaded")
        consts = [(centre[:, :], w["centre"]), (mean_at[:, :], w["mean_at"]), (ident[:, :], w["ident"]),
                  (ident16[:, :], w["ident16"]), (pick[:, :], w["pick"]), (pick_e[:, :], w["pick_e"]),
                  (tie[:, :], w["tie"]), (mask[:, :], w["mask"]), (mask_t[:, :], w["mask_t"]), (vecs[:, :], w["vecs"]),
                  (bqk[:, :], w["bqk"]), (b1[:, :], w["b1"])]
        n_const = 16 * len(consts)

        waits_met = {e.engine: sem(f"waits_met_{n}") for n, e in (("dve", nc.vector), ("pool", nc.gpsimd))}

        def apart(e):
            e.sem_inc(waits_met[e.engine], 1)

        def load_sp(sp):
            for c in range(4):
                sp.dma_start(X[:, c * T:(c + 1) * T], x[:, c * T:(c + 1) * T]).then_inc(s_x, 16)

        def load_act(act):
            for dst, src in consts:
                act.dma_start(dst, src).then_inc(s_const, 16)
        s_b2 = sem("b2_loaded")
        s_b2z = sem("b2_zeroed")

        def zero_b2(pool):
            pool.memset(b2rep[:, :, :], 0.0).then_inc(s_b2z, 1)

        def load_b2(sp):
            sp.wait_ge(s_b2z, 1)
            for k in range(3):
                for part in range(3 - k):
                    sp.dma_start(b2rep[part * E:(part + 1) * E, k, :], w["b2"]).then_inc(s_b2, 16)
        progs["pool"].append(zero_b2)
        progs["sp"] += [load_sp, load_b2]
        progs["act"].append(load_act)

        def layer_norm(tag, src, keep_first, double, affine, shifted, pe_first, dve_first):
            cent = sem(f"{tag}_centred")
            copied = sem(f"{tag}_copied")
            squared = sem(f"{tag}_squared")
            summed = sem(f"{tag}_summed")
            dchain = sem(f"{tag}_dve_chain")
            rooted = sem(f"{tag}_rooted")
            scaled = sem(f"{tag}_scale_parts")
            spread = sem(f"{tag}_spread")
            normed = sem(f"{tag}_normed")
            done = sem(f"{tag}_done")
            SQ = [ln_scratch[:, i, :] for i in (0, 1)]
            TMP = [ln_scratch[:, i, :] for i in (2, 3)]
            PV = bank[2][0:96, 0:P]
            scales = 2 if keep_first else 1

            def hcol(c):
                return c * CH + (c // 2 + 1 if shifted else 0)

            def pe(e):
                pe_first(e)
                for c in range(NCH + 1):
                    if c < NCH:
                        if c >= 2:
                            e.wait_ge(copied, c - 1)
                        e.matmul(bank[c % 2], centre[:, :], src[:, c * CH:(c + 1) * CH],
                                 start=True, stop=True).then_inc(cent, 1)
                    if c >= 1:
                        e.wait_ge(squared, c)
                        for i in range(4 * (c - 1), 4 * c):
                            m = e.matmul(PV, mean_at[:, 31 - i:127 - i], SQ[(c - 1) % 2][:, (i % 4) * P:(i % 4 + 1) * P],
                                         start=(i == 0), stop=(i == NBLK - 1))
                        m.then_inc(summed, 1)
                for c in range(NCH):
                    if c == 0:
                        e.wait_ge(scaled, 1)
                    if c >= 2:
                        e.wait_ge(normed, scales * (c - 1))
                    for s in range(scales):
                        for i in range(4):
                            m = e.matmul(bank[3 + 2 * (c % 2) + s][:, i * P:(i + 1) * P],
                                         pick[0:96, 4 * c + i:4 * c + i + 1].to_broadcast([96, P]),
                                         rp[:, s, :], start=True, stop=True)
                    m.then_inc(spread, 1)

            def dve(e):
                dve_first(e)
                for c in range(NCH):
                    e.wait_ge(cent, c + 1)
                    e.tensor_copy(XC[:, c * CH:(c + 1) * CH], bank[c % 2]).then_inc(copied, 1)
                n = [0]

                def step(ins):
                    n[0] += 1
                    ins.then_inc(dchain, 1)
                    e.wait_ge(dchain, n[0])
                e.wait_ge(summed, NCH)
                ve, sd, r1, t1, r2, r12 = (v[:, :] for v in var)
                step(e.tensor_scalar(ve, PV, EPS, None, ALU.add))
                e.wait_ge(rooted, 1)
                step(e.reciprocal(r1, sd))
                if double:
                    step(e.tensor_tensor(t1, PV, r1, ALU.mult))
                    step(e.tensor_tensor(t1, t1, r1, ALU.mult))
                    step(e.tensor_scalar(t1, t1, EPS, None, ALU.add))
                    e.wait_ge(rooted, 2)
                    step(e.reciprocal(r2, sd))
                    step(e.tensor_tensor(r12, r1, r2, ALU.mult))
                parts = [r12] if double else [r1]
                if keep_first:
                    parts.append(r1)
                for s, r in enumerate(parts):
                    a, q = rp[:, s, :], lr[:, s, :]
                    step(e.tensor_copy(a, r))
                    step(e.tensor_tensor(q, r, a, ALU.subtract))
                    step(e.tensor_copy(a[32:64], q[32:64]))
                    step(e.tensor_copy(a[64:96], q[64:96]))
                    step(e.tensor_tensor(q[64:96], q[64:96], a[64:96], ALU.subtract))
                    last = e.tensor_copy(a[64:96], q[64:96])
                    if s == len(parts) - 1:
                        last.then_inc(scaled, 1)
                for c in range(NCH):
                    e.wait_ge(spread, c + 1)
                    xc = XC[:, c * CH:(c + 1) * CH]
                    hc = H[:, hcol(c):hcol(c) + CH]
                    if affine:
                        if c >= 2:
                            e.wait_ge(done, c - 1)
                        hc = TMP[c % 2]
                    ins = e.tensor_tensor(hc, xc, bank[3 + 2 * (c % 2)], ALU.mult)
                    ins.then_inc(normed, 1)
                    if keep_first:
                        e.tensor_tensor(XP[:, c * CH:(c + 1) * CH], xc, bank[4 + 2 * (c % 2)],
                                        ALU.mult).then_inc(normed, 1)

            def act(e):
                for c in range(NCH):
                    e.wait_ge(copied, c + 1)
                    if c >= 2:
                        e.wait_ge(summed, c - 1)
                    e.activation(SQ[c % 2], XC[:, c * CH:(c + 1) * CH], ACT.Square).then_inc(squared, 1)
                e.wait_ge(dchain, 1)
                e.activation(var[1][:, :], var[0][:, :], ACT.Sqrt).then_inc(rooted, 1)
                if double:
                    e.wait_ge(dchain, 5)
                    e.activation(var[1][:, :], var[3][:, :], ACT.Sqrt).then_inc(rooted, 1)
                if affine:
                    for c in range(NCH):
                        e.wait_ge(normed, scales * c + 1)
                        e.activation(H[:, hcol(c):hcol(c) + CH], TMP[c % 2], ACT.Identity,
                                     scale=vec(affine[0]), bias=vec(affine[1])).then_inc(done, 1)
            progs["pe"].append(pe)
            progs["dve"].append(dve)
            progs["act"].append(act)
            if affine:
                return lambda e, c: e.wait_ge(done, c)
            return lambda e, c: e.wait_ge(normed, scales * c)

        def time_mix():
            wts = cut(3, P)
            wo = cut(P)
            wm = cut(3, 2, P)
            mix1 = cut(3)
            negw = cut(1)
            spare = cut(1)
            PP, AA, BB = cut(T + 1), cut(T + 1), cut(T + 1)
            EA, EX = [cut(4, CH), cut(4, CH)], [cut(4, CH), cut(4, CH)]
            EV, NV, SR = [[cut(CH), cut(CH)] for _ in range(3)]
            G1, G3, PM = [[cut(CH), cut(CH)] for _ in range(3)]
            NUM, DN, RW = G1, G3, PM
            load = sem("tm_weights")
            ready = sem("tm_prepared")
            kvr = sem("tm_kvr_done")
            owd = sem("tm_out_done")
            dve = Steps(sem("tm_dve"), [
                "pp0", "pp1", "a0", "b0", "m0", "a1", "b1", "m1", "d0", "d1",
                "ev0", "ev1", "aa0", "bb0", "nv0", "aa1", "bb1", "nv1",
                "rec0", "num0", "ns0", "rec1", "rw0", "num1", "ns1", "rw1"])
            act = Steps(sem("tm_act"), ["sg0", "sg1", "table", "ex0", "ex1"])
            pool = Steps(sem("tm_pool"), ["c0", "c1", "h0", "den0", "g0", "h1", "den1", "g1"])
            tm_added = sem("tm_added")

            def f_sp(e):
                e.dma_start(wts, w["att_kvr"]).then_inc(load, 16)
                e.dma_start(wo, w["att_ow"]).then_inc(load, 16)

            def f_pool(e):
                pool.start(e)
                with e.Fori(1, B + 1) as it:
                    for c in range(2):
                        dve.wait(e, f"m{c}", it)
                        act.wait(e, f"ex{c}", it - 1)
                        e.tensor_tensor(EA[c][:, 2, :], PP[:, c * CH:(c + 1) * CH], PM[c],
                                        ALU.subtract).then_inc(pool.sem, 1)
                    for c in range(2):
                        act.wait(e, f"ex{c}", it)
                        dve.wait(e, f"bb{c}", it)
                        e.tensor_tensor(G3[c], EX[c][:, 2, :], BB[:, c * CH:(c + 1) * CH],
                                        ALU.mult).then_inc(pool.sem, 1)
                        pool.wait(e, f"h{c}", it)
                        e.tensor_tensor(G3[c], G3[c], EX[c][:, 3, :], ALU.add).then_inc(pool.sem, 1)
                        e.tensor_tensor(G1[c], EX[c][:, 2, :], AA[:, c * CH:(c + 1) * CH],
                                        ALU.mult).then_inc(pool.sem, 1)

            def f_act(e):
                e.wait_ge(s_const, n_const)
                e.activation(negw, vec(DECAY), ACT.Exp).then_inc(ready, 1)
                act.start(e)
                with e.Fori(1, B + 1) as it:
                    for c in range(2):
                        e.wait_ge(kvr, it * 2 + (c - 1))
                        dve.wait(e, f"ns{c}", it - 1)
                        e.activation(SR[c], bank[3 * c + 2], ACT.Sigmoid).then_inc(act.sem, 1)
                    act.wait(e, "table", it - 1)
                    e.activation(spare, vec(DECAY), ACT.Exp, scale=0.0).then_inc(act.sem, 1)
                    for c in range(2):
                        dve.wait(e, f"d{c}", it)
                        pool.wait(e, f"c{c}", it)
                        dve.wait(e, f"nv{c}", it - 1)
                        pool.wait(e, f"g{c}", it - 1)
                        e.activation(EX[c], EA[c], ACT.Exp).then_inc(act.sem, 1)

            def f_pe(e):
                e.wait_ge(ready, 3)

                def kvr_of(c, first):
                    for m in range(3):
                        for half in range(2):
                            last = e.matmul(bank[3 * c + m], wm[:, m, half, :], col(H, first - half),
                                            start=(half == 0), stop=(half == 1))
                    last.then_inc(kvr, 1)
                kvr_of(0, 1)
                kvr_of(1, 1 + CH)

                def body(it, last):
                    if not last:
                        nxt = it * (T + 1) + 1
                        dve.wait(e, "nv0", it)
                        act.wait(e, "sg0", it)
                        kvr_of(0, nxt)
                        dve.wait(e, "nv1", it)
                        act.wait(e, "sg1", it)
                        kvr_of(1, nxt + CH)
                    for c in range(2):
                        dve.wait(e, f"rw{c}", it)
                        e.matmul(bank[6 + c], wo, PM[c], start=True, stop=True).then_inc(owd, 1)
                with e.Fori(1, B) as it:
                    body(it, False)
                body(B, True)

            def f_dve(e):
                e.wait_ge(load, 32)
                e.wait_ge(s_const, n_const)
                e.memset(PP[:, 0:1], -1e38)
                e.memset(AA[:, 0:1], 0.0)
                e.memset(BB[:, 0:1], 0.0)
                e.tensor_scalar(mix1, vecs[:, TMK:TMR + 1], -1.0, 1.0, ALU.mult, ALU.add).then_inc(ready, 1)
                e.wait_ge(ready, 2)
                for m in range(3):
                    e.tensor_scalar(wm[:, m, 0, :], wts[:, m, :], vecs[:, TMK + m:TMK + m + 1], None, ALU.mult)
                    last = e.tensor_scalar(wm[:, m, 1, :], wts[:, m, :], mix1[:, m:m + 1], None, ALU.mult)
                last.then_inc(ready, 1)
                e.tensor_scalar(negw, negw, -1.0, None, ALU.mult).then_inc(ready, 1)
                e.wait_ge(ready, 4)
                dve.start(e)
                u = vec(FIRST)

                def inc(ins):
                    ins.then_inc(dve.sem, 1)

                def add(c, it):
                    e.wait_ge(owd, it * 2 + (c - 1))
                    xp = col(XP, it * T - T + c * CH)
                    e.tensor_tensor(xp, bank[6 + c], xp, ALU.add).then_inc(tm_added, 1)

                def body(it, first):
                    def w_(name):
                        dve.wait(e, name, it)
                    lo = [slice(c * CH, (c + 1) * CH) for c in range(2)]
                    hi = [slice(c * CH + 1, (c + 1) * CH + 1) for c in range(2)]
                    for c in range(2):
                        e.wait_ge(kvr, it * 2 + (c - 1))
                        if c:
                            w_("pp0")
                        inc(e.tensor_tensor_scan(PP[:, hi[c]], negw.to_broadcast([P, CH]), bank[3 * c],
                                                 PP[:, c * CH:c * CH + 1], ALU.add, ALU.max))
                    if not first:
                        add(0, it - 1)
                        add(1, it - 1)
                    for c in range(2):
                        w_(f"pp{c}")
                        inc(e.scalar_tensor_tensor(out=EA[c][:, 0, :], in0=PP[:, lo[c]], scalar=negw,
                                                   in1=PP[:, hi[c]], op0=ALU.add, op1=ALU.subtract))
                        inc(e.tensor_tensor(EA[c][:, 1, :], bank[3 * c], PP[:, hi[c]], ALU.subtract))
                        inc(e.scalar_tensor_tensor(out=PM[c], in0=bank[3 * c], scalar=u, in1=PP[:, lo[c]],
                                                   op0=ALU.add, op1=ALU.max))
                    for c in range(2):
                        w_(f"m{c}")
                        inc(e.scalar_tensor_tensor(out=EA[c][:, 3, :], in0=bank[3 * c], scalar=u, in1=PM[c],
                                                   op0=ALU.add, op1=ALU.subtract))
                    for c in range(2):
                        act.wait(e, f"ex{c}", it)
                        inc(e.tensor_tensor(EV[c], EX[c][:, 1, :], bank[3 * c + 1], ALU.mult))
                    for c in range(2):
                        w_("ev1" if c == 0 else "aa0")
                        inc(e.tensor_tensor_scan(AA[:, hi[c]], EX[c][:, 0, :], EV[c],
                                                 AA[:, c * CH:c * CH + 1], ALU.mult, ALU.add))
                        if c:
                            w_("bb0")
                        inc(e.tensor_tensor_scan(BB[:, hi[c]], EX[c][:, 0, :], EX[c][:, 1, :],
                                                 BB[:, c * CH:c * CH + 1], ALU.mult, ALU.add))
                        inc(e.tensor_tensor(NV[c], EX[c][:, 3, :], bank[3 * c + 1], ALU.mult))

                    def num(c):
                        pool.wait(e, f"g{c}", it)
                        w_(f"nv{c}")
                        inc(e.tensor_tensor(NUM[c], NV[c], G1[c], ALU.add))

                    def rec(c):
                        pool.wait(e, f"den{c}", it)
                        inc(e.reciprocal(DN[c], DN[c]))

                    def ns(c):
                        w_(f"num{c}")
                        inc(e.tensor_tensor(NUM[c], NUM[c], SR[c], ALU.mult))

                    def rw(c):
                        w_(f"ns{c}")
                        inc(e.tensor_tensor(RW[c], NUM[c], DN[c], ALU.mult))
                    rec(0)
                    num(0)
                    ns(0)
                    rec(1)
                    rw(0)
                    num(1)
                    ns(1)
                    rw(1)
                body(1, True)
                with e.Fori(2, B + 1) as it:
                    body(it, False)
                add(0, B)
                add(1, B)
            for k, f in (("sp", f_sp), ("pool", f_pool), ("act", f_act), ("pe", f_pe), ("dve", f_dve)):
                progs[k].append(f)

            def finished(e):
                e.wait_ge(tm_added, 2 * B)
            return finished

        def channel_mix(wait_h):
            wk, wr, wv = cut(FB * P), cut(P), cut(FB, P)
            mix1 = cut(2)
            TK, TR, XK, XR = [[cut(CH), cut(CH)] for _ in range(4)]
            R = [cut(FB, CH), cut(FB, CH)]
            Q = [cut(FB, CH), cut(FB, CH)]
            SR = [cut(CH), cut(CH)]
            KV = [cut(CH), cut(CH)]
            XS = [cut(CH), cut(CH)]
            load = sem("cm_weights")
            ready = sem("cm_prepared")
            hidden = sem("cm_hidden_done")
            out_d = sem("cm_out_done")
            dve = Steps(sem("cm_dve"), ["tk0", "tr0", "xk0", "xr0", "tk1", "tr1", "xk1", "xr1",
                                        "sq0", "sq1", "kv0", "xa0", "kv1", "xa1"])
            act = Steps(sem("cm_act"), ["ra0", "rb0", "sg0", "ra1", "rb1", "sg1"])
            pool = Steps(sem("cm_pool"), ["xs0", "xs1", "sq0", "sq1"])

            def f_sp(e):
                tm_done(e)
                for dst, src in ((wk, w["f_kw"]), (wr, w["f_rw"]), (wv, w["f_vw"])):
                    e.dma_start(dst, src).then_inc(load, 16)

            def f_pe(e):
                e.wait_ge(load, 48)
                with e.Fori(1, B + 1) as it:
                    for c in range(2):
                        dve.wait(e, f"xr{c}", it)
                        for m in range(FB):
                            if m % 2 == 0:
                                act.wait(e, ("ra", "rb")[m // 2] + str(1 - c), it - 1 if c == 0 else it)
                            last = e.matmul(psum_pair[m // 2][:, m % 2, :], wk[:, m * P:(m + 1) * P], XK[c],
                                            start=True, stop=True)
                            if m % 2:
                                last.then_inc(hidden, 1)
                        act.wait(e, f"sg{c}", it - 1)
                        e.matmul(bank[c], wr, XR[c], start=True, stop=True).then_inc(hidden, 1)
                    for c in range(2):
                        dve.wait(e, f"sq{c}", it)
                        pool.wait(e, f"sq{c}", it)
                        dve.wait(e, f"kv{c}", it - 1)
                        for m in range(FB):
                            last = e.matmul(bank[(2, 7)[c]], wv[:, m, :], Q[c][:, m, :],
                                            start=(m == 0), stop=(m == FB - 1))
                        last.then_inc(out_d, 1)

            def f_act(e):
                act.start(e)
                with e.Fori(1, B + 1) as it:
                    for c in range(2):
                        for k in range(2):
                            e.wait_ge(hidden, it * 6 + (3 * c + k - 5))
                            dve.wait(e, f"sq{c}", it - 1)
                            pool.wait(e, f"sq{c}", it - 1)
                            e.activation(R[c][:, 2 * k:2 * k + 2, :], psum_pair[k][:, :, :],
                                         ACT.Relu).then_inc(act.sem, 1)
                        e.wait_ge(hidden, it * 6 + (3 * c - 3))
                        dve.wait(e, f"kv{c}", it - 1)
                        e.activation(SR[c], bank[c], ACT.Sigmoid).then_inc(act.sem, 1)

            def f_pool(e):
                tm_done(e)
                pool.start(e)
                with e.Fori(1, B + 1) as it:
                    for c in range(2):
                        at = it * T + (c * CH - T)
                        dve.wait(e, f"xa{c}", it - 1)
                        e.tensor_tensor(XS[c], col(X, at), col(XP, at), ALU.add).then_inc(pool.sem, 1)
                    for c in range(2):
                        act.wait(e, f"rb{c}", it)
                        e.tensor_tensor(Q[c][:, 2:4, :], R[c][:, 2:4, :], R[c][:, 2:4, :],
                                        ALU.mult).then_inc(pool.sem, 1)

            def f_dve(e):
                wait_h(e, NCH)
                e.tensor_scalar(mix1, vecs[:, FTMK:FTMR + 1], -1.0, 1.0, ALU.mult, ALU.add).then_inc(ready, 1)
                e.wait_ge(ready, 1)
                dve.start(e)

                def inc(ins):
                    ins.then_inc(dve.sem, 1)
                with e.Fori(1, B + 1) as it:
                    for c in range(2):
                        at = it * (T + 1) + (c * CH - T)
                        e.wait_ge(hidden, it * 6 + (3 * c - 6))
                        inc(e.tensor_scalar(TK[c], col(H, at - 1), mix1[:, 0:1], None, ALU.mult))
                        inc(e.tensor_scalar(TR[c], col(H, at - 1), mix1[:, 1:2], None, ALU.mult))
                        dve.wait(e, f"tk{c}", it)
                        inc(e.scalar_tensor_tensor(out=XK[c], in0=col(H, at), scalar=vec(FTMK), in1=TK[c],
                                                   op0=ALU.mult, op1=ALU.add))
                        dve.wait(e, f"tr{c}", it)
                        inc(e.scalar_tensor_tensor(out=XR[c], in0=col(H, at), scalar=vec(FTMR), in1=TR[c],
                                                   op0=ALU.mult, op1=ALU.add))
                    for c in range(2):
                        act.wait(e, f"ra{c}", it)
                        inc(e.tensor_tensor(Q[c][:, 0:2, :], R[c][:, 0:2, :], R[c][:, 0:2, :], ALU.mult))
                    for c in range(2):
                        at = it * T + (c * CH - T)
                        e.wait_ge(out_d, it * 2 + (c - 1))
                        act.wait(e, f"sg{c}", it)
                        inc(e.tensor_tensor(KV[c], bank[(2, 7)[c]], SR[c], ALU.mult))
                        dve.wait(e, f"kv{c}", it)
                        pool.wait(e, f"xs{c}", it)
                        inc(e.tensor_tensor(col(X, at), KV[c], XS[c], ALU.add))
            for k, f in (("sp", f_sp), ("pool", f_pool), ("act", f_act), ("pe", f_pe), ("dve", f_dve)):
                progs[k].append(f)
            return dve

        def experts(tag, before, wait_h, last_stage):
            used[0] = OPERANDS
            w1, w2 = cut(E, HB * P), cut(E, HB, P)
            gw = cut(E)
            GT = cut(N + CH, dt=BF16)
            HGT = [cut(HB, CH), cut(HB, CH)]
            r0 = used[0]
            R = [cut(HB, CH), cut(HB, CH)]
            G3 = arena[:, r0:r0 + NBLK * P // 2].bitcast(BF16).rearrange("p (b n) -> p b n", b=NBLK)
            LP, PA, KA, O1, O2 = (cut(NBLK, E) for _ in range(5))
            m1, m2, m3 = cut(NBLK), cut(NBLK), cut(NBLK)
            load = sem(f"{tag}_weights")
            zero = sem(f"{tag}_zeroed")
            logit = sem(f"{tag}_logits")
            chain = sem(f"{tag}_gate_chain")
            expd = sem(f"{tag}_gate_exp")
            turned = sem(f"{tag}_gates_turned")
            turned_s = sem(f"{tag}_gates_in_sbuf")
            z_done = sem(f"{tag}_hidden_done")
            relu_d = sem(f"{tag}_relu_done")
            gated = sem(f"{tag}_gated")
            y_done = sem(f"{tag}_expert_out_done")
            added = sem(f"{tag}_added")
            AHEAD, Y_AHEAD = 2, 4
            LEAD = 3
            hi_done = sem(f"{tag}_hidden_hi")
            lo_done = sem(f"{tag}_hidden_lo")
            w_hi = sem(f"{tag}_weights_hi")
            w_split = sem(f"{tag}_weights_split")
            hi_in = sem(f"{tag}_input_hi")
            in_split = sem(f"{tag}_input_split")

            def f_sp(e):
                before(e)
                for dst, src in ((gw, w["gate"]), (w1, w["W1"]), (w2, w["W2"])):
                    e.dma_start(dst, src).then_inc(load, 16)
                if last_stage:
                    stored = sem("stored")
                    with e.Fori(1, NCH + 1) as it:
                        e.wait_ge(added, it + AHEAD)
                        e.dma_start(out[:, bass.ds(it * CH - CH, CH)], col(X, it * CH - CH)).then_inc(stored, 16)
                    e.wait_ge(stored, 16 * NCH)

            def f_pool(e):
                before(e)
                e.memset(GT[:, N:N + CH], 0.0)
                e.memset(G3, 0.0).then_inc(zero, 1)
                e.memset(h_hi[:, N:N + CH].bitcast(F32), 0.0)
                e.memset(h_lo[:, N:N + CH].bitcast(F32), 0.0).then_inc(zero, 1)
                e.wait_ge(w_hi, 1)
                e.tensor_tensor(w1_lo[:], w1, w1_hi[:].bitcast(F32), ALU.subtract).then_inc(w_split, 1)
                for c in range(NCH):
                    r = slice(c * CH, (c + 1) * CH)
                    e.wait_ge(hi_in, c + 1)
                    e.tensor_tensor(h_lo[:, r], H[:, r], h_hi[:, r].bitcast(F32), ALU.subtract).then_inc(in_split, 1)
                e.wait_ge(w_hi, 2)
                e.tensor_tensor(w2_lo[:], w2, w2_hi[:].bitcast(F32), ALU.subtract).then_inc(w_split, 1)

            n_load = 48
            lg = bank[0][:, 0:NBLK * E].rearrange("p (b e) -> p b e", e=E)
            turn = [bank[1].bitcast(BF16), bank[2].bitcast(BF16)]

            def f_pe(e):
                e.wait_ge(load, n_load)
                for c in range(NCH):
                    wait_h(e, c + 1)
                    for i in range(4 * c, 4 * c + 4):
                        m = e.matmul(lg[:, i, :], H[:, i * P:(i + 1) * P], gw, start=True, stop=True)
                m.then_inc(logit, 1)
                e.wait_ge(chain, N_GATE)
                for q in range(NCH):
                    if q >= 2:
                        e.wait_ge(turned_s, q - 1)
                    for i in range(4):
                        m = e.transpose(turn[q % 2][:, i * P:(i + 1) * P], G3[:, 4 * q + i, :], ident16[:, :])
                    m.then_inc(turned, 1)

                def z(s, at, ex):
                    e.matmul(bank[1 + s], pick_e[:, ex:ex + 1].to_broadcast([P, P]), col(GT, at),
                             start=True, stop=True)
                    for k in range(HB):
                        ks = slice(k * P, (k + 1) * P)
                        e.matmul(psum_pair[s][:, k, :], w1_hi[:, ex, ks], col(h_hi, at), start=True, stop=False)
                        e.matmul(psum_pair[s][:, k, :], w1_hi[:, ex, ks], col(h_lo, at), start=False, stop=False)
                        m = e.matmul(psum_pair[s][:, k, :], w1_lo[:, ex, ks], col(h_hi, at), start=False, stop=True)
                    m.then_inc(z_done, 1)
                e.wait_ge(turned_s, NCH)
                e.wait_ge(w_split, 2)
                e.wait_ge(zero, 2)
                for ex in range(LEAD):
                    if ex >= 2:
                        e.wait_ge(relu_d, ex - 1 + AHEAD)
                        e.wait_ge(gated, ex - 1 + AHEAD)
                    z(ex % 2, 0, ex)
                with e.Fori(1, NCH // 2 + 1) as it:
                    for cc in range(2):
                        yb = bank[(0, 7)[cc]]
                        at = it * 2 * CH + (cc - 2) * CH
                        for ex in range(E):
                            s = it * 2 * E + ((cc - 2) * E + ex)
                            e.wait_ge(relu_d, s + (LEAD - 1) + AHEAD)
                            e.wait_ge(gated, s + (LEAD - 1) + AHEAD)
                            if ex + LEAD < E:
                                z((ex + LEAD) % 2, at, ex + LEAD)
                            else:
                                z((ex + LEAD) % 2, at + CH, ex + LEAD - E)
                            if ex == 0:
                                e.wait_ge(added, it * 2 + (cc - 2) + AHEAD - 1)
                                for k in range(3):
                                    e.matmul(yb, b2p[:, k, :], col(GT, at), start=(k == 0), stop=False)
                            e.wait_ge(hi_done, s + 1 + AHEAD)
                            e.wait_ge(lo_done, s + 1 + AHEAD)
                            for k in range(HB):
                                hi, lo = HG_HI[:, ex % 4, k, :], HG_LO[:, ex % 4, k, :]
                                e.matmul(yb, w2_hi[:, ex, k, :], hi, start=False, stop=False)
                                e.matmul(yb, w2_hi[:, ex, k, :], lo, start=False, stop=False)
                                m = e.matmul(yb, w2_lo[:, ex, k, :], hi, start=False,
                                             stop=(ex == E - 1 and k == HB - 1))
                            m.then_inc(y_done, 1)

            def f_act(e):
                e.wait_ge(load, n_load)
                for hi, w_ in ((w1_hi, w1), (w2_hi, w2)):
                    e.activation(hi[:], w_, ACT.Copy).then_inc(w_hi, 1)
                for c in range(NCH):
                    wait_h(e, c + 1)
                    r = slice(c * CH, (c + 1) * CH)
                    e.activation(h_hi[:, r], H[:, r], ACT.Copy).then_inc(hi_in, 1)
                e.wait_ge(chain, 2)
                e.activation(PA, LP, ACT.Exp).then_inc(expd, 1)
                e.sem_inc(relu_d, AHEAD)
                e.wait_ge(chain, N_GATE)

                def relu(s, ex):
                    e.wait_ge(z_done, s + 1)
                    e.wait_ge(gated, s - 1 + AHEAD)
                    for k in range(HB):
                        ins = e.activation(R[ex % 2][:, k, :], psum_pair[ex % 2][:, k, :], ACT.Relu,
                                           bias=b1[:, ex * HB + k:ex * HB + k + 1])
                    ins.then_inc(relu_d, 1)
                relu(0, 0)
                with e.Fori(1, NCH // 2 + 1) as it:
                    for cc in range(2):
                        for ex in range(E):
                            s = it * 2 * E + ((cc - 2) * E + ex)
                            relu(s + 1, (ex + 1) % E)
                            e.wait_ge(gated, s + 1 + AHEAD)
                            e.wait_ge(y_done, s - 3 + Y_AHEAD)
                            e.activation(HG_HI[:, ex % 4], HGT[ex % 2], ACT.Copy).then_inc(hi_done, 1)

            N_GATE = 2 + 16 + 5

            def f_dve(e):
                n = [0]

                def step(ins, dep=True):
                    n[0] += 1
                    ins.then_inc(chain, 1)
                    if dep:
                        e.wait_ge(chain, n[0])
                e.wait_ge(load, n_load)
                if tag == "f1":
                    e.wait_ge(s_b2, 96)
                    b2c = sem("b2_chain")
                    cnt = [0]

                    def st(ins):
                        cnt[0] += 1
                        ins.then_inc(b2c, 1)
                        e.wait_ge(b2c, cnt[0])
                    st(e.tensor_copy(b2p[:, :, :], b2rep[:, :, :]))
                    st(e.tensor_tensor(b2t[:, :, :], b2rep[:, 1:3, :], b2p[:, 1:3, :], ALU.subtract))
                    st(e.tensor_copy(b2p[:, 1:3, :], b2t[:, :, :]))
                    st(e.tensor_tensor(b2t[:, 1, :], b2t[:, 1, :], b2p[:, 2, :], ALU.subtract))
                    st(e.tensor_copy(b2p[:, 2, :], b2t[:, 1, :]))

                def over(t):
                    return t.unsqueeze(2).to_broadcast([P, NBLK, E])
                tie_b = tie[:, :].unsqueeze(1).to_broadcast([P, NBLK, E])
                e.wait_ge(logit, 1)
                step(e.tensor_reduce(m1, lg, AX.X, ALU.max))
                step(e.tensor_tensor(LP, lg, over(m1), ALU.subtract))
                e.wait_ge(expd, 1)
                step(e.tensor_reduce(m1, PA, AX.X, ALU.max))
                step(e.tensor_tensor(KA, PA, over(m1), ALU.is_ge))
                step(e.tensor_tensor(KA, KA, tie_b, ALU.mult))
                step(e.tensor_reduce(m2, KA, AX.X, ALU.max))
                step(e.tensor_tensor(O1, KA, over(m2), ALU.is_equal))
                step(e.scalar_tensor_tensor(out=LP, in0=O1, scalar=-2.0, in1=PA, op0=ALU.mult, op1=ALU.add))
                step(e.tensor_reduce(m1, LP, AX.X, ALU.max))
                step(e.tensor_tensor(KA, LP, over(m1), ALU.is_ge))
                step(e.tensor_tensor(KA, KA, tie_b, ALU.mult))
                step(e.tensor_reduce(m2, KA, AX.X, ALU.max))
                step(e.tensor_tensor(O2, KA, over(m2), ALU.is_equal))
                step(e.tensor_tensor(O1, O1, O2, ALU.add))
                step(e.tensor_tensor(PA, PA, O1, ALU.mult))
                step(e.tensor_reduce(m3, PA, AX.X, ALU.add))
                step(e.reciprocal(m1, m3))
                step(e.tensor_tensor(PA, PA, over(m1), ALU.mult))
                e.wait_ge(zero, 1)
                step(e.tensor_copy(G3[:, :, 0:E], PA))
                step(e.tensor_tensor(KA, PA, G3[:, :, 0:E], ALU.subtract))
                step(e.tensor_copy(G3[:, :, E:2 * E], KA))
                step(e.tensor_tensor(LP, KA, G3[:, :, E:2 * E], ALU.subtract))
                step(e.tensor_copy(G3[:, :, 2 * E:3 * E], LP))
                assert n[0] == N_GATE
                for q in range(NCH):
                    e.wait_ge(turned, q + 1)
                    e.tensor_copy(GT[:, q * CH:(q + 1) * CH], turn[q % 2][:, 0:CH]).then_inc(turned_s, 1)
                e.sem_inc(gated, AHEAD)
                e.sem_inc(added, AHEAD)
                e.sem_inc(lo_done, AHEAD)

                def gate(s, ex):
                    e.wait_ge(relu_d, s + 1 + AHEAD)
                    e.wait_ge(hi_done, s - 1 + AHEAD)
                    e.wait_ge(lo_done, s - 1 + AHEAD)
                    e.tensor_tensor(HGT[ex % 2], R[ex % 2],
                                    bank[1 + ex % 2].unsqueeze(1).to_broadcast([P, HB, CH]),
                                    ALU.mult).then_inc(gated, 1)

                def add(chunk, cc):
                    e.wait_ge(y_done, (chunk + 1) * E + Y_AHEAD)
                    xc = col(X, chunk * CH)
                    e.tensor_tensor(xc, bank[(0, 7)[cc]], xc, ALU.add).then_inc(added, 1)

                def body(it, first):
                    for cc in range(2):
                        for ex in range(E):
                            s = it * 2 * E + ((cc - 2) * E + ex)
                            gate(s + 1, (ex + 1) % E)
                            e.wait_ge(gated, s + 1 + AHEAD)
                            e.wait_ge(hi_done, s + 1 + AHEAD)
                            e.tensor_tensor(HG_LO[:, ex % 4], HGT[ex % 2], HG_HI[:, ex % 4].bitcast(F32),
                                            ALU.subtract).then_inc(lo_done, 1)
                            if ex == LEAD and not (first and cc == 0):
                                add(it * 2 + (cc - 3), 1 - cc)
                gate(0, 0)
                body(1, True)
                with e.Fori(2, NCH // 2 + 1) as it:
                    body(it, False)
                add(NCH - 1, 1)

            def f_pool2(e):
                e.sem_inc(y_done, Y_AHEAD)
                e.sem_inc(hi_done, AHEAD)
            for k, f in (("sp", f_sp), ("pool", f_pool), ("pool", f_pool2), ("act", f_act), ("pe", f_pe),
                         ("dve", f_dve)):
                progs[k].append(f)
            return lambda e: e.wait_ge(added, NCH + AHEAD)

        scr_q = nc.dram_tensor("scratch_q_parts", (B, 3, 2, P, CH), BF16, kind="Internal").ap()
        scr_k = nc.dram_tensor("scratch_k_parts", (B, 3, P, T), BF16, kind="Internal").ap()
        scr_v = nc.dram_tensor("scratch_values", (B, HG, P, VG), F32, kind="Internal").ap()
        scr_rel = nc.dram_tensor("scratch_bias_parts", (HG, 3, HG, S, T), BF16, kind="Internal").ap()
        scr_max = nc.dram_tensor("scratch_max_parts", (HG, 3, HG * 8, P), BF16, kind="Internal").ap()

        def attention(before, wait_h):
            QL = cut(HG, 2, HG, CH, dt=BF16)
            QU = cut(HG, HG, CH, dt=BF16)
            KK = cut(HG, HG, T, dt=BF16)
            VS = cut(HG, VG + 32)
            wqkv, wo = cut(3, P), cut(P)
            grid, rel = cut(T), cut(NH * S)
            bqs = cut(1)
            VA = cut(HG, 8, HG * VW)
            dump = [cut(CH, dt=BF16), cut(CH, dt=BF16)]
            NM = [cut(2, HG, 4), cut(2, HG, 4)]
            PF = [cut(HG, 4), cut(HG, 4)]
            NF, NR = cut(P), cut(P)
            N3 = [cut(3, P, dt=BF16), cut(3, P, dt=BF16)]
            RC = [cut(4, HG), cut(4, HG)]
            QF, KF, QR, KR = (XC[:, i * T:(i + 1) * T] for i in range(4))
            half_ = 3 * T // 2
            Q3, K3 = ([m.bitcast(BF16).rearrange("p (a n) -> p a n", a=3) for m in (XP[:, at:at + half_], cut(half_))]
                      for at in (0, half_))
            VT = [XP[:, 2 * half_ + i * CH:2 * half_ + (i + 1) * CH] for i in range(2)]
            PR = [b_[:, i * 4 * CH:(i + 1) * 4 * CH].rearrange("p (j n) -> p j n", j=HG)
                  for b_ in (XC, XP) for i in range(2)]

            ATT = H[:, 0:T].rearrange("p (k c) -> p k c", k=8)
            ATTT = H[:, T:2 * T]
            OS = [H[:, 2 * T + i * CH:2 * T + (i + 1) * CH] for i in range(2)]

            load = sem("at_weights")
            const_rows = sem("at_key_rows")
            prep = sem("at_prepared")
            rel_mm = sem("at_rel_product")
            rel_ch = sem("at_rel_chain")
            rel_out = sem("at_rel_copied")
            rel_st = [sem(f"at_rel{i}_stored") for i in range(2)]
            rel_ld = sem("at_rel_loaded")
            pe_s = Steps(sem("at_pe"), ["q0", "k0", "v0", "q1", "k1", "v1", "t0", "t1"])
            act_s = Steps(sem("at_act"), ["q0", "k0", "v0", "q1", "k1", "v1", "va0", "va1"])
            dve_s = Steps(sem("at_dve"), ["q1", "k1", "qr", "kr", "q2", "k2", "q3", "k3"])
            stored = [sem(f"at_parts{i}_stored") for i in range(2)]
            v_stored = sem("at_values_stored")
            slot_ld = [sem(f"at_slot{i}_loaded") for i in range(HG)]
            SLOT = 16 * 13
            ring_ready = sem("at_ring_ready")
            ring_free = sem("at_ring_free")
            pm_ready = sem("at_maxima_ready")
            nm_chain = sem("at_max_chain")
            nm_ready = sem("at_max_parts_ready")
            nm_stored = sem("at_max_parts_stored")
            nm_loaded = [sem(f"at_slot{i}_max_rows_loaded") for i in range(HG)]
            sc_ready = sem("at_scores_ready")
            exp_done = sem("at_exp_done")
            pv_done = sem("at_pv_done")
            os_done = sem("at_out_copied")
            rc_done = sem("at_recip_done")
            RING = 3
            PRO = 2 * (len(PIECES) + 1)
            IPB = HG * (len(PIECES) + 3) + 4

            def step(hg, with_max, before_=None):
                ev, left = [], list(PIECES) if with_max else []
                for i in range(NP_):
                    for half in range(2):
                        t = 2 * i + half
                        ev.append(("scores", t, hg, 0))
                        if before_:
                            ev += ending(t, *before_)
                        for _ in range((3, 2)[half]):
                            if left:
                                ev.append(("piece", left.pop(0), hg, 0))
                    if i >= 1:
                        ev.append(("pv", i - 1, hg, 0))
                    if i == HALF_END[0] + 2:
                        ev.append(("turn_out", 0, hg, 0))
                return ev + [("piece", p, hg, 0) for p in left]

            def ending(t, hg, b, with_max=True):
                ev = []
                if t == 1:
                    ev.append(("pv", NP_ - 1, hg, b))
                if t == 2 and with_max:
                    ev.append(("maxima", None, hg, b))
                if t == 3:
                    ev.append(("turn_out", 1, hg, b))
                if hg == HG - 1 and t in (5, 7):
                    ev.append(("turn_att", int(t == 7), hg, b))
                if hg == HG - 1 and t in (8, 9):
                    ev.append(("out", t - 8, hg, b))
                return ev
            HEAD_T = 10

            def batch(last):
                first = step(0, True, (HG - 1, -1))
                cut_at = first.index(("scores", HEAD_T, 0, 0))
                rest = first[cut_at:]
                for hg in range(1, HG):
                    rest += step(hg, not last or hg < 2, (hg - 1, 0))
                    if last and hg == HG - 1:
                        rest = [v for v in rest if v[0] != "maxima" or v[2] < 2]
                return first[:cut_at], rest

            RINGED = ("piece", "turn_out", "maxima", "turn_att", "out")

            def numbered(events, n=0):
                res = []
                for v in events:
                    res.append((*v, n))
                    n += v[0] in RINGED
                return res, n
            HEAD = [v for v in batch(False)[0] if v[3] == 0]
            HEAD_ITEMS = numbered(HEAD)[1]
            HEAD = numbered(HEAD, -HEAD_ITEMS)[0]
            BODY, n_body = numbered(batch(False)[1] + [(k, a_, g_, b_ + 1) for k, a_, g_, b_ in batch(False)[0]])
            LAST, LAST_ITEMS = numbered(batch(True)[1] +
                                        [v for t in range(HEAD_T) for v in ending(t, HG - 1, 0, False)])
            assert n_body == IPB
            TOTAL = PRO + HEAD_ITEMS + (B - 1) * IPB + LAST_ITEMS

            def item_no(it, local):
                return it * IPB + (PRO + HEAD_ITEMS - IPB + local)

            def item_of(events, kind, arg):
                for k, a_, g_, _, n in events:
                    if (k, a_, g_) == (kind, arg, HG - 1):
                        return n

            def over_batches(eng, head, body):
                head()
                with eng.Fori(1, B) as it:
                    body(it, False)
                body(B, True)

            def load_slot(e, b, hg):
                bs = bass.ds(b, 1)
                rows = slice(hg * 32, (hg + 1) * 32)

                def move(dst, src):
                    e.dma_start(dst, src).then_inc(slot_ld[hg], 16)
                for part, row, reps in ((0, 0, 3), (1, 3 * D, 2), (2, 5 * D, 1)):
                    dst = slice(row, row + reps * D)
                    for half in range(2):
                        src = scr_q[bs, part, half, rows, :].rearrange("o (d j) n -> o d (j n)", j=HG)
                        if reps > 1:
                            src = src.to_broadcast([reps, D, HG * CH])
                        else:
                            src = src.rearrange("o d n -> (o d) n")
                        move(QL[dst, hg, half, :, :].rearrange("p j n -> p (j n)"), src)
                        if half:
                            move(QU[dst, hg, :, :].rearrange("p j n -> p (j n)"), src)
                    src = scr_k[bs, 0:reps, rows, :].rearrange("o t (d j) n -> (o t) d (j n)", j=HG)
                    move(KK[dst, hg, :, :].rearrange("p j n -> p (j n)"), src)
                e.dma_start(VS[:, hg, 0:VG], scr_v[bs, hg, :, :].rearrange("o p n -> (o p) n"))\
                    .then_inc(slot_ld[hg], 16)

            def send_maxima(e, n, slot, par):
                e.wait_ge(nm_ready, n + 1)
                e.dma_start(scr_max[slot].rearrange("t r i -> r t i"), N3[par][0:32]).then_inc(nm_stored, 16)
                e.wait_ge(nm_stored, n * 16 + 16)
                rows = scr_max[slot].rearrange("t r i -> t (r i)")
                e.dma_start(QL[MAX0:ROWS, slot].rearrange("p a j n -> p (a j n)"), rows).then_inc(nm_loaded[slot], 16)
                e.dma_start(QU[MAX0:ROWS, slot].rearrange("p j n -> p (j n)"), rows[:, HG * CH:])\
                    .then_inc(nm_loaded[slot], 16)

            def all_stored(e):
                e.wait_ge(stored[0], 16 * B)
                e.wait_ge(stored[1], 16 * B)
                e.wait_ge(v_stored, 16 * B)

            def f_sp(e):
                before(e)
                for dst, src in ((wqkv, w["wqkv"]), (wo, w["wo"]), (grid[0:S], w["grid_t"]),
                                 (rel[0:S], w["rel"].rearrange("i h j -> i (h j)"))):
                    e.dma_start(dst, src).then_inc(load, 16)
                for s in range(HG):
                    e.dma_start(KK[REL0:ROWS, s, :, :], w["key_rows"].unsqueeze(1).to_broadcast([3 * SW + 3, HG, T]))\
                        .then_inc(const_rows, 16)

                def store_grid(hg):
                    e.wait_ge(rel_ch, 4 * hg + 4)
                    e.dma_start(scr_rel[hg].rearrange("t j s n -> (j s) t n"), (Q3, K3)[hg % 2][0])\
                        .then_inc(rel_st[hg % 2], 16)

                def load_grid(hg):
                    e.wait_ge(rel_st[hg % 2], 16 * (hg // 2) + 16)
                    for p in range(3):
                        rows = slice(REL0 + p * SW, REL0 + (p + 1) * SW)
                        for half in range(2):
                            e.dma_start(QL[rows, hg, half, :, :], scr_rel[hg, p, :, 0:SW, half * CH:(half + 1) * CH]
                                        .rearrange("j s n -> s j n")).then_inc(rel_ld, 16)
                        e.dma_start(QU[rows, hg, :, :], scr_rel[hg, p, :, S - SW:S, CH:T]
                                    .rearrange("j s n -> s j n")).then_inc(rel_ld, 16)

                def store_parts(b):
                    dve_s.wait(e, "q3", b + 1)
                    e.dma_start(scr_q[b].rearrange("t a p n -> p (t a) n"),
                                Q3[b % 2].rearrange("p t (a n) -> p (t a) n", a=2)).then_inc(stored[b % 2], 16)
                    dve_s.wait(e, "k3", b + 1)
                    e.dma_start(scr_k[b].rearrange("t p n -> p t n"), K3[b % 2]).then_inc(stored[b % 2], 16)
                    act_s.wait(e, "va1", b + 1)
                    e.dma_start(scr_v[b].rearrange("g p n -> p g n"),
                                VA.rearrange("p g k n -> p g (k n)")).then_inc(v_stored, 16)
                for hg in range(HG):
                    store_grid(hg)
                    if hg:
                        load_grid(hg - 1)
                load_grid(HG - 1)
                store_parts(0)
                store_parts(1)
                for st in (stored[0], stored[1], v_stored):
                    e.wait_ge(st, 32)
                load_slot(e, 0, 0)
                load_slot(e, 0, 1)
                store_parts(2)
                store_parts(3)
                all_stored(e)
                load_slot(e, 0, 2)
                load_slot(e, 0, 3)
                for n in range(2):
                    send_maxima(e, n, n, n % 2)

                def body(it, last):
                    for hg in range(HG):
                        if not last or hg < 2:
                            send_maxima(e, it * HG + (hg - 2), (hg + 2) % HG, hg % 2)
                        if not last:
                            e.wait_ge(pv_done, it * 40 + (10 * hg + 10 + NPB - 40))
                            load_slot(e, it, hg)
                over_batches(e, lambda: None, body)

            def f_pool(e):
                before(e)
                e.memset(VS[:, :, VG:VG + 32], 0.0)
                e.memset(VA.rearrange("p g k n -> p (g k n)")[:, D::VW], 1.0).then_inc(prep, 1)

                def split_maxima(n, par, after):
                    e.wait_ge(ring_free, after)
                    if not isinstance(n, int) or n >= 2:
                        e.wait_ge(nm_stored, n * 16 - 16)
                    apart(e)
                    e.tensor_scalar(N3[par][0:32, 0, :], NF[0:32], 1.0, None, ALU.mult).then_inc(nm_chain, 1)
                    e.wait_ge(nm_chain, n * 3 + 1)
                    e.tensor_tensor(NR[0:32], NF[0:32], N3[par][0:32, 0, :], ALU.subtract).then_inc(nm_chain, 1)
                    e.wait_ge(nm_chain, n * 3 + 2)
                    apart(e)
                    e.tensor_scalar(N3[par][0:32, 1, :], NR[0:32], 1.0, None, ALU.mult).then_inc(nm_chain, 1)
                    e.wait_ge(nm_chain, n * 3 + 3)
                    e.tensor_tensor(N3[par][0:32, 2, :], NR[0:32], N3[par][0:32, 1, :], ALU.subtract)\
                        .then_inc(nm_ready, 1)
                for g in range(2):
                    split_maxima(g, g, (g + 1) * (len(PIECES) + 1))

                def body(it, last):
                    for kind, _, hg, db, local in LAST if last else BODY:
                        if kind == "maxima":
                            split_maxima((it + db) * HG + (hg - 2), hg % 2, item_no(it, local) + 1)
                over_batches(e, lambda: None, body)

            def f_act(e):
                before(e)
                e.wait_ge(s_const, n_const)
                e.activation(bqs, bqk[:, 0:1], ACT.Copy, scale=SCALE).then_inc(prep, 1)
                e.wait_ge(prep, 2)

                def copy_grid(hg):
                    e.wait_ge(rel_mm, hg + 1)
                    if hg >= 2:
                        e.wait_ge(rel_ch, 4 * hg - 6)
                    for c in range(2):
                        ins = e.activation((QF, KF)[hg % 2][:, c * CH:(c + 1) * CH], bank[(0, 1, 2, 7)[c + 2 * (hg % 2)]], ACT.Copy,
                                           scale=GRID_SCALE)
                    ins.then_inc(rel_out, 1)

                for hg in range(HG):
                    copy_grid(hg)
                act_s.start(e)
                with e.Fori(1, B + 1) as it:
                    for c in range(2):
                        r = slice(c * CH, (c + 1) * CH)
                        pe_s.wait(e, f"q{c}", it)
                        dve_s.wait(e, "qr", it - 1)
                        e.activation(QF[:, r], bank[c], ACT.Identity, bias=bqs, scale=SCALE).then_inc(act_s.sem, 1)
                        pe_s.wait(e, f"k{c}", it)
                        dve_s.wait(e, "kr", it - 1)
                        e.activation(KF[:, r], bank[(2, 7)[c]], ACT.Identity, bias=bqk[:, 1:2])\
                            .then_inc(act_s.sem, 1)
                        pe_s.wait(e, f"v{c}", it)
                        pe_s.wait(e, f"t{c}", it - 1)
                        e.activation(VT[c], bank[3 + c], ACT.Identity, bias=vec(BV)).then_inc(act_s.sem, 1)
                    for c in range(2):
                        pe_s.wait(e, f"t{c}", it)
                        e.wait_ge(v_stored, it * 16 - 16)
                        for i in range(4):
                            src = bank[5 + c][:, i * P:(i + 1) * P].rearrange("p (g j d) -> p g j d", g=HG, j=HG)
                            dst = VA[:, :, 4 * c + i, :].rearrange("p g (j w) -> p g j w", w=VW)[:, :, :, 0:D]
                            ins = e.activation(dst, src, ACT.Copy)
                        ins.then_inc(act_s.sem, 1)
                all_stored(e)
                e.sem_inc(exp_done, 2)
                e.sem_inc(os_done, 1)

                def turned(it, hg, half, last=False):
                    for kind, arg, g, db, n in LAST if last and hg else BODY:
                        if (kind, arg, g) == ("turn_out", half, hg):
                            return item_no(it, n) + 1 - db * IPB

                def copy_out(it, hg, half, last=False):
                    e.wait_ge(pv_done, it * 40 + (10 * hg + HALF_END[half] + 1 + NPB - 40))
                    e.wait_ge(ring_ready, turned(it, hg - 1, half, last and hg > 1) if hg else turned(it, HG - 1, half) - IPB)
                    e.activation(OS[half], bank[7], ACT.Copy).then_inc(os_done, 1)

                def exps(it, hg, ts, with_copy=True, last=False):
                    for t in ts:
                        i, h = t // 2, t % 2
                        wid = max(p[3] + p[2] for p in PACKS[i])
                        e.wait_ge(sc_ready, it * 80 + (20 * hg + t + 1 - 80))
                        e.wait_ge(pv_done, it * 40 + (10 * hg + i + 1 - 40))
                        e.activation(PR[(10 * hg + i) % NPB][:, 2 * h:2 * h + 2, 0:wid],
                                     psum_pair[t % 2][:, :, 0:wid], ACT.Exp).then_inc(exp_done, 1)
                        if t == 2 * HALF_END[0] + 3:
                            copy_out(it, hg, 0, last)
                        if t == 1 and with_copy:
                            if hg:
                                copy_out(it, hg - 1, 1, last)
                            else:
                                copy_out(it - 1, HG - 1, 1)

                def body(it, last):
                    exps(it, 0, range(HEAD_T, 2 * NP_), last=last)
                    for hg in range(1, HG):
                        exps(it, hg, range(2 * NP_), last=last)
                    if last:
                        copy_out(it, HG - 1, 1, last)
                    else:
                        exps(it + 1, 0, range(HEAD_T))
                over_batches(e, lambda: exps(1, 0, range(HEAD_T), False), body)

            def f_pe(e):
                before(e)
                e.wait_ge(load, 64)
                for hg in range(HG):
                    for c in range(2):
                        if hg >= 2:
                            e.wait_ge(rel_out, hg - 1)
                        m = e.matmul(bank[(0, 1, 2, 7)[c + 2 * (hg % 2)]], rel[0:S, hg * P:(hg + 1) * P], grid[0:S, c * CH:(c + 1) * CH],
                                     start=True, stop=True)
                    m.then_inc(rel_mm, 1)
                e.wait_ge(rel_out, HG)
                wait_h(e, NCH)
                pe_s.start(e)
                with e.Fori(1, B + 1) as it:
                    for c in range(2):
                        for k, bk in enumerate((bank[c], bank[(2, 7)[c]], bank[3 + c])):
                            act_s.wait(e, f"{'qkv'[k]}{c}", it - 1)
                            e.matmul(bk, wqkv[:, k, :], col(H, it * T + (c * CH - T)),
                                     start=True, stop=True).then_inc(pe_s.sem, 1)
                    for c in range(2):
                        act_s.wait(e, f"v{c}", it)
                        act_s.wait(e, f"va{c}", it - 1)
                        for i in range(4):
                            m = e.transpose(bank[5 + c][:, i * P:(i + 1) * P], VT[c][:, i * P:(i + 1) * P],
                                            ident[:, :])
                        m.then_inc(pe_s.sem, 1)
                act_s.wait(e, "va1", B)
                e.wait_ge(const_rows, 16 * HG)
                e.wait_ge(rel_ld, 16 * 9 * HG)

                def piece(slot, p, bk):
                    j, qb, k0, n, _ = p
                    q = slice(qb % 4 * P, qb % 4 * P + P)
                    lhs = QL[0:MAX0, slot, qb // 4, j, q] if k0 == 0 else QU[0:MAX0, slot, j, q]
                    return e.matmul(bk[:, 0:n], lhs, KK[0:MAX0, slot, j, k0:k0 + n], start=True, stop=True)

                def maxima(n, par, bk):
                    e.wait_ge(pm_ready, n + 1)
                    return e.transpose(bk[0:32, 0:P], NM[par].rearrange("p a j q -> p (a j q)"), ident[:, :])
                no = 0
                for g in range(2):
                    e.wait_ge(slot_ld[g], SLOT)
                    for p in PIECES:
                        if no >= RING:
                            e.wait_ge(ring_free, no - RING + 1)
                        piece(g, p, bank[no % RING]).then_inc(ring_ready, 1)
                        no += 1
                    e.wait_ge(ring_free, no - RING + 1)
                    maxima(g, g % 2, bank[no % RING]).then_inc(ring_ready, 1)
                    no += 1
                assert no == PRO
                e.sem_inc(pv_done, NPB)

                def run(events, it0):
                    first_item = min(v[4] for v in events)
                    for kind, arg, hg, db, local in events:
                        it = it0 + db
                        slot2 = (hg + 2) % HG
                        if kind == "scores" and arg == 0:
                            e.wait_ge(nm_loaded[hg], it * 32)
                            e.wait_ge(slot_ld[hg], it * SLOT)
                        if kind == "piece" and arg == PIECES[0]:
                            e.wait_ge(slot_ld[slot2], it * SLOT + (SLOT if hg >= 2 else 0))
                        if kind in RINGED:
                            bk = bank[local % RING]
                            e.wait_ge(ring_free, item_no(it0, max(local - RING + 1, first_item)))
                        if kind == "piece":
                            piece(slot2, arg, bk).then_inc(ring_ready, 1)
                        elif kind == "maxima":
                            maxima(it * HG + (hg - 2), hg % 2, bk).then_inc(ring_ready, 1)
                        elif kind == "scores":
                            e.wait_ge(exp_done, it * 80 + (20 * hg + arg - 1 + 2 - 80))
                            for kb, n0, n, c0 in PACKS[arg // 2]:
                                diagonal = kb * P == n0
                                for jj in range(2):
                                    j = 2 * (arg % 2) + jj
                                    q = slice(n0 % CH, n0 % CH + n)
                                    rhs = QL[0:ROWS, hg, n0 // CH, j, q] if kb < 4 else QU[0:ROWS, hg, j, q]
                                    m = e.matmul(psum_pair[arg % 2][:, jj, c0:c0 + n],
                                                 KK[0:ROWS, hg, j, kb * P:(kb + 1) * P], rhs,
                                                 start=True, stop=True)
                                    if diagonal:
                                        m = e.matmul(psum_pair[arg % 2][:, jj, c0:c0 + P], ident16[:, :],
                                                     mask_t[:, :], start=False, stop=True,
                                                     skip_group_check=True)
                            m.then_inc(sc_ready, 1)
                        elif kind == "pv":
                            e.wait_ge(exp_done, it * 80 + (20 * hg + 2 * arg + 2 + 2 - 80))
                            first = arg in (0, HALF_END[0] + 1)
                            if first:
                                half = int(arg > 0)
                                e.wait_ge(os_done, it * (2 * HG) + (2 * hg + half + 1 - 2 * HG))
                            for kb, n0, n, c0 in PACKS[arg]:
                                q0 = n0 % CH
                                for j in range(HG):
                                    v0 = (kb * HG + j) * VW
                                    m = e.matmul(bank[7][32 * j:32 * j + 32, q0:q0 + n], VS[:, hg, v0:v0 + 32],
                                                 PR[(10 * hg + arg) % NPB][:, j, c0:c0 + n],
                                                 start=first, stop=arg in HALF_END,
                                                 skip_group_check=True)
                            m.then_inc(pv_done, 1)
                        elif kind == "turn_out":
                            e.wait_ge(os_done, it * (2 * HG) + (2 * hg + arg + 2 - 2 * HG))
                            for i in range(4):
                                m = e.transpose(bk[:, i * P:(i + 1) * P], OS[arg][:, i * P:(i + 1) * P],
                                                ident[:, :])
                            m.then_inc(ring_ready, 1)
                        elif kind == "turn_att":
                            e.wait_ge(ring_free, item_no(it0, item_of(events, "turn_out", 1) + 1))
                            for i in range(4):
                                m = e.transpose(bk[:, i * P:(i + 1) * P], ATT[:, 4 * arg + i, :], ident[:, :])
                            m.then_inc(ring_ready, 1)
                        elif kind == "out":
                            e.wait_ge(ring_free, item_no(it0, item_of(events, "turn_att", arg) + 1))
                            e.matmul(bk, wo, ATTT[:, arg * CH:(arg + 1) * CH], start=True, stop=True)\
                                .then_inc(ring_ready, 1)
                over_batches(e, lambda: run(HEAD, 1), lambda it, last: run(LAST if last else BODY, it))

            def f_dve(e):
                for hg in range(HG):
                    full, rest_, parts = ((QF, QR, Q3), (KF, KR, K3))[hg % 2]
                    parts = parts[0]
                    e.wait_ge(rel_out, hg + 1)
                    if hg >= 2:
                        e.wait_ge(rel_st[hg % 2], 16)
                    e.tensor_copy(parts[:, 0, :], full).then_inc(rel_ch, 1)
                    e.wait_ge(rel_ch, 4 * hg + 1)
                    e.tensor_tensor(rest_, full, parts[:, 0, :], ALU.subtract).then_inc(rel_ch, 1)
                    e.wait_ge(rel_ch, 4 * hg + 2)
                    e.tensor_copy(parts[:, 1, :], rest_).then_inc(rel_ch, 1)
                    e.wait_ge(rel_ch, 4 * hg + 3)
                    e.tensor_tensor(parts[:, 2, :], rest_, parts[:, 1, :], ALU.subtract).then_inc(rel_ch, 1)
                dve_s.start(e)
                for st in rel_st:
                    e.wait_ge(st, 16 * HG // 2)
                with e.Fori(1, B // 2 + 1) as it2:
                    for bb in range(2):
                        it = it2 * 2 + (bb - 1)
                        act_s.wait(e, "q1", it)
                        e.wait_ge(stored[bb], it2 * 32 - 32)
                        e.tensor_copy(Q3[bb][:, 0, :], QF).then_inc(dve_s.sem, 1)
                        act_s.wait(e, "k1", it)
                        e.tensor_copy(K3[bb][:, 0, :], KF).then_inc(dve_s.sem, 1)
                        dve_s.wait(e, "q1", it)
                        e.tensor_tensor(QR, QF, Q3[bb][:, 0, :], ALU.subtract).then_inc(dve_s.sem, 1)
                        dve_s.wait(e, "k1", it)
                        e.tensor_tensor(KR, KF, K3[bb][:, 0, :], ALU.subtract).then_inc(dve_s.sem, 1)
                        dve_s.wait(e, "qr", it)
                        e.tensor_copy(Q3[bb][:, 1, :], QR).then_inc(dve_s.sem, 1)
                        dve_s.wait(e, "kr", it)
                        e.tensor_copy(K3[bb][:, 1, :], KR).then_inc(dve_s.sem, 1)
                        dve_s.wait(e, "q2", it)
                        e.tensor_tensor(Q3[bb][:, 2, :], QR, Q3[bb][:, 1, :], ALU.subtract).then_inc(dve_s.sem, 1)
                        dve_s.wait(e, "k2", it)
                        e.tensor_tensor(K3[bb][:, 2, :], KR, K3[bb][:, 1, :], ALU.subtract).then_inc(dve_s.sem, 1)

                def piece(p, par, bk, no):
                    j, qb, k0, n, diag = p
                    if not diag:
                        e.tensor_reduce(PF[par][:, j, qb - 4:qb - 3], bk[:, 0:n], AX.X, ALU.max).then_inc(ring_free, 1)
                        return
                    apart(e)
                    e.tensor_tensor_reduce(dump[no % 2][:, 0:n], bk[:, 0:n], mask[:, CH - n:CH], 1.0, 1e8 * NEG,
                                           ALU.add, ALU.max, NM[par][:, qb // 4, j, qb % 4:qb % 4 + 1]).then_inc(ring_free, 1)

                def combine(par, after):
                    e.wait_ge(ring_free, after)
                    e.tensor_tensor(NM[par][:, 1], NM[par][:, 1], PF[par], ALU.max).then_inc(pm_ready, 1)

                def maxima(n, bk):
                    if not isinstance(n, int) or n >= 1:
                        e.wait_ge(nm_ready, n)
                    e.tensor_scalar(NF[0:32], bk[0:32, 0:P], -1.0, None, ALU.mult).then_inc(ring_free, 1)
                no = 0
                for g in range(2):
                    for i, p in enumerate(PIECES):
                        e.wait_ge(ring_ready, no + 1)
                        if no >= 2:
                            e.wait_ge(ring_free, no - 1)
                        piece(p, g % 2, bank[no % RING], no)
                        no += 1
                    combine(g % 2, no)
                    e.wait_ge(ring_ready, no + 1)
                    maxima(g, bank[no % RING])
                    no += 1

                def run(events, it0):
                    for kind, arg, hg, db, local in events:
                        if kind not in RINGED:
                            continue
                        it = it0 + db
                        bk = bank[local % RING]
                        e.wait_ge(ring_ready, item_no(it0, local) + 1)
                        e.wait_ge(ring_free, item_no(it0, local) - 1)
                        if kind == "piece":
                            piece(arg, hg % 2, bk, local)
                            if arg == PIECES[-1]:
                                combine(hg % 2, item_no(it0, local) + 1)
                        elif kind == "maxima":
                            maxima(it * HG + (hg - 2), bk)
                        elif kind == "turn_out":
                            v = bk.rearrange("p (k j w) -> p k j w", k=4, j=HG)
                            e.reciprocal(RC[arg], v[:, :, :, D:VW].rearrange("p k j w -> p k (j w)")).then_inc(rc_done, 1)
                            e.wait_ge(rc_done, it * (2 * HG) + (2 * hg + arg + 1 - 2 * HG))
                            o = ATT[:, 4 * arg:4 * arg + 4, hg * 32:(hg + 1) * 32]
                            e.tensor_tensor(o.rearrange("p k (j d) -> p k j d", j=HG), v[:, :, :, 0:D],
                                            RC[arg].unsqueeze(3).to_broadcast([P, 4, HG, D]), ALU.mult)\
                                .then_inc(ring_free, 1)
                        elif kind == "turn_att":
                            e.tensor_copy(ATTT[:, arg * CH:(arg + 1) * CH], bk).then_inc(ring_free, 1)
                        elif kind == "out":
                            xc = col(X, it * T + (arg * CH - T))
                            e.scalar_tensor_tensor(out=xc, in0=bk, scalar=vec(BO), in1=xc, op0=ALU.add,
                                                   op1=ALU.add).then_inc(ring_free, 1)
                over_batches(e, lambda: run(HEAD, 1), lambda it, last: run(LAST if last else BODY, it))

            for k, f in (("sp", f_sp), ("pool", f_pool), ("act", f_act), ("pe", f_pe), ("dve", f_dve)):
                progs[k].append(f)
            return lambda e: e.wait_ge(ring_free, TOTAL)

        def zero_first(e):
            for b in range(B):
                e.memset(H[:, b * (T + 1):b * (T + 1) + 1], 0.0)
            e.memset(H[:, B * (T + 1):], 0.0).then_inc(s_hz, 1)
        s_hz = sem("h_padded")

        def pe_first1(e):
            e.wait_ge(s_const, n_const)
            e.wait_ge(s_x, 64)
        h1 = layer_norm("ln1", X, True, True, (LN1W, LN1B), True, pe_first1, zero_first)

        def wait_ln1(e):
            h1(e, NCH)
            e.wait_ge(s_hz, 1)
        progs["pe"].append(wait_ln1)
        progs["dve"].append(wait_ln1)
        used[0] = 0
        tm_done = time_mix()

        def after_tm(e):
            tm_done(e)
        used[0] = 0
        h2 = layer_norm("ln2", XP, False, False, (LN2W, LN2B), True, after_tm, lambda e: None)
        cm_dve = channel_mix(h2)

        def after_cm(e):
            cm_dve.wait(e, "xa1", B)
        used[0] = 0
        used[0] = 0
        h3 = layer_norm("ln3", X, False, False, None, False, after_cm, lambda e: None)
        after_f1 = experts("f1", after_cm, h3, False)
        h4 = layer_norm("ln4", X, False, True, (GAM, BET), False, after_f1, lambda e: None)
        used[0] = 0
        after_at = attention(after_f1, h4)
        h5 = layer_norm("ln5", X, False, False, None, False, after_at, lambda e: None)
        used[0] = 0
        experts("f2", after_at, h5, True)

        @block.sync
        def _(e):
            for f in progs["sp"]:
                f(e)

        @block.scalar
        def _(e):
            for f in progs["act"]:
                f(e)

        @block.gpsimd
        def _(e):
            for f in progs["pool"]:
                f(e)

        @block.tensor
        def _(e):
            for f in progs["pe"]:
                f(e)

        @block.vector
        def _(e):
            for f in progs["dve"]:
                f(e)


def bf16_bits(a):
    return (np.ascontiguousarray(a, dtype=np.float32).view(np.uint32) >> 16).astype(np.uint16)


def shape_constants():
    eye = np.eye(P, dtype=np.float32)
    mean_at = np.zeros((P, 127), np.float32)
    mean_at[:, [31, 63, 95]] = 1.0 / C
    pick = np.zeros((P, S), np.float32)
    pick_e = np.zeros((P, E), np.float32)
    for p in range(3):
        pick[p * S:(p + 1) * S] = np.eye(S)
        pick_e[p * E:(p + 1) * E] = np.eye(E)
    mask = np.zeros((P, CH), np.float32)
    mask[:, CH - P:] = np.where(np.arange(P)[None, :] > np.arange(P)[:, None], NEG, 0.0)
    k = (T - 1) // (S - 1)
    m = np.zeros((T, S), np.float32)
    for n in range(T - 1):
        m[n, n // k] += k - n % k
        m[n, min(n // k + 1, S - 1)] += n % k
    keys = np.zeros((3 * SW + 3, T), np.float32)
    for p in range(3):
        keys[p * SW:(p + 1) * SW, :T // 2] = m[:T // 2, :SW].T
        keys[p * SW:(p + 1) * SW, T // 2:] = m[T // 2:, S - SW:].T
    keys[3 * SW:] = 1.0
    return {
        "centre": eye - np.float32(1.0 / C), "mean_at": mean_at, "ident": eye, "ident16": bf16_bits(eye),
        "pick": bf16_bits(pick), "pick_e": bf16_bits(pick_e),
        "tie": np.tile((E - np.arange(E)).astype(np.float32), (P, 1)), "mask": mask,
        "mask_t": bf16_bits(mask[:, CH - P:].T),
        "grid_t": np.ascontiguousarray(m.T), "key_rows": bf16_bits(keys),
    }


def layouts(inp):
    a = {k: np.asarray(v) for k, v in inp.items()}

    def by_width(m):
        return m.reshape(HG, HG, D, -1).transpose(0, 2, 1, 3).reshape(m.shape)
    A, Bt, F = "L0_attn_a_", "L0_attn_b_", "L0_ffn_"
    t = {
        "x": a[A + "x"].reshape(N, C).T,
        "vecs": np.stack([a[A + k] for k in ("ln1_w", "ln1_b", "ln2_w", "ln2_b", "time_decay", "time_first",
                                             "tmk", "tmv", "tmr", "f_tmk", "f_tmr")]
                         + [a[Bt + k] for k in ("gamma", "beta", "bo", "bv")], axis=1),
        "bqk": np.stack([by_width(a[Bt + "bq"]), by_width(a[Bt + "bk"])], axis=1),
        "att_kvr": np.stack([a[A + "att_kw"].T, a[A + "att_vw"].T, a[A + "att_rw"].T], axis=1),
        "att_ow": a[A + "att_ow"].T,
        "f_kw": a[A + "f_kw"].T,
        "f_rw": a[A + "f_rw"].T,
        "f_vw": a[A + "f_vw"].T.reshape(FB, P, C).transpose(1, 0, 2),
        "gate": a[F + "gate"],
        "W1": a[F + "W1"].transpose(1, 0, 2),
        "b1": a[F + "b1"].reshape(E * HB, P).T,
        "W2": a[F + "W2"].reshape(E, HB, P, C).transpose(2, 0, 1, 3),
        "b2": a[F + "b2"],
        "wqkv": np.stack([by_width(a[Bt + "Wq"]).T, by_width(a[Bt + "Wk"]).T, a[Bt + "Wv"].T], axis=1),
        "wo": a[Bt + "Wo"].T,
        "rel": a[Bt + "rel_bias"].transpose(1, 0, 2),
    }
    return {k: np.ascontiguousarray(v) for k, v in t.items()}


def kernel(**inputs):
    import concourse.bacc as _bacc
    from concourse.bass_utils import run_bass_kernel_spmd as _run

    nc = _bacc.Bacc("TRN2", target_bir_lowering=False, num_devices=1)
    arrays, aps = {}, {}
    for name, v in {**layouts(inputs), **shape_constants()}.items():
        arrays[f"in_{name}"] = v
        aps[name] = nc.dram_tensor(f"in_{name}", v.shape, mybir.dt.from_np(v.dtype), kind="ExternalInput").ap()
        if v.dtype == np.uint16:
            aps[name] = aps[name].bitcast(BF16)
    out = nc.dram_tensor("out", (C, N), F32, kind="ExternalOutput").ap()
    x = aps.pop("x")
    build(nc, x, aps, out)
    r = _run(nc, [arrays], core_ids=[0])
    return np.ascontiguousarray(r.results[0]["out"].T).reshape(B, T, C)
```

```python
from contextlib import ExitStack

import numpy as np
import concourse.bass as bass
from concourse import mybir

F32 = mybir.dt.float32
BF16 = mybir.dt.bfloat16
F32R = mybir.dt.float32r
ALU = mybir.AluOpType
ACT = mybir.ActivationFunctionType
AX = mybir.AxisListType

P = 128
B, T, C = 4, 1024, 128
N = B * T
CH = 512
NCH = N // CH
NBLK = N // P
FB = 4
E, HB = 8, 2
NH, D = 16, 8
HG = 4
S = 32
SW = 17
EPS = 1e-5
NEG = -1.0e30
QK_ROWS = 6 * D
REL0 = QK_ROWS
MAX0 = REL0 + 3 * SW
ROWS = MAX0 + 3
VW = D + 1
VG = 8 * HG * VW
SCALE = D ** -0.5
GRID_SCALE = ((S - 1) / (T - 1)) ** 2

PACKS = [
    [(0, 0, 512, 0)], [(1, 128, 384, 0), (3, 384, 128, 384)], [(2, 256, 256, 0)],
    [(0, 512, 512, 0)], [(1, 512, 512, 0)], [(2, 512, 512, 0)], [(3, 512, 512, 0)],
    [(4, 512, 512, 0)], [(5, 640, 384, 0), (7, 896, 128, 384)], [(6, 768, 256, 0)],
]
HALF_END = (2, 9)
NP_ = len(PACKS)
NPB = 4

ITEMS = []
for _j in range(HG):
    for _q in range(4):
        ITEMS.append([(_j, _q + 4, 0, CH, False, 0)])
        if _q < 3:
            ITEMS.append([(_j, _q, 0, (_q + 1) * P, True, 0), (_j, 6 - _q, CH, (3 - _q) * P, True, (_q + 1) * P)])
    ITEMS += [[(_j, _q, 512 * (_q // 4), CH, True, 0)] for _q in (3, 7)]


class Steps:

    def __init__(self, sem, names):
        self.sem, self.names = sem, names

    def start(self, eng):
        eng.sem_inc(self.sem, len(self.names))

    def at(self, name, it):
        return it * len(self.names) + (self.names.index(name) + 1)

    def wait(self, eng, name, it):
        eng.wait_ge(self.sem, self.at(name, it))


def build(nc, x, w, out):
    with ExitStack() as ctx:
        def sb(name, shape, dt=F32):
            return ctx.enter_context(nc.sbuf_tensor(name, shape, dt))

        def sem(name):
            return ctx.enter_context(nc.semaphore(name))

        bank = [ctx.enter_context(nc.psum_tensor(f"bank{i}", [P, CH], F32)) for i in range(3)]
        psum_pair = [ctx.enter_context(nc.psum_tensor(f"pair{i}", [P, 2, CH], F32)) for i in range(2)]
        bank += [psum_pair[0][:, 0, :], psum_pair[0][:, 1, :], psum_pair[1][:, 0, :], psum_pair[1][:, 1, :]]
        bank.append(ctx.enter_context(nc.psum_tensor("bank7", [P, CH], F32)))
        bank = [b if i in (3, 4, 5, 6) else b[:, :] for i, b in enumerate(bank)]

        X = sb("X", [P, N])
        H = sb("H", [P, B * (T + 1) + CH + 1])
        centre = sb("centre", [P, P])
        mean_at = sb("mean_at", [P, 31 + NCH])
        parts_at = sb("parts_at", [P, 2])
        ident = sb("ident", [P, P])
        ident16 = sb("ident16", [P, P], BF16)
        pick = sb("pick", [P, NBLK], BF16)
        pick_e = sb("pick_e", [P, E], BF16)
        tie = sb("tie", [P, E])
        mask = sb("mask", [P, CH])
        mask_t = sb("mask_t", [P, P], BF16)
        vecs = sb("vecs", [P, 15])
        (LN1W, LN1B, LN2W, LN2B, DECAY, FIRST, TMK, TMV, TMR, FTMK, FTMR, GAM, BET, BO, BV) = range(15)
        bqk = sb("bqk", [P, 2])
        b1 = sb("b1", [P, E * HB])
        b2_at = sb("b2_at", [P, 2])
        b2rep = sb("b2rep", [P, P])
        b2p = sb("b2p", [P, P], BF16)
        b2t = sb("b2t", [P, P])
        var = [sb(f"lnv{i}", [P, P]) for i in range(6)]
        rp = sb("rp", [P, 2, P], BF16)
        lr = sb("lr", [P, 2, P])
        ln_scratch = sb("ln_scratch", [P, 4, CH])
        with ExitStack() as room:
            HG_HI, HG_LO = (room.enter_context(nc.sbuf_tensor(name, [P, 4, HB, CH], F32R))
                            for name in ("gated_hi", "gated_lo"))
        XC = sb("XC", [P, N])
        XP = sb("XP", [P, N])
        with ExitStack() as room:
            w1_hi, w1_lo = (room.enter_context(nc.sbuf_tensor(name, [P, E, HB * P], F32R))
                            for name in ("w1_hi", "w1_lo"))
            w2_hi, w2_lo = (room.enter_context(nc.sbuf_tensor(name, [P, E, HB, P], F32R))
                            for name in ("w2_hi", "w2_lo"))
            h_hi, h_lo = (room.enter_context(nc.sbuf_tensor(name, [P, N + CH], F32R))
                          for name in ("h_hi", "h_lo"))
        OPERANDS = 4 * E * HB * P + 2 * (N + CH)
        ARENA = 30 * 1024
        arena = sb("arena", [P, ARENA])
        used = [0]

        def cut(*dims, dt=F32):
            n = int(np.prod(dims))
            words = n if dt == F32 else (n + 1) // 2
            a = arena[:, used[0]:used[0] + words]
            used[0] += words
            assert used[0] <= ARENA, used
            if dt != F32:
                a = a.bitcast(dt)
            if len(dims) == 1:
                return a
            names = "abcd"[:len(dims)]
            return a.rearrange(f"p ({' '.join(names)}) -> p {' '.join(names)}",
                               **{k: v for k, v in zip(names[1:], dims[1:])})

        block = ctx.enter_context(nc.Block())
        progs = {k: [] for k in ("pe", "dve", "act", "pool", "sp")}

        def vec(i):
            return vecs[:, i:i + 1]

        def col(t, a, n=CH):
            return t[:, bass.ds(a, n)]

        s_x = [sem(f"x_batch{i}_loaded") for i in range(B)]
        s_first = sem("first_constants_loaded")
        s_const = sem("constants_loaded")
        first_consts = [(centre[:, :], w["centre"]), (mean_at[:, :], w["mean_at"])]
        consts = [(parts_at[:, :], w["parts_at"]), (b2_at[:, :], w["b2_at"]), (ident[:, :], w["ident"]),
                  (ident16[:, :], w["ident16"]), (pick[:, :], w["pick"]), (pick_e[:, :], w["pick_e"]),
                  (tie[:, :], w["tie"]), (mask[:, :], w["mask"]), (mask_t[:, :], w["mask_t"]), (vecs[:, :], w["vecs"]),
                  (bqk[:, :], w["bqk"]), (b1[:, :], w["b1"])]
        n_const = 16 * len(consts)

        waits_met = {e.engine: sem(f"waits_met_{n}") for n, e in (("dve", nc.vector), ("pool", nc.gpsimd))}

        def apart(e):
            e.sem_inc(waits_met[e.engine], 1)

        def load_sp(sp):
            for c in range(4):
                sp.dma_start(X[:, c * T:(c + 1) * T], x[:, c * T:(c + 1) * T]).then_inc(s_x[c], 16)
            for dst, src in consts:
                sp.dma_start(dst, src).then_inc(s_const, 16)

        def load_act(act):
            for dst, src in first_consts:
                act.dma_start(dst, src).then_inc(s_first, 16)
        s_b2 = sem("b2_loaded")
        s_b2z = sem("b2_zeroed")

        def zero_b2(pool):
            pool.memset(b2rep[:, :], 0.0).then_inc(s_b2z, 1)

        def load_b2(sp):
            sp.wait_ge(s_b2z, 1)
            for k in range(6):
                sp.dma_start(b2rep[k * E:(k + 1) * E, :], w["b2"]).then_inc(s_b2, 16)
        progs["pool"].append(zero_b2)
        progs["sp"] += [load_sp, load_b2]
        progs["act"].append(load_act)

        def layer_norm(tag, src, keep_first, double, affine, shifted, pe_first, dve_first, wait_src=None):
            cent = sem(f"{tag}_centred")
            copied = sem(f"{tag}_copied")
            squared = sem(f"{tag}_squared")
            summed = sem(f"{tag}_summed")
            dchain = sem(f"{tag}_dve_chain")
            rooted = sem(f"{tag}_rooted")
            spread = sem(f"{tag}_spread")
            normed = sem(f"{tag}_normed")
            done = sem(f"{tag}_done") if affine else None
            SQ = [ln_scratch[:, i, :] for i in (0, 1)]
            TMP = [ln_scratch[:, i, :] for i in (2, 3)]
            PV = bank[2][:, 0:P]
            scales = 2 if keep_first else 1
            CHAIN = 2 + (5 if double else 0) + 5 * scales

            def hcol(c):
                return c * CH + (c // 2 + 1 if shifted else 0)

            def pe(e):
                pe_first(e)
                for c in range(NCH + 2):
                    if c < NCH:
                        if c >= 2:
                            e.wait_ge(copied, c - 1)
                        if wait_src:
                            wait_src(e, c)
                        e.matmul(bank[c % 2], centre[:, :], src[:, c * CH:(c + 1) * CH],
                                 start=True, stop=True).then_inc(cent, 1)
                    if c >= 2:
                        e.wait_ge(squared, c - 1)
                        for g in range(4):
                            m = e.matmul(PV[32 * g:32 * g + 32], mean_at[:, NCH + 1 - c:NCH + 33 - c],
                                         SQ[c % 2][:, g * P:(g + 1) * P], start=(c == 2), stop=(c == NCH + 1),
                                         skip_group_check=True)
                        m.then_inc(summed, 1)
                for c in range(NCH):
                    if c == 0:
                        e.wait_ge(dchain, CHAIN)
                    if c >= 2:
                        e.wait_ge(normed, scales * (c - 1))
                    for s in range(scales):
                        for i in range(4):
                            m = e.matmul(bank[3 + 2 * (c % 2) + s][:, i * P:(i + 1) * P],
                                         pick[:, 4 * c + i:4 * c + i + 1].to_broadcast([P, P]),
                                         rp[:, s, :], start=True, stop=True)
                    m.then_inc(spread, 1)

            def dve(e):
                dve_first(e)
                for c in range(NCH):
                    e.wait_ge(cent, c + 1)
                    e.tensor_copy(XC[:, c * CH:(c + 1) * CH], bank[c % 2]).then_inc(copied, 1)
                n = [0]

                def step(ins):
                    n[0] += 1
                    ins.then_inc(dchain, 1)
                    e.wait_ge(dchain, n[0])
                e.wait_ge(summed, NCH)
                if wait_src:
                    e.wait_ge(s_const, n_const)
                ve, sd, r1, t1, r2, r12 = (v[:, :] for v in var)
                step(e.tensor_scalar(ve, PV, EPS, None, ALU.add))
                e.wait_ge(rooted, 1)
                step(e.reciprocal(r1, sd))
                if double:
                    step(e.tensor_tensor(t1, PV, r1, ALU.mult))
                    step(e.tensor_tensor(t1, t1, r1, ALU.mult))
                    step(e.tensor_scalar(t1, t1, EPS, None, ALU.add))
                    e.wait_ge(rooted, 2)
                    step(e.reciprocal(r2, sd))
                    step(e.tensor_tensor(r12, r1, r2, ALU.mult))
                parts = [r12] if double else [r1]
                if keep_first:
                    parts.append(r1)
                for s, r in enumerate(parts):
                    a, q = rp[:, s, :], lr[:, s, :]
                    step(e.tensor_copy(a, r))
                    step(e.scalar_tensor_tensor(out=q, in0=a, scalar=parts_at[:, 0:1], in1=r,
                                                op0=ALU.mult, op1=ALU.add))
                    step(e.tensor_copy(a, q))
                    step(e.scalar_tensor_tensor(out=q, in0=a, scalar=parts_at[:, 1:2], in1=q,
                                                op0=ALU.mult, op1=ALU.add))
                    step(e.tensor_copy(a, q))
                assert n[0] == CHAIN
                for c in range(NCH):
                    e.wait_ge(spread, c + 1)
                    xc = XC[:, c * CH:(c + 1) * CH]
                    hc = H[:, hcol(c):hcol(c) + CH]
                    if affine:
                        if c >= 2:
                            e.wait_ge(done, c - 1)
                        hc = TMP[c % 2]
                    ins = e.tensor_tensor(hc, xc, bank[3 + 2 * (c % 2)], ALU.mult)
                    ins.then_inc(normed, 1)
                    if keep_first:
                        e.tensor_tensor(XP[:, c * CH:(c + 1) * CH], xc, bank[4 + 2 * (c % 2)],
                                        ALU.mult).then_inc(normed, 1)

            def act(e):
                for c in range(NCH):
                    e.wait_ge(copied, c + 1)
                    if c >= 2:
                        e.wait_ge(summed, c - 1)
                    e.activation(SQ[c % 2], XC[:, c * CH:(c + 1) * CH], ACT.Square).then_inc(squared, 1)
                e.wait_ge(dchain, 1)
                e.activation(var[1][:, :], var[0][:, :], ACT.Sqrt).then_inc(rooted, 1)
                if double:
                    e.wait_ge(dchain, 5)
                    e.activation(var[1][:, :], var[3][:, :], ACT.Sqrt).then_inc(rooted, 1)
                if affine:
                    for c in range(NCH):
                        e.wait_ge(normed, scales * c + 1)
                        e.activation(H[:, hcol(c):hcol(c) + CH], TMP[c % 2], ACT.Identity,
                                     scale=vec(affine[0]), bias=vec(affine[1])).then_inc(done, 1)
            progs["pe"].append(pe)
            progs["dve"].append(dve)
            progs["act"].append(act)
            if affine:
                return lambda e, c: e.wait_ge(done, c)
            return lambda e, c: e.wait_ge(normed, scales * c)

        def time_mix():
            wts = cut(3, P)
            wo = cut(P)
            wm = cut(3, 2, P)
            mix1 = cut(3)
            negw = cut(1)
            spare = cut(1)
            PP, AA, BB = cut(T + 1), cut(T + 1), cut(T + 1)
            EA, EX = [cut(4, CH), cut(4, CH)], [cut(4, CH), cut(4, CH)]
            EV, NV, SR = [[cut(CH), cut(CH)] for _ in range(3)]
            G1, G3, PM = [[cut(CH), cut(CH)] for _ in range(3)]
            NUM, DN, RW = G1, G3, PM
            load = sem("tm_weights")
            ready = sem("tm_prepared")
            kvr = sem("tm_kvr_done")
            owd = sem("tm_out_done")
            dve = Steps(sem("tm_dve"), [
                "pp0", "pp1", "a0", "b0", "m0", "a1", "b1", "m1", "d0", "d1",
                "ev0", "ev1", "aa0", "bb0", "nv0", "aa1", "bb1", "nv1",
                "rec0", "num0", "ns0", "rec1", "rw0", "num1", "ns1", "rw1"])
            act = Steps(sem("tm_act"), ["sg0", "sg1", "table", "ex0", "ex1"])
            pool = Steps(sem("tm_pool"), ["c0", "c1", "h0", "den0", "g0", "h1", "den1", "g1"])
            tm_added = sem("tm_added")

            def f_sp(e):
                e.dma_start(wts, w["att_kvr"]).then_inc(load, 16)
                e.dma_start(wo, w["att_ow"]).then_inc(load, 16)

            def f_pool(e):
                pool.start(e)
                with e.Fori(1, B + 1) as it:
                    for c in range(2):
                        dve.wait(e, f"m{c}", it)
                        act.wait(e, f"ex{c}", it - 1)
                        e.tensor_tensor(EA[c][:, 2, :], PP[:, c * CH:(c + 1) * CH], PM[c],
                                        ALU.subtract).then_inc(pool.sem, 1)
                    for c in range(2):
                        act.wait(e, f"ex{c}", it)
                        dve.wait(e, f"bb{c}", it)
                        e.tensor_tensor(G3[c], EX[c][:, 2, :], BB[:, c * CH:(c + 1) * CH],
                                        ALU.mult).then_inc(pool.sem, 1)
                        pool.wait(e, f"h{c}", it)
                        e.tensor_tensor(G3[c], G3[c], EX[c][:, 3, :], ALU.add).then_inc(pool.sem, 1)
                        e.tensor_tensor(G1[c], EX[c][:, 2, :], AA[:, c * CH:(c + 1) * CH],
                                        ALU.mult).then_inc(pool.sem, 1)

            def f_act(e):
                e.wait_ge(s_const, n_const)
                e.activation(negw, vec(DECAY), ACT.Exp).then_inc(ready, 1)
                act.start(e)
                with e.Fori(1, B + 1) as it:
                    for c in range(2):
                        e.wait_ge(kvr, it * 2 + (c - 1))
                        dve.wait(e, f"ns{c}", it - 1)
                        e.activation(SR[c], bank[3 * c + 2], ACT.Sigmoid).then_inc(act.sem, 1)
                    act.wait(e, "table", it - 1)
                    e.activation(spare, vec(DECAY), ACT.Exp, scale=0.0).then_inc(act.sem, 1)
                    for c in range(2):
                        dve.wait(e, f"d{c}", it)
                        pool.wait(e, f"c{c}", it)
                        dve.wait(e, f"nv{c}", it - 1)
                        pool.wait(e, f"g{c}", it - 1)
                        e.activation(EX[c], EA[c], ACT.Exp).then_inc(act.sem, 1)

            def f_pe(e):
                e.wait_ge(ready, 3)

                def kvr_of(c, first):
                    for m in range(3):
                        for half in range(2):
                            last = e.matmul(bank[3 * c + m], wm[:, m, half, :], col(H, first - half),
                                            start=(half == 0), stop=(half == 1))
                    last.then_inc(kvr, 1)
                kvr_of(0, 1)
                kvr_of(1, 1 + CH)

                def body(it, last):
                    if not last:
                        nxt = it * (T + 1) + 1
                        dve.wait(e, "nv0", it)
                        act.wait(e, "sg0", it)
                        kvr_of(0, nxt)
                        dve.wait(e, "nv1", it)
                        act.wait(e, "sg1", it)
                        kvr_of(1, nxt + CH)
                    for c in range(2):
                        dve.wait(e, f"rw{c}", it)
                        e.matmul(bank[6 + c], wo, PM[c], start=True, stop=True).then_inc(owd, 1)
                with e.Fori(1, B) as it:
                    body(it, False)
                body(B, True)

            def f_dve(e):
                e.wait_ge(load, 32)
                e.wait_ge(s_const, n_const)
                e.memset(PP[:, 0:1], -1e38)
                e.memset(AA[:, 0:1], 0.0)
                e.memset(BB[:, 0:1], 0.0)
                e.tensor_scalar(mix1, vecs[:, TMK:TMR + 1], -1.0, 1.0, ALU.mult, ALU.add).then_inc(ready, 1)
                e.wait_ge(ready, 2)
                for m in range(3):
                    e.tensor_scalar(wm[:, m, 0, :], wts[:, m, :], vecs[:, TMK + m:TMK + m + 1], None, ALU.mult)
                    last = e.tensor_scalar(wm[:, m, 1, :], wts[:, m, :], mix1[:, m:m + 1], None, ALU.mult)
                last.then_inc(ready, 1)
                e.tensor_scalar(negw, negw, -1.0, None, ALU.mult).then_inc(ready, 1)
                e.wait_ge(ready, 4)
                dve.start(e)
                u = vec(FIRST)

                def inc(ins):
                    ins.then_inc(dve.sem, 1)

                def add(c, it):
                    e.wait_ge(owd, it * 2 + (c - 1))
                    xp = col(XP, it * T - T + c * CH)
                    e.tensor_tensor(xp, bank[6 + c], xp, ALU.add).then_inc(tm_added, 1)

                def body(it, first):
                    def w_(name):
                        dve.wait(e, name, it)
                    lo = [slice(c * CH, (c + 1) * CH) for c in range(2)]
                    hi = [slice(c * CH + 1, (c + 1) * CH + 1) for c in range(2)]
                    for c in range(2):
                        e.wait_ge(kvr, it * 2 + (c - 1))
                        if c:
                            w_("pp0")
                        inc(e.tensor_tensor_scan(PP[:, hi[c]], negw.to_broadcast([P, CH]), bank[3 * c],
                                                 PP[:, c * CH:c * CH + 1], ALU.add, ALU.max))
                    if not first:
                        add(0, it - 1)
                        add(1, it - 1)
                    for c in range(2):
                        w_(f"pp{c}")
                        inc(e.scalar_tensor_tensor(out=EA[c][:, 0, :], in0=PP[:, lo[c]], scalar=negw,
                                                   in1=PP[:, hi[c]], op0=ALU.add, op1=ALU.subtract))
                        inc(e.tensor_tensor(EA[c][:, 1, :], bank[3 * c], PP[:, hi[c]], ALU.subtract))
                        inc(e.scalar_tensor_tensor(out=PM[c], in0=bank[3 * c], scalar=u, in1=PP[:, lo[c]],
                                                   op0=ALU.add, op1=ALU.max))
                    for c in range(2):
                        w_(f"m{c}")
                        inc(e.scalar_tensor_tensor(out=EA[c][:, 3, :], in0=bank[3 * c], scalar=u, in1=PM[c],
                                                   op0=ALU.add, op1=ALU.subtract))
                    for c in range(2):
                        act.wait(e, f"ex{c}", it)
                        inc(e.tensor_tensor(EV[c], EX[c][:, 1, :], bank[3 * c + 1], ALU.mult))
                    for c in range(2):
                        w_("ev1" if c == 0 else "aa0")
                        inc(e.tensor_tensor_scan(AA[:, hi[c]], EX[c][:, 0, :], EV[c],
                                                 AA[:, c * CH:c * CH + 1], ALU.mult, ALU.add))
                        if c:
                            w_("bb0")
                        inc(e.tensor_tensor_scan(BB[:, hi[c]], EX[c][:, 0, :], EX[c][:, 1, :],
                                                 BB[:, c * CH:c * CH + 1], ALU.mult, ALU.add))
                        inc(e.tensor_tensor(NV[c], EX[c][:, 3, :], bank[3 * c + 1], ALU.mult))

                    def num(c):
                        pool.wait(e, f"g{c}", it)
                        w_(f"nv{c}")
                        inc(e.tensor_tensor(NUM[c], NV[c], G1[c], ALU.add))

                    def rec(c):
                        pool.wait(e, f"den{c}", it)
                        inc(e.reciprocal(DN[c], DN[c]))

                    def ns(c):
                        w_(f"num{c}")
                        inc(e.tensor_tensor(NUM[c], NUM[c], SR[c], ALU.mult))

                    def rw(c):
                        w_(f"ns{c}")
                        inc(e.tensor_tensor(RW[c], NUM[c], DN[c], ALU.mult))
                    rec(0)
                    num(0)
                    ns(0)
                    rec(1)
                    rw(0)
                    num(1)
                    ns(1)
                    rw(1)
                body(1, True)
                with e.Fori(2, B + 1) as it:
                    body(it, False)
                add(0, B)
                add(1, B)
            for k, f in (("sp", f_sp), ("pool", f_pool), ("act", f_act), ("pe", f_pe), ("dve", f_dve)):
                progs[k].append(f)

            def finished(e):
                e.wait_ge(tm_added, 2 * B)
            return finished

        def channel_mix(wait_h):
            wk, wr, wv = cut(FB * P), cut(P), cut(FB, P)
            mix1 = cut(2)
            TK, TR, XK, XR = [[cut(CH), cut(CH)] for _ in range(4)]
            R = [cut(FB, CH), cut(FB, CH)]
            Q = [cut(FB, CH), cut(FB, CH)]
            SR = [cut(CH), cut(CH)]
            KV = [cut(CH), cut(CH)]
            XS = [cut(CH), cut(CH)]
            load = sem("cm_weights")
            ready = sem("cm_prepared")
            hidden = sem("cm_hidden_done")
            out_d = sem("cm_out_done")
            mixed = Steps(sem("cm_mixed"), ["tk0", "tr0", "xk0", "xr0", "tk1", "tr1", "xk1", "xr1"])
            dve = Steps(sem("cm_dve"), ["sq0", "sq1", "kv0", "xa0", "kv1", "xa1"])
            act = Steps(sem("cm_act"), ["ra0", "rb0", "sg0", "ra1", "rb1", "sg1"])
            pool = Steps(sem("cm_pool"), ["xs0", "xs1", "sq0", "sq1"])

            def f_sp(e):
                tm_done(e)
                for dst, src in ((wk, w["f_kw"]), (wr, w["f_rw"]), (wv, w["f_vw"])):
                    e.dma_start(dst, src).then_inc(load, 16)

            def f_pe(e):
                e.sem_inc(hidden, 6)
                e.wait_ge(load, 48)
                with e.Fori(1, B + 1) as it:
                    for c in range(2):
                        mixed.wait(e, f"xr{c}", it)
                        for m in range(FB):
                            if m % 2 == 0:
                                act.wait(e, ("ra", "rb")[m // 2] + str(1 - c), it - 1 if c == 0 else it)
                            last = e.matmul(psum_pair[m // 2][:, m % 2, :], wk[:, m * P:(m + 1) * P], XK[c],
                                            start=True, stop=True)
                            if m % 2:
                                last.then_inc(hidden, 1)
                        act.wait(e, f"sg{c}", it - 1)
                        e.matmul(bank[c], wr, XR[c], start=True, stop=True).then_inc(hidden, 1)
                    for c in range(2):
                        dve.wait(e, f"sq{c}", it)
                        pool.wait(e, f"sq{c}", it)
                        dve.wait(e, f"kv{c}", it - 1)
                        for m in range(FB):
                            last = e.matmul(bank[(2, 7)[c]], wv[:, m, :], Q[c][:, m, :],
                                            start=(m == 0), stop=(m == FB - 1))
                        last.then_inc(out_d, 1)

            def f_act(e):
                act.start(e)
                with e.Fori(1, B + 1) as it:
                    for c in range(2):
                        for k in range(2):
                            e.wait_ge(hidden, it * 6 + (3 * c + k + 1))
                            dve.wait(e, f"sq{c}", it - 1)
                            pool.wait(e, f"sq{c}", it - 1)
                            e.activation(R[c][:, 2 * k:2 * k + 2, :], psum_pair[k][:, :, :],
                                         ACT.Relu).then_inc(act.sem, 1)
                        e.wait_ge(hidden, it * 6 + (3 * c + 3))
                        dve.wait(e, f"kv{c}", it - 1)
                        e.activation(SR[c], bank[c], ACT.Sigmoid).then_inc(act.sem, 1)

            def f_pool(e):
                tm_done(e)
                pool.start(e)
                with e.Fori(1, B + 1) as it:
                    for c in range(2):
                        at = it * T + (c * CH - T)
                        dve.wait(e, f"xa{c}", it - 1)
                        e.tensor_tensor(XS[c], col(X, at), col(XP, at), ALU.add).then_inc(pool.sem, 1)
                    for c in range(2):
                        act.wait(e, f"rb{c}", it)
                        e.tensor_tensor(Q[c][:, 2:4, :], R[c][:, 2:4, :], R[c][:, 2:4, :],
                                        ALU.mult).then_inc(pool.sem, 1)

            def f_dve(e):
                wait_h(e, NCH)
                e.tensor_scalar(mix1, vecs[:, FTMK:FTMR + 1], -1.0, 1.0, ALU.mult, ALU.add).then_inc(ready, 1)
                e.wait_ge(ready, 1)
                dve.start(e)
                mixed.start(e)

                def mixes(it):
                    for c in range(2):
                        at = it * (T + 1) + (c * CH - T)
                        e.wait_ge(hidden, it * 6 - 3 + 3 * c)
                        for t, m in ((TK, 0), (TR, 1)):
                            e.tensor_scalar(t[c], col(H, at - 1), mix1[:, m:m + 1], None, ALU.mult)\
                                .then_inc(mixed.sem, 1)
                        mixed.wait(e, f"tk{c}", it)
                        e.scalar_tensor_tensor(out=XK[c], in0=col(H, at), scalar=vec(FTMK), in1=TK[c],
                                               op0=ALU.mult, op1=ALU.add).then_inc(mixed.sem, 1)
                        mixed.wait(e, f"tr{c}", it)
                        e.scalar_tensor_tensor(out=XR[c], in0=col(H, at), scalar=vec(FTMR), in1=TR[c],
                                               op0=ALU.mult, op1=ALU.add).then_inc(mixed.sem, 1)

                def body(it, last):
                    for c in range(2):
                        act.wait(e, f"ra{c}", it)
                        e.tensor_tensor(Q[c][:, 0:2, :], R[c][:, 0:2, :], R[c][:, 0:2, :], ALU.mult)\
                            .then_inc(dve.sem, 1)
                    if not last:
                        mixes(it + 1)
                    for c in range(2):
                        at = it * T + (c * CH - T)
                        e.wait_ge(out_d, it * 2 + (c - 1))
                        act.wait(e, f"sg{c}", it)
                        e.tensor_tensor(KV[c], bank[(2, 7)[c]], SR[c], ALU.mult).then_inc(dve.sem, 1)
                        dve.wait(e, f"kv{c}", it)
                        pool.wait(e, f"xs{c}", it)
                        e.tensor_tensor(col(X, at), KV[c], XS[c], ALU.add).then_inc(dve.sem, 1)
                mixes(1)
                with e.Fori(1, B) as it:
                    body(it, False)
                body(B, True)
            for k, f in (("sp", f_sp), ("pool", f_pool), ("act", f_act), ("pe", f_pe), ("dve", f_dve)):
                progs[k].append(f)
            return dve

        def experts(tag, before, wait_h, last_stage):
            used[0] = OPERANDS
            w1, w2 = cut(E, HB * P), cut(E, HB, P)
            gw = cut(32)
            LT = [cut(CH), cut(CH)]
            lg = cut(NBLK, E)
            GT = cut(N + CH, dt=BF16)
            HGT = [cut(HB, CH), cut(HB, CH)]
            r0 = used[0]
            R = [cut(HB, CH), cut(HB, CH)]
            G3 = arena[:, r0:r0 + NBLK * P // 2].bitcast(BF16).rearrange("p (b n) -> p b n", b=NBLK)
            LP, PA, KA, O1, O2 = (cut(NBLK, E) for _ in range(5))
            m1, m2, m3 = cut(NBLK), cut(NBLK), cut(NBLK)
            load = sem(f"{tag}_weights")
            zero = sem(f"{tag}_zeroed")
            logit = sem(f"{tag}_logits")
            lt_in = sem(f"{tag}_logits_in_sbuf")
            lg_turned = sem(f"{tag}_logits_turned")
            lg_in = sem(f"{tag}_logits_token_major")
            chain = sem(f"{tag}_gate_chain")
            expd = sem(f"{tag}_gate_exp")
            turned = sem(f"{tag}_gates_turned")
            turned_s = sem(f"{tag}_gates_in_sbuf")
            z_done = sem(f"{tag}_hidden_done")
            relu_d = sem(f"{tag}_relu_done")
            gated = sem(f"{tag}_gated")
            y_done = sem(f"{tag}_expert_out_done")
            added = sem(f"{tag}_added")
            AHEAD, Y_AHEAD = 2, 4
            LEAD = 3
            hi_done = sem(f"{tag}_hidden_hi")
            lo_done = sem(f"{tag}_hidden_lo")
            w_hi = sem(f"{tag}_weights_hi")
            w_split = sem(f"{tag}_weights_split")
            hi_in = sem(f"{tag}_input_hi")
            in_split = sem(f"{tag}_input_split")

            def f_sp(e):
                before(e)
                for dst, src in ((gw[:, 0:E], w["gate"]), (w1, w["W1"]), (w2, w["W2"])):
                    e.dma_start(dst, src).then_inc(load, 16)
                if last_stage:
                    stored = sem("stored")
                    with e.Fori(1, NCH + 1) as it:
                        e.wait_ge(added, it + AHEAD)
                        e.dma_start(out[:, bass.ds(it * CH - CH, CH)], col(X, it * CH - CH)).then_inc(stored, 16)
                    e.wait_ge(stored, 16 * NCH)

            def f_pool(e):
                before(e)
                e.memset(gw[:, E:32], 0.0)
                e.memset(GT[:, N:N + CH], 0.0)
                e.memset(G3, 0.0).then_inc(zero, 1)
                e.memset(h_hi[:, N:N + CH].bitcast(F32), 0.0)
                e.memset(h_lo[:, N:N + CH].bitcast(F32), 0.0).then_inc(zero, 1)
                e.wait_ge(w_hi, 1)
                e.tensor_tensor(w1_lo[:], w1, w1_hi[:].bitcast(F32), ALU.subtract).then_inc(w_split, 1)
                for c in range(NCH):
                    r = slice(c * CH, (c + 1) * CH)
                    e.wait_ge(hi_in, c + 1)
                    e.tensor_tensor(h_lo[:, r], H[:, r], h_hi[:, r].bitcast(F32), ALU.subtract).then_inc(in_split, 1)
                e.wait_ge(w_hi, 2)
                e.tensor_tensor(w2_lo[:], w2, w2_hi[:].bitcast(F32), ALU.subtract).then_inc(w_split, 1)

            n_load = 48
            lt_bank, lg_bank = (bank[7], bank[0]), (bank[1], bank[2])
            turn = [bank[1].bitcast(BF16), bank[2].bitcast(BF16)]

            def f_pe(e):
                def hidden(s, at, ex):
                    for k in range(HB):
                        ks = slice(k * P, (k + 1) * P)
                        e.matmul(psum_pair[s][:, k, :], w1_hi[:, ex, ks], col(h_hi, at), start=True, stop=False)
                        e.matmul(psum_pair[s][:, k, :], w1_hi[:, ex, ks], col(h_lo, at), start=False, stop=False)
                        m = e.matmul(psum_pair[s][:, k, :], w1_lo[:, ex, ks], col(h_hi, at), start=False, stop=True)
                    return m

                def spread_gate(s, at, ex):
                    return e.matmul(bank[1 + s], pick_e[:, ex:ex + 1].to_broadcast([P, P]), col(GT, at),
                                    start=True, stop=True)
                e.wait_ge(load, n_load)
                e.wait_ge(zero, 1)
                for half in range(2):
                    for g in range(4):
                        c = 4 * half + g
                        wait_h(e, c + 1)
                        m = e.matmul(lt_bank[half][32 * g:32 * g + 32], gw, H[:, c * CH:(c + 1) * CH],
                                     start=True, stop=True)
                    m.then_inc(logit, 1)
                for half in range(2):
                    e.wait_ge(lt_in, half + 1)
                    for k in range(4):
                        m = e.transpose(lg_bank[half][:, k * P:(k + 1) * P], LT[half][:, k * P:(k + 1) * P], ident[:, :])
                    m.then_inc(lg_turned, 1)
                e.wait_ge(w_split, 1)
                e.wait_ge(in_split, 1)
                hidden(0, 0, 0)
                hidden(1, 0, 1)
                e.wait_ge(chain, N_GATE)
                for q in range(NCH):
                    if q >= 2:
                        e.wait_ge(turned_s, q - 1)
                    for i in range(4):
                        m = e.transpose(turn[q % 2][:, i * P:(i + 1) * P], G3[:, 4 * q + i, :], ident16[:, :])
                    m.then_inc(turned, 1)

                def z(s, at, ex):
                    spread_gate(s, at, ex)
                    hidden(s, at, ex).then_inc(z_done, 1)
                e.wait_ge(turned_s, NCH)
                e.wait_ge(w_split, 2)
                e.wait_ge(zero, 2)
                for ex in range(2):
                    spread_gate(ex, 0, ex).then_inc(z_done, 1)
                e.wait_ge(relu_d, 1 + AHEAD)
                e.wait_ge(gated, 1 + AHEAD)
                z(0, 0, 2)
                with e.Fori(1, NCH // 2 + 1) as it:
                    for cc in range(2):
                        yb = bank[(0, 7)[cc]]
                        at = it * 2 * CH + (cc - 2) * CH
                        for ex in range(E):
                            s = it * 2 * E + ((cc - 2) * E + ex)
                            e.wait_ge(relu_d, s + (LEAD - 1) + AHEAD)
                            e.wait_ge(gated, s + (LEAD - 1) + AHEAD)
                            if ex + LEAD < E:
                                z((ex + LEAD) % 2, at, ex + LEAD)
                            else:
                                z((ex + LEAD) % 2, at + CH, ex + LEAD - E)
                            if ex == 0:
                                e.wait_ge(added, it * 2 + (cc - 2) + AHEAD - 1)
                                e.matmul(yb, b2p[:, :], col(GT, at), start=True, stop=False)
                            e.wait_ge(hi_done, s + 1 + AHEAD)
                            e.wait_ge(lo_done, s + 1 + AHEAD)
                            for k in range(HB):
                                hi, lo = HG_HI[:, ex % 4, k, :], HG_LO[:, ex % 4, k, :]
                                e.matmul(yb, w2_hi[:, ex, k, :], hi, start=False, stop=False)
                                e.matmul(yb, w2_hi[:, ex, k, :], lo, start=False, stop=False)
                                m = e.matmul(yb, w2_lo[:, ex, k, :], hi, start=False,
                                             stop=(ex == E - 1 and k == HB - 1))
                            m.then_inc(y_done, 1)

            def f_act(e):
                e.wait_ge(load, n_load)
                for hi, w_ in ((w1_hi, w1), (w2_hi, w2)):
                    e.activation(hi[:], w_, ACT.Copy).then_inc(w_hi, 1)

                def hi_of_input(half):
                    for c in range(4 * half, 4 * half + 4):
                        wait_h(e, c + 1)
                        r = slice(c * CH, (c + 1) * CH)
                        e.activation(h_hi[:, r], H[:, r], ACT.Copy).then_inc(hi_in, 1)

                def logits_in(half):
                    e.wait_ge(logit, half + 1)
                    e.activation(LT[half], lt_bank[half], ACT.Copy).then_inc(lt_in, 1)

                def token_major(half):
                    e.wait_ge(lg_turned, half + 1)
                    src = lg_bank[half].rearrange("p (k g r) -> p g k r", k=4, g=4)[:, :, :, 0:E]
                    dst = lg[:, 16 * half:16 * half + 16, :].rearrange("p (g k) e -> p g k e", g=4)
                    e.activation(dst, src, ACT.Copy).then_inc(lg_in, 1)
                hi_of_input(0)
                logits_in(0)
                hi_of_input(1)
                logits_in(1)
                token_major(0)
                token_major(1)
                e.wait_ge(chain, 2)
                e.activation(PA, LP, ACT.Exp).then_inc(expd, 1)
                e.sem_inc(relu_d, AHEAD)
                e.wait_ge(chain, N_GATE)

                def relu(s, ex):
                    e.wait_ge(z_done, s + 1)
                    e.wait_ge(gated, s - 1 + AHEAD)
                    for k in range(HB):
                        ins = e.activation(R[ex % 2][:, k, :], psum_pair[ex % 2][:, k, :], ACT.Relu,
                                           bias=b1[:, ex * HB + k:ex * HB + k + 1])
                    ins.then_inc(relu_d, 1)
                relu(0, 0)
                with e.Fori(1, NCH // 2 + 1) as it:
                    for cc in range(2):
                        for ex in range(E):
                            s = it * 2 * E + ((cc - 2) * E + ex)
                            relu(s + 1, (ex + 1) % E)
                            e.wait_ge(gated, s + 1 + AHEAD)
                            e.wait_ge(y_done, s - 3 + Y_AHEAD)
                            e.activation(HG_HI[:, ex % 4], HGT[ex % 2], ACT.Copy).then_inc(hi_done, 1)

            N_GATE = 2 + 16 + 7

            def f_dve(e):
                n = [0]

                def step(ins, dep=True):
                    n[0] += 1
                    ins.then_inc(chain, 1)
                    if dep:
                        e.wait_ge(chain, n[0])
                e.wait_ge(load, n_load)
                if tag == "f1":
                    e.wait_ge(s_b2, 96)
                    b2c = sem("b2_chain")
                    cnt = [0]

                    def st(ins):
                        cnt[0] += 1
                        ins.then_inc(b2c, 1)
                        e.wait_ge(b2c, cnt[0])
                    st(e.tensor_copy(b2p[:, :], b2rep[:, :]))
                    for k, full in enumerate((b2rep, b2t)):
                        st(e.scalar_tensor_tensor(out=b2t[:, :], in0=b2p[:, :], scalar=b2_at[:, k:k + 1],
                                                  in1=full[:, :], op0=ALU.mult, op1=ALU.add))
                        st(e.tensor_copy(b2p[:, :], b2t[:, :]))

                def over(t):
                    return t.unsqueeze(2).to_broadcast([P, NBLK, E])
                tie_b = tie[:, :].unsqueeze(1).to_broadcast([P, NBLK, E])
                e.wait_ge(lg_in, 2)
                step(e.tensor_reduce(m1, lg, AX.X, ALU.max))
                step(e.tensor_tensor(LP, lg, over(m1), ALU.subtract))
                e.wait_ge(expd, 1)
                step(e.tensor_reduce(m1, PA, AX.X, ALU.max))
                step(e.tensor_tensor(KA, PA, over(m1), ALU.is_ge))
                step(e.tensor_tensor(KA, KA, tie_b, ALU.mult))
                step(e.tensor_reduce(m2, KA, AX.X, ALU.max))
                step(e.tensor_tensor(O1, KA, over(m2), ALU.is_equal))
                step(e.scalar_tensor_tensor(out=LP, in0=O1, scalar=-2.0, in1=PA, op0=ALU.mult, op1=ALU.add))
                step(e.tensor_reduce(m1, LP, AX.X, ALU.max))
                step(e.tensor_tensor(KA, LP, over(m1), ALU.is_ge))
                step(e.tensor_tensor(KA, KA, tie_b, ALU.mult))
                step(e.tensor_reduce(m2, KA, AX.X, ALU.max))
                step(e.tensor_tensor(O2, KA, over(m2), ALU.is_equal))
                step(e.tensor_tensor(O1, O1, O2, ALU.add))
                step(e.tensor_tensor(PA, PA, O1, ALU.mult))
                step(e.tensor_reduce(m3, PA, AX.X, ALU.add))
                step(e.reciprocal(m1, m3))
                step(e.tensor_tensor(PA, PA, over(m1), ALU.mult))
                e.wait_ge(zero, 1)
                step(e.tensor_copy(G3[:, :, 0:E], PA))
                step(e.tensor_tensor(KA, PA, G3[:, :, 0:E], ALU.subtract))
                step(e.tensor_copy(G3[:, :, E:2 * E], KA))
                step(e.tensor_tensor(LP, KA, G3[:, :, E:2 * E], ALU.subtract))
                step(e.tensor_copy(G3[:, :, 2 * E:3 * E], LP))
                step(e.tensor_copy(G3[:, :, 3 * E:4 * E], G3[:, :, 0:E]), False)
                step(e.tensor_copy(G3[:, :, 4 * E:6 * E], G3[:, :, 0:2 * E]))
                assert n[0] == N_GATE
                for q in range(NCH):
                    e.wait_ge(turned, q + 1)
                    e.tensor_copy(GT[:, q * CH:(q + 1) * CH], turn[q % 2][:, 0:CH]).then_inc(turned_s, 1)
                e.sem_inc(gated, AHEAD)
                e.sem_inc(added, AHEAD)
                e.sem_inc(lo_done, AHEAD)

                def gate(s, ex):
                    e.wait_ge(relu_d, s + 1 + AHEAD)
                    e.wait_ge(hi_done, s - 1 + AHEAD)
                    e.wait_ge(lo_done, s - 1 + AHEAD)
                    e.tensor_tensor(HGT[ex % 2], R[ex % 2],
                                    bank[1 + ex % 2].unsqueeze(1).to_broadcast([P, HB, CH]),
                                    ALU.mult).then_inc(gated, 1)

                def add(chunk, cc):
                    e.wait_ge(y_done, (chunk + 1) * E + Y_AHEAD)
                    xc = col(X, chunk * CH)
                    e.tensor_tensor(xc, bank[(0, 7)[cc]], xc, ALU.add).then_inc(added, 1)

                def body(it, first):
                    for cc in range(2):
                        for ex in range(E):
                            s = it * 2 * E + ((cc - 2) * E + ex)
                            gate(s + 1, (ex + 1) % E)
                            e.wait_ge(gated, s + 1 + AHEAD)
                            e.wait_ge(hi_done, s + 1 + AHEAD)
                            e.tensor_tensor(HG_LO[:, ex % 4], HGT[ex % 2], HG_HI[:, ex % 4].bitcast(F32),
                                            ALU.subtract).then_inc(lo_done, 1)
                            if ex == LEAD and not (first and cc == 0):
                                add(it * 2 + (cc - 3), 1 - cc)
                gate(0, 0)
                body(1, True)
                with e.Fori(2, NCH // 2 + 1) as it:
                    body(it, False)
                add(NCH - 1, 1)

            def f_pool_ahead(e):
                e.sem_inc(y_done, Y_AHEAD)
                e.sem_inc(hi_done, AHEAD)
            for k, f in (("sp", f_sp), ("pool", f_pool), ("pool", f_pool_ahead), ("act", f_act), ("pe", f_pe),
                         ("dve", f_dve)):
                progs[k].append(f)
            return lambda e: e.wait_ge(added, NCH + AHEAD)

        scr_q = nc.dram_tensor("scratch_q_parts", (B, 3, 2, P, CH), BF16, kind="Internal").ap()
        scr_k = nc.dram_tensor("scratch_k_parts", (B, 3, P, T), BF16, kind="Internal").ap()
        scr_v = nc.dram_tensor("scratch_values", (B, HG, P, VG), F32, kind="Internal").ap()
        scr_rel = nc.dram_tensor("scratch_bias_parts", (HG, 3, HG, S, T), BF16, kind="Internal").ap()
        scr_max = nc.dram_tensor("scratch_max_parts", (HG, 3, HG * 8, P), BF16, kind="Internal").ap()

        def attention(before, wait_h):
            QL = cut(HG, 2, HG, CH, dt=BF16)
            QU = cut(HG, HG, CH, dt=BF16)
            KK = cut(HG, HG, T, dt=BF16)
            VS = cut(HG, VG + 32)
            wqkv, wo = cut(3, P), cut(P)
            grid, rel = cut(T), cut(NH * S)
            bqs = cut(1)
            VA = cut(HG, 8, HG * VW)
            dump = [[cut(CH, dt=BF16), cut(CH, dt=BF16)] for _ in range(2)]
            NM = [cut(2, HG, 4), cut(2, HG, 4)]
            PF = [cut(HG, 4), cut(HG, 4)]
            NF, NR = cut(P), cut(P)
            N3 = [cut(3, P, dt=BF16), cut(3, P, dt=BF16)]
            RC = [cut(4, HG), cut(4, HG)]
            QF, KF, QR, KR = (XC[:, i * T:(i + 1) * T] for i in range(4))
            half_ = 3 * T // 2
            Q3, K3 = ([m.bitcast(BF16).rearrange("p (a n) -> p a n", a=3) for m in (XP[:, at:at + half_], cut(half_))]
                      for at in (0, half_))
            VT = [XP[:, 2 * half_ + i * CH:2 * half_ + (i + 1) * CH] for i in range(2)]
            PR = [b_[:, i * 4 * CH:(i + 1) * 4 * CH].rearrange("p (j n) -> p j n", j=HG)
                  for b_ in (XC, XP) for i in range(2)]

            ATT = H[:, 0:T].rearrange("p (k c) -> p k c", k=8)
            ATTT = H[:, T:2 * T]
            OS = [H[:, 2 * T + i * CH:2 * T + (i + 1) * CH] for i in range(2)]

            load = sem("at_weights")
            const_rows = sem("at_key_rows")
            prep = sem("at_prepared")
            rel_mm = sem("at_rel_product")
            rel_ch = sem("at_rel_chain")
            rel_out = sem("at_rel_copied")
            rel_st = [sem(f"at_rel{i}_stored") for i in range(2)]
            rel_ld = sem("at_rel_loaded")
            pe_s = Steps(sem("at_pe"), ["q0", "k0", "v0", "q1", "k1", "v1", "t0", "t1"])
            act_s = Steps(sem("at_act"), ["q0", "k0", "v0", "q1", "k1", "v1", "va0", "va1"])
            dve_s = Steps(sem("at_dve"), ["q1", "k1", "qr", "kr", "q2", "k2", "q3", "k3"])
            stored = [sem(f"at_parts{i}_stored") for i in range(2)]
            v_stored = sem("at_values_stored")
            slot_ld = [sem(f"at_slot{i}_loaded") for i in range(HG)]
            SLOT = 16 * 13
            ring_ready = sem("at_ring_ready")
            ring_free = sem("at_ring_free")
            pm_ready = sem("at_maxima_ready")
            nm_chain = sem("at_max_chain")
            nm_ready = sem("at_max_parts_ready")
            nm_stored = sem("at_max_parts_stored")
            nm_loaded = [sem(f"at_slot{i}_max_rows_loaded") for i in range(HG)]
            sc_ready = sem("at_scores_ready")
            exp_done = sem("at_exp_done")
            pv_done = sem("at_pv_done")
            os_done = sem("at_out_copied")
            rc_done = sem("at_recip_done")
            RING = 3
            PRO = 2 * (len(ITEMS) + 1)
            IPB = HG * (len(ITEMS) + 3) + 4

            SPREAD = (2, 2, 1, 2, 1, 2, 2, 1, 2, 2, 2, 2, 2, 2, 2, 2, 2, 2, 2, 1)

            def step(hg, with_max, before_=None):
                ev, left = [], list(ITEMS) if with_max else []
                for i in range(NP_):
                    for half in range(2):
                        t = 2 * i + half
                        ev.append(("scores", t, hg, 0))
                        if before_:
                            ev += ending(t, *before_)
                        for _ in range(SPREAD[t]):
                            if left:
                                ev.append(("piece", left.pop(0), hg, 0))
                    if i >= 1:
                        ev.append(("pv", i - 1, hg, 0))
                    if i == HALF_END[0] + 2:
                        ev.append(("turn_out", 0, hg, 0))
                return ev + [("piece", p, hg, 0) for p in left]

            def ending(t, hg, b, with_max=True):
                ev = []
                if t == 1:
                    ev.append(("pv", NP_ - 1, hg, b))
                if t == 2 and with_max:
                    ev.append(("maxima", None, hg, b))
                if t == 3:
                    ev.append(("turn_out", 1, hg, b))
                if hg == HG - 1 and t in (5, 7):
                    ev.append(("turn_att", int(t == 7), hg, b))
                if hg == HG - 1 and t in (8, 9):
                    ev.append(("out", t - 8, hg, b))
                return ev
            HEAD_T = 10

            def batch(last):
                first = step(0, True, (HG - 1, -1))
                cut_at = first.index(("scores", HEAD_T, 0, 0))
                rest = first[cut_at:]
                for hg in range(1, HG):
                    rest += step(hg, not last or hg < 2, (hg - 1, 0))
                    if last and hg == HG - 1:
                        rest = [v for v in rest if v[0] != "maxima" or v[2] < 2]
                return first[:cut_at], rest

            RINGED = ("piece", "turn_out", "maxima", "turn_att", "out")

            def numbered(events, n=0):
                res = []
                for v in events:
                    res.append((*v, n))
                    n += v[0] in RINGED
                return res, n
            HEAD = [v for v in batch(False)[0] if v[3] == 0]
            HEAD_ITEMS = numbered(HEAD)[1]
            HEAD = numbered(HEAD, -HEAD_ITEMS)[0]
            BODY, n_body = numbered(batch(False)[1] + [(k, a_, g_, b_ + 1) for k, a_, g_, b_ in batch(False)[0]])
            LAST, LAST_ITEMS = numbered(batch(True)[1] +
                                        [v for t in range(HEAD_T) for v in ending(t, HG - 1, 0, False)])
            assert n_body == IPB
            TOTAL = PRO + HEAD_ITEMS + (B - 1) * IPB + LAST_ITEMS

            def item_no(it, local):
                return it * IPB + (PRO + HEAD_ITEMS - IPB + local)

            def item_of(events, kind, arg):
                for k, a_, g_, _, n in events:
                    if (k, a_, g_) == (kind, arg, HG - 1):
                        return n

            def over_batches(eng, head, body):
                head()
                with eng.Fori(1, B) as it:
                    body(it, False)
                body(B, True)

            def load_slot(e, b, hg):
                bs = bass.ds(b, 1)
                rows = slice(hg * 32, (hg + 1) * 32)

                def move(dst, src):
                    e.dma_start(dst, src).then_inc(slot_ld[hg], 16)
                for part, row, reps in ((0, 0, 3), (1, 3 * D, 2), (2, 5 * D, 1)):
                    dst = slice(row, row + reps * D)
                    for half in range(2):
                        src = scr_q[bs, part, half, rows, :].rearrange("o (d j) n -> o d (j n)", j=HG)
                        if reps > 1:
                            src = src.to_broadcast([reps, D, HG * CH])
                        else:
                            src = src.rearrange("o d n -> (o d) n")
                        move(QL[dst, hg, half, :, :].rearrange("p j n -> p (j n)"), src)
                        if half:
                            move(QU[dst, hg, :, :].rearrange("p j n -> p (j n)"), src)
                    src = scr_k[bs, 0:reps, rows, :].rearrange("o t (d j) n -> (o t) d (j n)", j=HG)
                    move(KK[dst, hg, :, :].rearrange("p j n -> p (j n)"), src)
                e.dma_start(VS[:, hg, 0:VG], scr_v[bs, hg, :, :].rearrange("o p n -> (o p) n"))\
                    .then_inc(slot_ld[hg], 16)

            def send_maxima(e, n, slot, par):
                e.wait_ge(nm_ready, n + 1)
                e.dma_start(scr_max[slot].rearrange("t r i -> r t i"), N3[par][0:32]).then_inc(nm_stored, 16)
                e.wait_ge(nm_stored, n * 16 + 16)
                rows = scr_max[slot].rearrange("t r i -> t (r i)")
                e.dma_start(QL[MAX0:ROWS, slot].rearrange("p a j n -> p (a j n)"), rows).then_inc(nm_loaded[slot], 16)
                e.dma_start(QU[MAX0:ROWS, slot].rearrange("p j n -> p (j n)"), rows[:, HG * CH:])\
                    .then_inc(nm_loaded[slot], 16)

            def all_stored(e):
                e.wait_ge(stored[0], 16 * B + 32)
                e.wait_ge(stored[1], 16 * B + 32)
                e.wait_ge(v_stored, 16 * B + 16)

            def f_sp(e):
                before(e)
                for dst, src in ((wqkv, w["wqkv"]), (wo, w["wo"]), (grid[0:S], w["grid_t"]),
                                 (rel[0:S], w["rel"].rearrange("i h j -> i (h j)"))):
                    e.dma_start(dst, src).then_inc(load, 16)
                for s in range(HG):
                    e.dma_start(KK[REL0:ROWS, s, :, :], w["key_rows"].unsqueeze(1).to_broadcast([3 * SW + 3, HG, T]))\
                        .then_inc(const_rows, 16)

                def store_grid(hg):
                    e.wait_ge(rel_ch, 4 * hg + 4)
                    e.dma_start(scr_rel[hg].rearrange("t j s n -> (j s) t n"), (Q3, K3)[hg % 2][0])\
                        .then_inc(rel_st[hg % 2], 16)

                def load_grid(hg):
                    e.wait_ge(rel_st[hg % 2], 16 * (hg // 2) + 16)
                    for p in range(3):
                        rows = slice(REL0 + p * SW, REL0 + (p + 1) * SW)
                        for half in range(2):
                            e.dma_start(QL[rows, hg, half, :, :], scr_rel[hg, p, :, 0:SW, half * CH:(half + 1) * CH]
                                        .rearrange("j s n -> s j n")).then_inc(rel_ld, 16)
                        e.dma_start(QU[rows, hg, :, :], scr_rel[hg, p, :, S - SW:S, CH:T]
                                    .rearrange("j s n -> s j n")).then_inc(rel_ld, 16)

                def store_parts(b):
                    dve_s.wait(e, "q3", b + 1)
                    e.dma_start(scr_q[b].rearrange("t a p n -> p (t a) n"),
                                Q3[b % 2].rearrange("p t (a n) -> p (t a) n", a=2)).then_inc(stored[b % 2], 16)
                    dve_s.wait(e, "k3", b + 1)
                    e.dma_start(scr_k[b].rearrange("t p n -> p t n"), K3[b % 2]).then_inc(stored[b % 2], 16)
                    act_s.wait(e, "va1", b + 1)
                    e.dma_start(scr_v[b].rearrange("g p n -> p g n"),
                                VA.rearrange("p g k n -> p g (k n)")).then_inc(v_stored, 16)
                for st, n in ((stored[0], 32), (stored[1], 32), (v_stored, 16)):
                    e.sem_inc(st, n)
                for hg in range(HG):
                    store_grid(hg)
                    if hg:
                        load_grid(hg - 1)
                load_grid(HG - 1)
                store_parts(0)
                store_parts(1)
                for st, n in ((stored[0], 64), (stored[1], 64), (v_stored, 48)):
                    e.wait_ge(st, n)
                load_slot(e, 0, 0)
                load_slot(e, 0, 1)
                store_parts(2)
                store_parts(3)
                all_stored(e)
                load_slot(e, 0, 2)
                load_slot(e, 0, 3)
                for n in range(2):
                    send_maxima(e, n, n, n % 2)

                def body(it, last):
                    for hg in range(HG):
                        if not last or hg < 2:
                            send_maxima(e, it * HG + (hg - 2), (hg + 2) % HG, hg % 2)
                        if not last:
                            e.wait_ge(pv_done, it * 40 + (10 * hg + 10 + NPB - 40))
                            load_slot(e, it, hg)
                over_batches(e, lambda: None, body)

            def f_pool(e):
                before(e)
                e.memset(VS[:, :, VG:VG + 32], 0.0)
                e.memset(VA.rearrange("p g k n -> p (g k n)")[:, D::VW], 1.0).then_inc(prep, 1)

                def split_maxima(n, par, after):
                    e.wait_ge(ring_free, after)
                    if not isinstance(n, int) or n >= 2:
                        e.wait_ge(nm_stored, n * 16 - 16)
                    apart(e)
                    e.tensor_scalar(N3[par][0:32, 0, :], NF[0:32], 1.0, None, ALU.mult).then_inc(nm_chain, 1)
                    e.wait_ge(nm_chain, n * 3 + 1)
                    e.tensor_tensor(NR[0:32], NF[0:32], N3[par][0:32, 0, :], ALU.subtract).then_inc(nm_chain, 1)
                    e.wait_ge(nm_chain, n * 3 + 2)
                    apart(e)
                    e.tensor_scalar(N3[par][0:32, 1, :], NR[0:32], 1.0, None, ALU.mult).then_inc(nm_chain, 1)
                    e.wait_ge(nm_chain, n * 3 + 3)
                    e.tensor_tensor(N3[par][0:32, 2, :], NR[0:32], N3[par][0:32, 1, :], ALU.subtract)\
                        .then_inc(nm_ready, 1)
                for g in range(2):
                    split_maxima(g, g, (g + 1) * (len(ITEMS) + 1))

                def body(it, last):
                    for kind, _, hg, db, local in LAST if last else BODY:
                        if kind == "maxima":
                            split_maxima((it + db) * HG + (hg - 2), hg % 2, item_no(it, local) + 1)
                over_batches(e, lambda: None, body)

            def f_act(e):
                before(e)
                e.wait_ge(s_const, n_const)
                e.activation(bqs, bqk[:, 0:1], ACT.Copy, scale=SCALE).then_inc(prep, 1)
                e.wait_ge(prep, 2)

                def copy_grid(hg):
                    e.wait_ge(rel_mm, hg + 1)
                    if hg >= 2:
                        e.wait_ge(rel_ch, 4 * hg - 6)
                    for c in range(2):
                        ins = e.activation((QF, KF)[hg % 2][:, c * CH:(c + 1) * CH], bank[(0, 1, 2, 7)[c + 2 * (hg % 2)]], ACT.Copy,
                                           scale=GRID_SCALE)
                    ins.then_inc(rel_out, 1)

                for hg in range(HG):
                    copy_grid(hg)
                act_s.start(e)
                with e.Fori(1, B + 1) as it:
                    for c in range(2):
                        r = slice(c * CH, (c + 1) * CH)
                        pe_s.wait(e, f"q{c}", it)
                        dve_s.wait(e, "qr", it - 1)
                        e.activation(QF[:, r], bank[c], ACT.Identity, bias=bqs, scale=SCALE).then_inc(act_s.sem, 1)
                        pe_s.wait(e, f"k{c}", it)
                        dve_s.wait(e, "kr", it - 1)
                        e.activation(KF[:, r], bank[(2, 7)[c]], ACT.Identity, bias=bqk[:, 1:2])\
                            .then_inc(act_s.sem, 1)
                        pe_s.wait(e, f"v{c}", it)
                        pe_s.wait(e, f"t{c}", it - 1)
                        e.activation(VT[c], bank[3 + c], ACT.Identity, bias=vec(BV)).then_inc(act_s.sem, 1)
                    for c in range(2):
                        pe_s.wait(e, f"t{c}", it)
                        e.wait_ge(v_stored, it * 16)
                        for i in range(4):
                            src = bank[5 + c][:, i * P:(i + 1) * P].rearrange("p (g j d) -> p g j d", g=HG, j=HG)
                            dst = VA[:, :, 4 * c + i, :].rearrange("p g (j w) -> p g j w", w=VW)[:, :, :, 0:D]
                            ins = e.activation(dst, src, ACT.Copy)
                        ins.then_inc(act_s.sem, 1)
                all_stored(e)
                e.sem_inc(exp_done, 2)
                e.sem_inc(os_done, 1)

                def turned(it, hg, half, last=False):
                    for kind, arg, g, db, n in LAST if last and hg else BODY:
                        if (kind, arg, g) == ("turn_out", half, hg):
                            return item_no(it, n) + 1 - db * IPB

                def copy_out(it, hg, half, last=False):
                    e.wait_ge(pv_done, it * 40 + (10 * hg + HALF_END[half] + 1 + NPB - 40))
                    e.wait_ge(ring_ready, turned(it, hg - 1, half, last and hg > 1) if hg else turned(it, HG - 1, half) - IPB)
                    e.activation(OS[half], bank[7], ACT.Copy).then_inc(os_done, 1)

                def exps(it, hg, ts, with_copy=True, last=False):
                    for t in ts:
                        i, h = t // 2, t % 2
                        wid = max(p[3] + p[2] for p in PACKS[i])
                        e.wait_ge(sc_ready, it * 80 + (20 * hg + t + 1 - 80))
                        e.wait_ge(pv_done, it * 40 + (10 * hg + i + 1 - 40))
                        e.activation(PR[(10 * hg + i) % NPB][:, 2 * h:2 * h + 2, 0:wid],
                                     psum_pair[t % 2][:, :, 0:wid], ACT.Exp).then_inc(exp_done, 1)
                        if t == 2 * HALF_END[0] + 3:
                            copy_out(it, hg, 0, last)
                        if t == 1 and with_copy:
                            if hg:
                                copy_out(it, hg - 1, 1, last)
                            else:
                                copy_out(it - 1, HG - 1, 1)

                def body(it, last):
                    exps(it, 0, range(HEAD_T, 2 * NP_), last=last)
                    for hg in range(1, HG):
                        exps(it, hg, range(2 * NP_), last=last)
                    if last:
                        copy_out(it, HG - 1, 1, last)
                    else:
                        exps(it + 1, 0, range(HEAD_T))
                over_batches(e, lambda: exps(1, 0, range(HEAD_T), False), body)

            def f_pe(e):
                before(e)
                e.wait_ge(load, 64)
                for hg in range(HG):
                    for c in range(2):
                        if hg >= 2:
                            e.wait_ge(rel_out, hg - 1)
                        m = e.matmul(bank[(0, 1, 2, 7)[c + 2 * (hg % 2)]], rel[0:S, hg * P:(hg + 1) * P], grid[0:S, c * CH:(c + 1) * CH],
                                     start=True, stop=True)
                    m.then_inc(rel_mm, 1)
                e.wait_ge(rel_out, HG)
                wait_h(e, NCH)
                pe_s.start(e)
                with e.Fori(1, B + 1) as it:
                    for c in range(2):
                        for k, bk in enumerate((bank[c], bank[(2, 7)[c]], bank[3 + c])):
                            act_s.wait(e, f"{'qkv'[k]}{c}", it - 1)
                            e.matmul(bk, wqkv[:, k, :], col(H, it * T + (c * CH - T)),
                                     start=True, stop=True).then_inc(pe_s.sem, 1)
                    for c in range(2):
                        act_s.wait(e, f"v{c}", it)
                        act_s.wait(e, f"va{c}", it - 1)
                        for i in range(4):
                            m = e.transpose(bank[5 + c][:, i * P:(i + 1) * P], VT[c][:, i * P:(i + 1) * P],
                                            ident[:, :])
                        m.then_inc(pe_s.sem, 1)
                act_s.wait(e, "k1", B)
                e.wait_ge(const_rows, 16 * HG)
                e.wait_ge(rel_ld, 16 * 9 * HG)

                def piece(slot, p, bk):
                    j, qb, k0, n, _, c0 = p
                    q = slice(qb % 4 * P, qb % 4 * P + P)
                    lhs = QL[0:MAX0, slot, qb // 4, j, q] if k0 == 0 else QU[0:MAX0, slot, j, q]
                    return e.matmul(bk[:, c0:c0 + n], lhs, KK[0:MAX0, slot, j, k0:k0 + n], start=True, stop=True)

                def item(slot, pieces, bk):
                    for p in pieces:
                        m = piece(slot, p, bk)
                    return m

                def maxima(n, par, bk):
                    e.wait_ge(pm_ready, n + 1)
                    return e.transpose(bk[0:32, 0:P], NM[par].rearrange("p a j q -> p (a j q)"), ident[:, :])
                no = 0
                for g in range(2):
                    e.wait_ge(slot_ld[g], SLOT)
                    for p in ITEMS:
                        if no >= RING:
                            e.wait_ge(ring_free, no - RING + 1)
                        item(g, p, bank[no % RING]).then_inc(ring_ready, 1)
                        no += 1
                    e.wait_ge(ring_free, no - RING + 1)
                    maxima(g, g % 2, bank[no % RING]).then_inc(ring_ready, 1)
                    no += 1
                assert no == PRO
                act_s.wait(e, "va1", B)
                e.sem_inc(pv_done, NPB)

                def run(events, it0):
                    first_item = min(v[4] for v in events)
                    for kind, arg, hg, db, local in events:
                        it = it0 + db
                        slot2 = (hg + 2) % HG
                        if kind == "scores" and arg == 0:
                            e.wait_ge(nm_loaded[hg], it * 32)
                            e.wait_ge(slot_ld[hg], it * SLOT)
                        if kind == "piece" and arg == ITEMS[0]:
                            e.wait_ge(slot_ld[slot2], it * SLOT + (SLOT if hg >= 2 else 0))
                        if kind in RINGED:
                            bk = bank[local % RING]
                            e.wait_ge(ring_free, item_no(it0, max(local - RING + 1, first_item)))
                        if kind == "piece":
                            item(slot2, arg, bk).then_inc(ring_ready, 1)
                        elif kind == "maxima":
                            maxima(it * HG + (hg - 2), hg % 2, bk).then_inc(ring_ready, 1)
                        elif kind == "scores":
                            e.wait_ge(exp_done, it * 80 + (20 * hg + arg - 1 + 2 - 80))
                            for kb, n0, n, c0 in PACKS[arg // 2]:
                                diagonal = kb * P == n0
                                for jj in range(2):
                                    j = 2 * (arg % 2) + jj
                                    q = slice(n0 % CH, n0 % CH + n)
                                    rhs = QL[0:ROWS, hg, n0 // CH, j, q] if kb < 4 else QU[0:ROWS, hg, j, q]
                                    m = e.matmul(psum_pair[arg % 2][:, jj, c0:c0 + n],
                                                 KK[0:ROWS, hg, j, kb * P:(kb + 1) * P], rhs,
                                                 start=True, stop=True)
                                    if diagonal:
                                        m = e.matmul(psum_pair[arg % 2][:, jj, c0:c0 + P], ident16[:, :],
                                                     mask_t[:, :], start=False, stop=True,
                                                     skip_group_check=True)
                            m.then_inc(sc_ready, 1)
                        elif kind == "pv":
                            e.wait_ge(exp_done, it * 80 + (20 * hg + 2 * arg + 2 + 2 - 80))
                            first = arg in (0, HALF_END[0] + 1)
                            if first:
                                half = int(arg > 0)
                                e.wait_ge(os_done, it * (2 * HG) + (2 * hg + half + 1 - 2 * HG))
                            for kb, n0, n, c0 in PACKS[arg]:
                                q0 = n0 % CH
                                for j in range(HG):
                                    v0 = (kb * HG + j) * VW
                                    m = e.matmul(bank[7][32 * j:32 * j + 32, q0:q0 + n], VS[:, hg, v0:v0 + 32],
                                                 PR[(10 * hg + arg) % NPB][:, j, c0:c0 + n],
                                                 start=first, stop=arg in HALF_END,
                                                 skip_group_check=True)
                            m.then_inc(pv_done, 1)
                        elif kind == "turn_out":
                            e.wait_ge(os_done, it * (2 * HG) + (2 * hg + arg + 2 - 2 * HG))
                            for i in range(4):
                                m = e.transpose(bk[:, i * P:(i + 1) * P], OS[arg][:, i * P:(i + 1) * P],
                                                ident[:, :])
                            m.then_inc(ring_ready, 1)
                        elif kind == "turn_att":
                            e.wait_ge(ring_free, item_no(it0, item_of(events, "turn_out", 1) + 1))
                            for i in range(4):
                                m = e.transpose(bk[:, i * P:(i + 1) * P], ATT[:, 4 * arg + i, :], ident[:, :])
                            m.then_inc(ring_ready, 1)
                        elif kind == "out":
                            e.wait_ge(ring_free, item_no(it0, item_of(events, "turn_att", arg) + 1))
                            e.matmul(bk, wo, ATTT[:, arg * CH:(arg + 1) * CH], start=True, stop=True)\
                                .then_inc(ring_ready, 1)
                over_batches(e, lambda: run(HEAD, 1), lambda it, last: run(LAST if last else BODY, it))

            def f_dve(e):
                for hg in range(HG):
                    full, rest_, parts = ((QF, QR, Q3), (KF, KR, K3))[hg % 2]
                    parts = parts[0]
                    e.wait_ge(rel_out, hg + 1)
                    if hg >= 2:
                        e.wait_ge(rel_st[hg % 2], 16)
                    e.tensor_copy(parts[:, 0, :], full).then_inc(rel_ch, 1)
                    e.wait_ge(rel_ch, 4 * hg + 1)
                    e.tensor_tensor(rest_, full, parts[:, 0, :], ALU.subtract).then_inc(rel_ch, 1)
                    e.wait_ge(rel_ch, 4 * hg + 2)
                    e.tensor_copy(parts[:, 1, :], rest_).then_inc(rel_ch, 1)
                    e.wait_ge(rel_ch, 4 * hg + 3)
                    e.tensor_tensor(parts[:, 2, :], rest_, parts[:, 1, :], ALU.subtract).then_inc(rel_ch, 1)
                dve_s.start(e)
                for st in rel_st:
                    e.wait_ge(st, 16 * HG // 2)
                with e.Fori(1, B // 2 + 1) as it2:
                    for bb in range(2):
                        it = it2 * 2 + (bb - 1)
                        act_s.wait(e, "q1", it)
                        e.wait_ge(stored[bb], it2 * 32)
                        e.tensor_copy(Q3[bb][:, 0, :], QF).then_inc(dve_s.sem, 1)
                        act_s.wait(e, "k1", it)
                        e.tensor_copy(K3[bb][:, 0, :], KF).then_inc(dve_s.sem, 1)
                        dve_s.wait(e, "q1", it)
                        e.tensor_tensor(QR, QF, Q3[bb][:, 0, :], ALU.subtract).then_inc(dve_s.sem, 1)
                        dve_s.wait(e, "k1", it)
                        e.tensor_tensor(KR, KF, K3[bb][:, 0, :], ALU.subtract).then_inc(dve_s.sem, 1)
                        dve_s.wait(e, "qr", it)
                        e.tensor_copy(Q3[bb][:, 1, :], QR).then_inc(dve_s.sem, 1)
                        dve_s.wait(e, "kr", it)
                        e.tensor_copy(K3[bb][:, 1, :], KR).then_inc(dve_s.sem, 1)
                        dve_s.wait(e, "q2", it)
                        e.tensor_tensor(Q3[bb][:, 2, :], QR, Q3[bb][:, 1, :], ALU.subtract).then_inc(dve_s.sem, 1)
                        dve_s.wait(e, "k2", it)
                        e.tensor_tensor(K3[bb][:, 2, :], KR, K3[bb][:, 1, :], ALU.subtract).then_inc(dve_s.sem, 1)

                def item(pieces, par, bk, no):
                    for i, (j, qb, _, n, diag, c0) in enumerate(pieces):
                        src = bk[:, c0:c0 + n]
                        if diag:
                            apart(e)
                            ins = e.tensor_tensor_reduce(dump[no % 2][i][:, 0:n], src, mask[:, CH - n:CH], 1.0,
                                                         1e8 * NEG, ALU.add, ALU.max,
                                                         NM[par][:, qb // 4, j, qb % 4:qb % 4 + 1])
                        else:
                            ins = e.tensor_reduce(PF[par][:, j, qb - 4:qb - 3], src, AX.X, ALU.max)
                    ins.then_inc(ring_free, 1)

                def combine(par, after):
                    e.wait_ge(ring_free, after)
                    e.tensor_tensor(NM[par][:, 1], NM[par][:, 1], PF[par], ALU.max).then_inc(pm_ready, 1)

                def maxima(n, bk):
                    if not isinstance(n, int) or n >= 1:
                        e.wait_ge(nm_ready, n)
                    e.tensor_scalar(NF[0:32], bk[0:32, 0:P], -1.0, None, ALU.mult).then_inc(ring_free, 1)
                no = 0
                for g in range(2):
                    for i, p in enumerate(ITEMS):
                        e.wait_ge(ring_ready, no + 1)
                        if no >= 2:
                            e.wait_ge(ring_free, no - 1)
                        item(p, g % 2, bank[no % RING], no)
                        no += 1
                    combine(g % 2, no)
                    e.wait_ge(ring_ready, no + 1)
                    maxima(g, bank[no % RING])
                    no += 1

                def run(events, it0):
                    for kind, arg, hg, db, local in events:
                        if kind not in RINGED:
                            continue
                        it = it0 + db
                        bk = bank[local % RING]
                        e.wait_ge(ring_ready, item_no(it0, local) + 1)
                        e.wait_ge(ring_free, item_no(it0, local) - 1)
                        if kind == "piece":
                            item(arg, hg % 2, bk, local)
                            if arg == ITEMS[-1]:
                                combine(hg % 2, item_no(it0, local) + 1)
                        elif kind == "maxima":
                            maxima(it * HG + (hg - 2), bk)
                        elif kind == "turn_out":
                            v = bk.rearrange("p (k j w) -> p k j w", k=4, j=HG)
                            e.reciprocal(RC[arg], v[:, :, :, D:VW].rearrange("p k j w -> p k (j w)")).then_inc(rc_done, 1)
                            e.wait_ge(rc_done, it * (2 * HG) + (2 * hg + arg + 1 - 2 * HG))
                            o = ATT[:, 4 * arg:4 * arg + 4, hg * 32:(hg + 1) * 32]
                            e.tensor_tensor(o.rearrange("p k (j d) -> p k j d", j=HG), v[:, :, :, 0:D],
                                            RC[arg].unsqueeze(3).to_broadcast([P, 4, HG, D]), ALU.mult)\
                                .then_inc(ring_free, 1)
                        elif kind == "turn_att":
                            e.tensor_copy(ATTT[:, arg * CH:(arg + 1) * CH], bk).then_inc(ring_free, 1)
                        elif kind == "out":
                            xc = col(X, it * T + (arg * CH - T))
                            e.scalar_tensor_tensor(out=xc, in0=bk, scalar=vec(BO), in1=xc, op0=ALU.add,
                                                   op1=ALU.add).then_inc(ring_free, 1)
                over_batches(e, lambda: run(HEAD, 1), lambda it, last: run(LAST if last else BODY, it))

            for k, f in (("sp", f_sp), ("pool", f_pool), ("act", f_act), ("pe", f_pe), ("dve", f_dve)):
                progs[k].append(f)
            return lambda e: e.wait_ge(ring_free, TOTAL)

        def zero_first(e):
            for b in range(B):
                e.memset(H[:, b * (T + 1):b * (T + 1) + 1], 0.0)
            e.memset(H[:, B * (T + 1):], 0.0).then_inc(s_hz, 1)
        s_hz = sem("h_padded")

        def pe_first1(e):
            e.wait_ge(s_first, 16 * len(first_consts))
        h1 = layer_norm("ln1", X, True, True, (LN1W, LN1B), True, pe_first1, zero_first,
                        lambda e, c: e.wait_ge(s_x[c // 2], 16))

        def wait_ln1(e):
            h1(e, NCH)
            e.wait_ge(s_hz, 1)
        progs["pe"].append(wait_ln1)
        progs["dve"].append(wait_ln1)
        used[0] = 0
        tm_done = time_mix()

        def after_tm(e):
            tm_done(e)
        used[0] = 0
        h2 = layer_norm("ln2", XP, False, False, (LN2W, LN2B), True, after_tm, lambda e: None)
        cm_dve = channel_mix(h2)

        def after_cm(e):
            cm_dve.wait(e, "xa1", B)
        used[0] = 0
        used[0] = 0
        h3 = layer_norm("ln3", X, False, False, None, False, after_cm, lambda e: None)
        after_f1 = experts("f1", after_cm, h3, False)
        h4 = layer_norm("ln4", X, False, True, (GAM, BET), False, after_f1, lambda e: None)
        used[0] = 0
        after_at = attention(after_f1, h4)
        h5 = layer_norm("ln5", X, False, False, None, False, after_at, lambda e: None)
        used[0] = 0
        experts("f2", after_at, h5, True)

        @block.sync
        def _(e):
            for f in progs["sp"]:
                f(e)

        @block.scalar
        def _(e):
            for f in progs["act"]:
                f(e)

        @block.gpsimd
        def _(e):
            for f in progs["pool"]:
                f(e)

        @block.tensor
        def _(e):
            for f in progs["pe"]:
                f(e)

        @block.vector
        def _(e):
            for f in progs["dve"]:
                f(e)


def bf16_bits(a):
    return (np.ascontiguousarray(a, dtype=np.float32).view(np.uint32) >> 16).astype(np.uint16)


def shape_constants():
    eye = np.eye(P, dtype=np.float32)
    mean_at = np.zeros((P, 31 + NCH), np.float32)
    mean_at[:, [NCH - 1, 2 * NCH - 1, 3 * NCH - 1]] = 1.0 / C
    pick = np.zeros((P, NBLK), np.float32)
    parts_at = np.zeros((P, 2), np.float32)
    pick_e = np.zeros((P, E), np.float32)
    for p in range(3):
        for g in range(4):
            rows = slice(32 * g + NCH * p, 32 * g + NCH * (p + 1))
            pick[rows, g::4] = np.eye(NCH)
            parts_at[rows] = [(0, 0), (-1, 0), (-1, -1)][p]
        pick_e[p * E:(p + 1) * E] = np.eye(E)
    b2_at = np.zeros((P, 2), np.float32)
    b2_at[24:32] = (-1, -1)
    b2_at[32:48] = (-1, 0)
    mask = np.zeros((P, CH), np.float32)
    mask[:, CH - P:] = np.where(np.arange(P)[None, :] > np.arange(P)[:, None], NEG, 0.0)
    k = (T - 1) // (S - 1)
    m = np.zeros((T, S), np.float32)
    for n in range(T - 1):
        m[n, n // k] += k - n % k
        m[n, min(n // k + 1, S - 1)] += n % k
    keys = np.zeros((3 * SW + 3, T), np.float32)
    for p in range(3):
        keys[p * SW:(p + 1) * SW, :T // 2] = m[:T // 2, :SW].T
        keys[p * SW:(p + 1) * SW, T // 2:] = m[T // 2:, S - SW:].T
    keys[3 * SW:] = 1.0
    return {
        "centre": eye - np.float32(1.0 / C), "mean_at": mean_at, "parts_at": parts_at, "b2_at": b2_at, "ident": eye, "ident16": bf16_bits(eye),
        "pick": bf16_bits(pick), "pick_e": bf16_bits(pick_e),
        "tie": np.tile((E - np.arange(E)).astype(np.float32), (P, 1)), "mask": mask,
        "mask_t": bf16_bits(mask[:, CH - P:].T),
        "grid_t": np.ascontiguousarray(m.T), "key_rows": bf16_bits(keys),
    }


def layouts(inp):
    a = {k: np.asarray(v) for k, v in inp.items()}

    def by_width(m):
        return m.reshape(HG, HG, D, -1).transpose(0, 2, 1, 3).reshape(m.shape)
    A, Bt, F = "L0_attn_a_", "L0_attn_b_", "L0_ffn_"
    t = {
        "x": a[A + "x"].reshape(N, C).T,
        "vecs": np.stack([a[A + k] for k in ("ln1_w", "ln1_b", "ln2_w", "ln2_b", "time_decay", "time_first",
                                             "tmk", "tmv", "tmr", "f_tmk", "f_tmr")]
                         + [a[Bt + k] for k in ("gamma", "beta", "bo", "bv")], axis=1),
        "bqk": np.stack([by_width(a[Bt + "bq"]), by_width(a[Bt + "bk"])], axis=1),
        "att_kvr": np.stack([a[A + "att_kw"].T, a[A + "att_vw"].T, a[A + "att_rw"].T], axis=1),
        "att_ow": a[A + "att_ow"].T,
        "f_kw": a[A + "f_kw"].T,
        "f_rw": a[A + "f_rw"].T,
        "f_vw": a[A + "f_vw"].T.reshape(FB, P, C).transpose(1, 0, 2),
        "gate": a[F + "gate"],
        "W1": a[F + "W1"].transpose(1, 0, 2),
        "b1": a[F + "b1"].reshape(E * HB, P).T,
        "W2": a[F + "W2"].reshape(E, HB, P, C).transpose(2, 0, 1, 3),
        "b2": a[F + "b2"],
        "wqkv": np.stack([by_width(a[Bt + "Wq"]).T, by_width(a[Bt + "Wk"]).T, a[Bt + "Wv"].T], axis=1),
        "wo": a[Bt + "Wo"].T,
        "rel": a[Bt + "rel_bias"].transpose(1, 0, 2),
    }
    return {k: np.ascontiguousarray(v) for k, v in t.items()}


def kernel(**inputs):
    import concourse.bacc as _bacc
    from concourse.bass_utils import run_bass_kernel_spmd as _run

    nc = _bacc.Bacc("TRN2", target_bir_lowering=False, num_devices=1)
    arrays, aps = {}, {}
    for name, v in {**layouts(inputs), **shape_constants()}.items():
        arrays[f"in_{name}"] = v
        aps[name] = nc.dram_tensor(f"in_{name}", v.shape, mybir.dt.from_np(v.dtype), kind="ExternalInput").ap()
        if v.dtype == np.uint16:
            aps[name] = aps[name].bitcast(BF16)
    out = nc.dram_tensor("out", (C, N), F32, kind="ExternalOutput").ap()
    x = aps.pop("x")
    build(nc, x, aps, out)
    r = _run(nc, [arrays], core_ids=[0])
    return np.ascontiguousarray(r.results[0]["out"].T).reshape(B, T, C)
```
